# Optimizing a Trainium2 kernel written in Bass

```python
import numpy as np
import jax
import jax.numpy as jnp

def _softmax(x, axis=-1):
    return jax.nn.softmax(x, axis=axis)

def _gelu(x):
    return jax.nn.gelu(x, approximate=True)

def _silu(x):
    return jax.nn.silu(x)

def _sigmoid(x):
    return jax.nn.sigmoid(x)

def _layernorm(x, axis=-1, eps=1e-05):
    m = jnp.mean(x, axis=axis, keepdims=True)
    v = jnp.var(x, axis=axis, keepdims=True)
    return (x - m) / jnp.sqrt(v + eps)

def _scatter_add(tgt, idx, src, axis=0):
    return tgt.at[idx].add(src)

def _segment_sum(src, seg, n):
    return jax.ops.segment_sum(src, seg, n)
kernel_name = 'mk_gnn_resnorm_d4_gnn_r8_ebf4bb'

def setup_inputs(seed: int=0):
    np.random.seed(seed)
    _w = jnp.asarray

    def _rec_inputs():
        import jax
        import jax.numpy as jnp
        _gk = jax.random.key(seed)
        x = -0.0005121 + 1.001 * jax.random.normal(jax.random.fold_in(_gk, 1), (12500, 32), jnp.float32)
        src = jax.random.randint(jax.random.fold_in(_gk, 2), (400000,), 0, 12500, jnp.int32)
        dst = jnp.minimum((12500 * jax.random.uniform(jax.random.fold_in(_gk, 3), (400000,)) ** 2.0).astype(jnp.int32), 99999)
        _o = jnp.argsort(dst, stable=True)
        src = src[_o]
        dst = dst[_o]
        edge_attr_32 = 0.000196303 + 1.00016 * jax.random.normal(jax.random.fold_in(_gk, 12), (400000, 32), jnp.float32)
        return (x, src, dst, edge_attr_32)
    x, src, dst, edge_attr_32 = _rec_inputs()

    def _L0_gnn_setup():
        import jax, jax.numpy as jnp
        import numpy as np
        N_NODES = 12500
        N_EDGES = 200000
        IN_FEAT = 32
        OUT_FEAT = 32

        def _gna_forward(feat, src, dst, w1_W, w1_b, w2_W, w2_b, a):
            n = feat.shape[0]
            h_src = feat[src]
            h_dst = feat[dst]
            dt = h_dst - h_src
            a_vec = a[0]
            aij = dt @ (w2_W.T @ a_vec) + jnp.dot(a_vec, w2_b)
            ss = h_src @ w2_W.T + w2_b
            m = jax.ops.segment_max(aij, dst, num_segments=n)
            aexp = jnp.exp(aij - m[dst])
            denom = jax.ops.segment_sum(aexp, dst, num_segments=n)
            alpha = aexp / denom[dst]
            res = jax.ops.segment_sum(alpha[:, None] * ss, dst, num_segments=n)
            out = res + feat @ w1_W.T + w1_b
            return out
        key = jax.random.key(seed)
        k = jax.random.split(key, 8)
        feat = jax.random.normal(k[0], (N_NODES, IN_FEAT), dtype=jnp.float32)
        src = jax.random.randint(k[1], (N_EDGES,), 0, N_NODES, dtype=jnp.int64)
        dst = jax.random.randint(k[2], (N_EDGES,), 0, N_NODES, dtype=jnp.int64)
        s1 = 1.0 / np.sqrt(IN_FEAT)
        w1_W = jax.random.uniform(k[3], (OUT_FEAT, IN_FEAT), jnp.float32, -s1, s1)
        w1_b = jax.random.uniform(k[4], (OUT_FEAT,), jnp.float32, -s1, s1)
        w2_W = jax.random.uniform(k[5], (OUT_FEAT, IN_FEAT), jnp.float32, -s1, s1)
        w2_b = jax.random.uniform(k[6], (OUT_FEAT,), jnp.float32, -s1, s1)
        a = jax.random.normal(k[7], (1, OUT_FEAT), dtype=jnp.float32)
        return {'feat': feat, 'src': src, 'dst': dst, 'w1_W': w1_W, 'w1_b': w1_b, 'w2_W': w2_W, 'w2_b': w2_b, 'a': a}
    _L0_gnn_all = _L0_gnn_setup()
    _L0_gnn_in = {k: v for k, v in _L0_gnn_all.items() if k in ('w1_W', 'w1_b', 'w2_W', 'w2_b', 'a')}
    del _L0_gnn_all

    def _L1_gnn_setup():
        import jax, jax.numpy as jnp
        import numpy as np
        N_NODES = 12500
        N_EDGES = 200000
        LATENT_DIM = 32
        NUM_LAYERS = 3
        key = jax.random.key(seed)
        k_x, k_e = jax.random.split(key)
        x = jax.random.normal(k_x, (N_NODES, LATENT_DIM), dtype=jnp.float32)
        edge_index = jax.random.randint(k_e, (2, N_EDGES), 0, N_NODES, dtype=jnp.int64)
        return {'x': x, 'edge_index': edge_index, 'num_layers': NUM_LAYERS}
    _L1_gnn_all = _L1_gnn_setup()
    _L1_gnn_in = {k: v for k, v in _L1_gnn_all.items() if k in ()}
    del _L1_gnn_all

    def _L2_gnn_setup():
        import jax, jax.numpy as jnp
        import numpy as np
        N_NODES = 6250
        N_EDGES = 100000
        X_DIM = 32
        E_DIM = 32
        HID = 64
        OUT = 32
        key = jax.random.key(seed)
        ks = jax.random.split(key, 6)
        x = jax.random.normal(ks[0], (N_NODES, X_DIM), dtype=jnp.float32)
        edge_index = jax.random.randint(ks[1], (2, N_EDGES), 0, N_NODES, dtype=jnp.int64)
        edge_attr = jax.random.normal(ks[2], (N_EDGES, E_DIM), dtype=jnp.float32)
        in_dim = 2 * X_DIM + E_DIM
        W1 = jax.random.normal(ks[3], (in_dim, HID), dtype=jnp.float32) * (1.0 / np.sqrt(in_dim))
        b1 = jnp.zeros((HID,), dtype=jnp.float32)
        W2 = jax.random.normal(ks[4], (HID, OUT), dtype=jnp.float32) * (1.0 / np.sqrt(HID))
        b2 = jnp.zeros((OUT,), dtype=jnp.float32)
        return {'x': x, 'edge_index': edge_index, 'edge_attr': edge_attr, 'W1': W1, 'b1': b1, 'W2': W2, 'b2': b2}
    _L2_gnn_all = _L2_gnn_setup()
    _L2_gnn_in = {k: v for k, v in _L2_gnn_all.items() if k in ('W1', 'b1', 'W2', 'b2')}
    del _L2_gnn_all

    def _L3_gnn_setup():
        import jax, jax.numpy as jnp
        import numpy as np
        N_LAYERS = 3
        N_NODES = 62500
        N_EDGES = 312500
        EMBED_DIM = 32
        key = jax.random.key(seed)
        k_w, k_e = jax.random.split(key)
        weight = jax.random.normal(k_w, (N_NODES, EMBED_DIM), dtype=jnp.float32) * 0.1
        edge_index = jax.random.randint(k_e, (2, N_EDGES), 0, N_NODES, dtype=jnp.int32)
        return {'weight': weight, 'edge_index': edge_index}
    _L3_gnn_all = _L3_gnn_setup()
    _L3_gnn_in = {k: v for k, v in _L3_gnn_all.items() if k in ()}
    del _L3_gnn_all
    return {'x': x, 'src': src, 'dst': dst, 'edge_attr_32': edge_attr_32, 'L0_gnn_w1_W': _L0_gnn_in['w1_W'], 'L0_gnn_w1_b': _L0_gnn_in['w1_b'], 'L0_gnn_w2_W': _L0_gnn_in['w2_W'], 'L0_gnn_w2_b': _L0_gnn_in['w2_b'], 'L0_gnn_a': _L0_gnn_in['a'], 'L2_gnn_W1': _L2_gnn_in['W1'], 'L2_gnn_b1': _L2_gnn_in['b1'], 'L2_gnn_W2': _L2_gnn_in['W2'], 'L2_gnn_b2': _L2_gnn_in['b2']}

def reference(x, src, dst, edge_attr_32, L0_gnn_w1_W, L0_gnn_w1_b, L0_gnn_w2_W, L0_gnn_w2_b, L0_gnn_a, L2_gnn_W1, L2_gnn_b1, L2_gnn_W2, L2_gnn_b2):
    import jax
    import jax.numpy as jnp

    def _L0_gnn_ref(feat, src, dst, w1_W, w1_b, w2_W, w2_b, a):
        import jax, jax.numpy as jnp
        import numpy as np
        N_NODES = 12500
        N_EDGES = 200000
        IN_FEAT = 32
        OUT_FEAT = 32

        def _gna_forward(feat, src, dst, w1_W, w1_b, w2_W, w2_b, a):
            n = feat.shape[0]
            h_src = feat[src]
            h_dst = feat[dst]
            dt = h_dst - h_src
            a_vec = a[0]
            aij = dt @ (w2_W.T @ a_vec) + jnp.dot(a_vec, w2_b)
            ss = h_src @ w2_W.T + w2_b
            m = jax.ops.segment_max(aij, dst, num_segments=n)
            aexp = jnp.exp(aij - m[dst])
            denom = jax.ops.segment_sum(aexp, dst, num_segments=n)
            alpha = aexp / denom[dst]
            res = jax.ops.segment_sum(alpha[:, None] * ss, dst, num_segments=n)
            out = res + feat @ w1_W.T + w1_b
            return out
        return _gna_forward(feat, src, dst, w1_W, w1_b, w2_W, w2_b, a)

    def _L1_gnn_ref(x, edge_index, num_layers):
        import jax, jax.numpy as jnp
        import numpy as np
        N_NODES = 12500
        N_EDGES = 200000
        LATENT_DIM = 32
        NUM_LAYERS = 3
        N = x.shape[0]
        src = edge_index[0]
        dst = edge_index[1]
        cnt = jax.ops.segment_sum(jnp.ones((edge_index.shape[1],), x.dtype), dst, num_segments=N)
        denom = jnp.maximum(cnt, 1.0)[:, None]
        scale = 1.0 / (num_layers + 1)
        final = x * scale
        for _ in range(num_layers):
            summed = jax.ops.segment_sum(x[src], dst, num_segments=N)
            x = summed / denom
            final = final + x * scale
        return final

    def _L2_gnn_ref(x, edge_index, edge_attr, W1, b1, W2, b2):
        import jax, jax.numpy as jnp
        import numpy as np
        N_NODES = 6250
        N_EDGES = 100000
        X_DIM = 32
        E_DIM = 32
        HID = 64
        OUT = 32
        num_nodes = x.shape[0]
        rol, col = (edge_index[0], edge_index[1])
        e_feat = jnp.concatenate([x[rol], x[col], edge_attr], axis=-1)
        h = jax.nn.relu(e_feat @ W1 + b1)
        v = h @ W2 + b2
        x_cand = jax.ops.segment_max(v, col, num_segments=num_nodes)
        return jnp.maximum(x_cand, x[:, -v.shape[-1]:])

    def _L3_gnn_ref(weight, edge_index):
        import jax, jax.numpy as jnp
        import numpy as np
        N_LAYERS = 3
        N_NODES = 62500
        N_EDGES = 312500
        EMBED_DIM = 32
        src, dst = (edge_index[0], edge_index[1])
        n = weight.shape[0]
        deg = jax.ops.segment_sum(jnp.ones(src.shape, dtype=weight.dtype), dst, num_segments=n)
        deg_inv_sqrt = jnp.where(deg > 0, jax.lax.rsqrt(deg), jnp.zeros((), weight.dtype))
        norm = deg_inv_sqrt[src] * deg_inv_sqrt[dst]
        x = weight
        acc = weight
        for _ in range(N_LAYERS):
            msgs = norm[:, None] * x[src]
            x = jax.ops.segment_sum(msgs, dst, num_segments=n)
            acc = acc + x
        return acc / (N_LAYERS + 1)
    edge_index = jnp.stack([src, dst])
    x = _layernorm(x + _L0_gnn_ref(x, src, dst, L0_gnn_w1_W, L0_gnn_w1_b, L0_gnn_w2_W, L0_gnn_w2_b, L0_gnn_a), axis=-1)
    x = _layernorm(x + _L1_gnn_ref(x, edge_index, 3), axis=-1)
    x = _layernorm(x + _L2_gnn_ref(x, edge_index, edge_attr_32, L2_gnn_W1, L2_gnn_b1, L2_gnn_W2, L2_gnn_b2), axis=-1)
    x = _layernorm(x + _L3_gnn_ref(x, edge_index), axis=-1)
    return x

_drawn_inputs = setup_inputs


def setup_inputs(seed=0):
    import zlib

    import numpy as np

    out = dict(_drawn_inputs(seed))
    spreads = {'L2_gnn_b1': (0.0, 0.1), 'L2_gnn_b2': (0.0, 0.1)}
    factors = {}
    for name, (base, spread) in spreads.items():
        noise = np.random.default_rng([zlib.crc32(name.encode()), seed]).standard_normal(out[name].shape)
        drawn = base * np.exp(spread * noise) if base else spread * noise
        out[name] = jnp.asarray(drawn.astype(out[name].dtype))
    for name, factor in factors.items():
        out[name] = (out[name] * factor).astype(out[name].dtype)
    return out
```

```python
import concourse.bass as bass
from concourse import mybir
from contextlib import ExitStack

P = 128
N_NODES, N_EDGES, FEAT, HID = 12500, 400000, 32, 64
NH = -(-N_NODES // P)
N_PAD = NH * P
TILES = N_EDGES // P
SUB = 32
BLOCK = 512
N_BLOCKS = -(-(TILES + N_NODES - 1) // BLOCK)
SLOTS = N_BLOCKS * BLOCK
SLOT_COLS = SLOTS // P
N_SUBS = SLOTS // SUB
HI_PART = 14
N_PARTS = NH // HI_PART
MATRIX_PARTS = (slice(0, 4), slice(4, N_PARTS))
CHUNK = 512
LANES = CHUNK // P
GROUPS = 4
CHUNKS = -(-N_EDGES // CHUNK)
GROUP_CHUNKS = -(-CHUNKS // GROUPS)
GROUP_EDGES = GROUP_CHUNKS * CHUNK
E_PAD = GROUPS * GROUP_EDGES
SLOT_BATCH = 31
N_BATCHES = SLOT_COLS // SLOT_BATCH
INFO_SPARE = 13056
NEG = -1.0e30
EPS = 1e-5
Y0_ROW = FEAT + 2

f32, bf16, i32 = mybir.dt.float32, mybir.dt.bfloat16, mybir.dt.int32
ALU = mybir.AluOpType
ACT = mybir.ActivationFunctionType
AX = mybir.AxisListType


class Names:
    pass


def rows_of(ap):
    return bass.IndirectOffsetOnAxis(ap=ap, axis=0)


def over_features(ap):
    return ap.unsqueeze(2).to_broadcast([P, NH, FEAT])


def prepare_constants(nc, sb, sem, pb, D, S):
    zeros = sb("zeros", [P, 7168], f32)
    ones_i = sb("ones_i", [P, 1], i32)
    theta = sb("theta", [P, 25], i32)
    theta_t = sb("theta_t", [P, 25], i32)
    tile_head_cols = -(-(TILES - 1) // P)
    src_pad = sb("src_pad", [P, LANES], i32)
    dst_run = TILES
    dst_sb = sb("dst_sb", [P, dst_run + 1], i32)
    keep = sb("keep", [P, dst_run], bf16)
    neg = sb("neg", [P, dst_run], bf16)
    zero_bf = sb("zero_bf", [P, 128], bf16)

    made = sem("const_made")
    zeroed = sem("const_zeros_made")
    flags_zero = sem("const_slot_flags_zeroed")
    inject_zero = sem("const_inject_zeroed")
    heads_loaded = sem("const_tile_heads_loaded")
    heads_added = sem("const_tile_heads_added")
    flags_set = sem("const_slot_flags_set")
    table_copied = sem("const_edge_table_copied")
    dst_loaded = sem("const_dst_loaded")
    dst_edge = sem("const_dst_edge_made")
    keep_made = sem("const_keep_made")
    neg_made = sem("const_neg_made")
    flags_stored = sem("const_scan_flags_stored")
    src_zero = sem("const_src_index_zeroed")
    src_loaded = sem("const_src_index_loaded")

    with nc.Block() as block:
        @block.sync
        def _(sp):
            heads = D.dst[:].rearrange("(t e) -> t e", e=P)[1:TILES, 0:1]
            full = (tile_head_cols - 1) * P
            sp.dma_start(theta[:, 0:tile_head_cols - 1],
                         heads[0:full].rearrange("(r p) o -> p (r o)", p=P),
                         allow_slow_non_contiguous=True).then_inc(heads_loaded, 16)
            sp.dma_start(theta[0:TILES - 1 - full, tile_head_cols - 1:tile_head_cols],
                         heads[full:TILES - 1],
                         allow_slow_non_contiguous=True).then_inc(heads_loaded, 16)
            sp.dma_start(D.edge_table[:, 0:P], D.src[:].rearrange("(t e) -> t e", e=P)).then_inc(table_copied, 16)
            sp.dma_start(D.edge_table[:, P:2 * P], D.dst[:].rearrange("(t e) -> t e", e=P)).then_inc(table_copied, 16)
            runs = D.dst[:].rearrange("(p i) -> p i", p=P)
            sp.wait_ge(dst_edge, 1)
            sp.dma_start(dst_sb[:, 1:dst_run + 1], runs).then_inc(dst_loaded, 16)
            sp.dma_start(dst_sb[1:P, 0:1], runs[0:P - 1, dst_run - 1:dst_run],
                         allow_slow_non_contiguous=True).then_inc(dst_loaded, 16)
            sp.wait_ge(src_zero, 1)
            whole = N_EDGES // CHUNK
            sp.dma_start(S.src_all[:, 0:whole * LANES].rearrange("p (k j) -> p k j", j=LANES),
                         D.src[0:whole * CHUNK].rearrange("(k p j) -> p k j", p=P, j=LANES)).then_inc(src_loaded, 16)
            rest = (N_EDGES - whole * CHUNK) // LANES
            sp.dma_start(S.src_all[0:rest, whole * LANES:(whole + 1) * LANES],
                         D.src[whole * CHUNK:N_EDGES].rearrange("(p j) -> p j", j=LANES)).then_inc(src_loaded, 16)
            sp.wait_ge(keep_made, 1)
            sp.dma_start(D.keep[0:N_EDGES].rearrange("(p i) -> p i", p=P), keep[:]).then_inc(flags_stored, 16)
            sp.wait_ge(neg_made, 1)
            sp.dma_start(D.neg[0:N_EDGES].rearrange("(p i) -> p i", p=P), neg[:]).then_inc(flags_stored, 16)
            pad = (E_PAD - N_EDGES) // P
            sp.dma_start(D.keep[N_EDGES:E_PAD].rearrange("(p i) -> p i", p=P), zero_bf[:, 0:pad]).then_inc(flags_stored, 16)
            sp.dma_start(D.neg[N_EDGES:E_PAD].rearrange("(p i) -> p i", p=P), zero_bf[:, 0:pad]).then_inc(flags_stored, 16)
            sp.wait_ge(table_copied, 32)
            sp.wait_ge(src_loaded, 32)
            sp.wait_ge(flags_stored, 64)

        @block.scalar
        def _(act):
            act.wait_ge(zeroed, 1)
            act.dma_start(D.slot_flags[:].rearrange("(p i) o -> p (i o)", p=P),
                          zeros[:, 0:(SLOTS + P) // P].bitcast(i32)).then_inc(flags_zero, 16)
            per = P * 7168 // FEAT
            for r in range(E_PAD // per):
                act.dma_start(D.inject[r * per:(r + 1) * per, :].rearrange("(p i) f -> p (i f)", p=P),
                              zeros[:]).then_inc(inject_zero, 16)
            act.wait_ge(inject_zero, 16 * (E_PAD // per))

        @block.gpsimd
        def _(pool):
            pg = nc.gpsimd
            pg.iota(S.ramp_hi[:], pattern=[[1, NH]], base=1, channel_multiplier=0,
                    allow_small_or_imprecise_dtypes=True)
            pg.iota(S.ramp_lo[:], pattern=[[1, P]], base=0, channel_multiplier=0,
                    allow_small_or_imprecise_dtypes=True)
            pg.iota(S.slot_id[:], pattern=[[P, SLOT_COLS]], base=0, channel_multiplier=1,
                    allow_small_or_imprecise_dtypes=True)
            pg.iota(S.node_id[:], pattern=[[P, NH]], base=0, channel_multiplier=1,
                    allow_small_or_imprecise_dtypes=True)
            pg.iota(theta_t[:], pattern=[[P, 25]], base=1, channel_multiplier=1)
            pg.memset(ones_i[:], 1)
            pg.memset(S.ident[:], 1.0)
            pg.memset(S.before[:], 1.0)
            pg.memset(S.group_pick[:], 0.0)
            pg.memset(S.part_sum[:], 0.0).then_inc(made, 1)
            pool.wait_ge(made, 1)
            pg.affine_select(out=S.ident[:], in_=S.ident[:], compare_op=ALU.is_equal, fill=0.0,
                             base=0, pattern=[[-1, P]], channel_multiplier=1)
            pg.affine_select(out=S.before[:], in_=S.before[:], compare_op=ALU.is_gt, fill=0.0,
                             base=0, pattern=[[1, P]], channel_multiplier=-1)
            pg.affine_select(out=S.group_pick[:], in_=S.group_pick[:], compare_op=ALU.not_equal, fill=1.0,
                             base=0, pattern=[[-FEAT, GROUPS]], channel_multiplier=1).then_inc(made, 1)
            for part in range(3):
                pool.wait_ge(made, 2 + part)
                pg.affine_select(out=S.part_sum[:], in_=S.part_sum[:], compare_op=ALU.not_equal, fill=1.0,
                                 base=-FEAT * part, pattern=[[-1, FEAT]], channel_multiplier=1).then_inc(made, 1)
            pool.wait_ge(heads_loaded, 32)
            full = tile_head_cols - 1
            last = TILES - 1 - full * P
            pg.tensor_tensor(theta[:, 0:full], theta[:, 0:full], theta_t[:, 0:full], ALU.add)
            pg.tensor_tensor(theta[0:last, full:], theta[0:last, full:], theta_t[0:last, full:], ALU.add).then_inc(heads_added, 1)
            pool.wait_ge(heads_added, 1)
            pool.wait_ge(flags_zero, 16)
            for r in range(tile_head_cols):
                n = P if r < full else last
                pg.indirect_dma_start(out=D.slot_flags[:], out_offset=rows_of(theta[0:n, r:r + 1]),
                                      in_=ones_i[0:n, :], in_offset=None).then_inc(flags_set, 16)
            pool.wait_ge(flags_set, 16 * tile_head_cols)

        @block.vector
        def _(dve):
            nc.vector.memset(zeros[:], 0.0)
            nc.vector.memset(zero_bf[:], 0.0).then_inc(zeroed, 1)
            nc.vector.memset(dst_sb[:, 0:1], -1).then_inc(dst_edge, 1)
            nc.vector.memset(S.src_all[:], 0).then_inc(src_zero, 1)
            dve.wait_ge(dst_loaded, 32)
            nc.vector.tensor_tensor(keep[:], dst_sb[:, 1:dst_run + 1], dst_sb[:, 0:dst_run],
                                    ALU.is_equal).then_inc(keep_made, 1)
            dve.wait_ge(keep_made, 1)
            nc.vector.tensor_scalar(neg[:], keep[:], 1.0, -NEG, ALU.subtract, ALU.mult).then_inc(neg_made, 1)
            dve.wait_ge(made, 2)
            nc.vector.tensor_copy(S.ident_bf[:], S.ident[:])


def prepare_nodes(nc, sb, sem, pb, D, S):
    STEP = 7
    w_nat = sb("w_nat", [FEAT, 2, FEAT], f32)
    a_col = sb("a_col", [FEAT, 1], f32)
    a_neg = sb("a_neg", [FEAT, FEAT], f32)
    w_all = sb("w_all", [FEAT + 1, 3, FEAT], f32)
    x_step = sb("x_step", [P, STEP, FEAT], f32)
    xt = sb("xt", [FEAT + 1, STEP * P], f32)
    table = sb("table", [P, NH, 2 * FEAT], f32)
    p_w = pb("p_w", [FEAT, 3, FEAT], f32)
    p_xt = pb("p_xt", [FEAT, 1024], f32)
    p_lin = pb("p_lin", [P, 2, 512], f32)

    pad_zero = sem("nodes_pad_zeroed")
    x_loaded = sem("nodes_x_loaded")
    w_loaded = sem("nodes_w_loaded")
    a_made = sem("nodes_a_negated")
    w_turned = sem("nodes_w_turned")
    w_made = sem("nodes_w_made")
    x_staged = sem("nodes_x_staged")
    x_turned = sem("nodes_x_turned")
    xt_made = sem("nodes_xt_made")
    multiplied = sem("nodes_multiplied")
    emptied = sem("nodes_emptied")
    stored = sem("nodes_table_stored")
    full = N_NODES // P

    with nc.Block() as block:
        @block.sync
        def _(sp):
            sp.wait_ge(pad_zero, 1)
            sp.dma_start(S.x[:, 0:full, :], D.x[0:full * P, :].rearrange("(h p) f -> p h f", p=P)).then_inc(x_loaded, 16)
            sp.dma_start(S.x[0:N_NODES - full * P, full, :], D.x[full * P:N_NODES, :]).then_inc(x_loaded, 16)
            sp.dma_start(w_nat[:, 0, :], D.w2_W[:, :]).then_inc(w_loaded, 16)
            sp.dma_start(w_nat[:, 1, :], D.w1_W[:, :]).then_inc(w_loaded, 16)
            sp.dma_start(a_col[:], D.a[:, :].rearrange("o k -> k o"), allow_slow_non_contiguous=True).then_inc(w_loaded, 16)
            sp.dma_start(w_all[FEAT:FEAT + 1, 0, :], D.w2_b[:].unsqueeze(0)).then_inc(w_loaded, 16)
            sp.dma_start(w_all[FEAT:FEAT + 1, 2, :], D.w1_b[:].unsqueeze(0)).then_inc(w_loaded, 16)
            sp.wait_ge(emptied, 4 * (NH // STEP))
            sp.dma_start(D.table0[:, :].rearrange("(h p) f -> p h f", p=P), table[:]).then_inc(stored, 16)
            sp.wait_ge(stored, 16)

        @block.vector
        def _(dve):
            nc.vector.memset(S.x[:, full, :], 0.0).then_inc(pad_zero, 1)
            nc.vector.memset(xt[FEAT:FEAT + 1, :], 1.0)
            nc.vector.memset(w_all[FEAT:FEAT + 1, 1, :], 0.0)
            dve.wait_ge(w_loaded, 80)
            nc.vector.tensor_scalar(a_neg[:], a_col[:].to_broadcast([FEAT, FEAT]), -1.0, None, ALU.mult).then_inc(a_made, 1)
            dve.wait_ge(w_turned, 1)
            nc.vector.tensor_copy(w_all[0:FEAT], p_w[:]).then_inc(w_made, 1)
            dve.wait_ge(x_loaded, 32)
            with dve.Fori(0, NH // STEP) as i:
                dve.wait_ge(x_turned, i)
                nc.vector.tensor_copy(x_step[:], S.x[:, bass.ds(i * STEP, STEP), :]).then_inc(x_staged, 1)
                dve.wait_ge(x_turned, i + 1)
                dve.wait_ge(multiplied, i)
                nc.vector.tensor_copy(xt[0:FEAT, :], p_xt[:, 0:STEP * P]).then_inc(xt_made, 1)
                dve.wait_ge(multiplied, i + 1)
                for bank, n in ((0, 4), (1, 3)):
                    lin = p_lin[:, bank, 0:n * 96].rearrange("p (j c) -> p j c", c=96)
                    at = bass.ds(i * STEP + 4 * bank, n)
                    nc.vector.tensor_copy(table[:, at, :], lin[:, :, 0:2 * FEAT]).then_inc(emptied, 1)
                    nc.vector.tensor_tensor(S.base[:, at, :], x_step[:, 4 * bank:4 * bank + n, :],
                                            lin[:, :, 2 * FEAT:3 * FEAT], ALU.add).then_inc(emptied, 1)
                dve.wait_ge(emptied, 4 * i + 4)

        @block.tensor
        def _(pe):
            pe.wait_ge(w_loaded, 80)
            pe.wait_ge(a_made, 1)
            nc.tensor.transpose(p_w[:, 0, :], w_nat[:, 0, :], S.ident[0:FEAT, 0:FEAT])
            nc.tensor.matmul(p_w[:, 1, :], w_nat[:, 0, :], a_neg[:], start=True, stop=True)
            nc.tensor.transpose(p_w[:, 2, :], w_nat[:, 1, :], S.ident[0:FEAT, 0:FEAT]).then_inc(w_turned, 1)
            with pe.Fori(0, NH // STEP) as i:
                pe.wait_ge(xt_made, i)
                pe.wait_ge(x_staged, i + 1)
                for j in range(STEP):
                    last = nc.tensor.transpose(p_xt[:, j * P:(j + 1) * P], x_step[:, j, :], S.ident[:])
                last.then_inc(x_turned, 1)
                pe.wait_ge(emptied, 4 * i)
                pe.wait_ge(w_made, 1)
                pe.wait_ge(xt_made, i + 1)
                for j in range(STEP):
                    last = nc.tensor.matmul(p_lin[:, j // 4, 96 * (j % 4):96 * (j % 4) + 96],
                                            xt[:, j * P:(j + 1) * P], w_all[:].rearrange("k b f -> k (b f)"),
                                            start=True, stop=True)
                last.then_inc(multiplied, 1)


def prepare_slots(nc, sb, sem, pb, D, S):
    C, B = SLOT_COLS, SLOT_BATCH
    flags = sb("flags", [C, 2, P], i32)
    flags_f = sb("flags_f", [C, 2, P], f32)
    ones = sb("ones", [C, P], f32)
    run = sb("run", [C, P], f32)
    whole = sb("whole", [C, P], f32)
    tile_of = sb("tile_of", [P, C], f32)
    going = sb("going", [P, C], f32)
    node_of = sb("node_of", [P, C], f32)
    tile_idx = sb("tile_idx", [P, C], i32)
    idx_ring = sb("idx_ring", [P, B], i32)
    edges = sb("edges", [P, B, 2 * P], i32)
    match = sb("match", [P, B, P], bf16)
    hi = sb("hi", [P, B, P], i32)
    key_hi = sb("key_hi", [P, B, P], bf16)
    key_lo = sb("key_lo", [P, B, P], bf16)
    count = sb("count", [P, C], f32)
    info = sb("info_sb", [P, C, 2], i32)
    info_idx = sb("info_idx", [P, C], i32)
    info_f = sb("info_f", [P, C], f32)
    info_ring = sb("info_ring", [P, B, 2], i32)
    first_row = sb("first_row", [1, 2], i32)
    p_a = pb("p_a", [P, 512], f32)
    p_keys = pb("p_keys", [P, 4, 1024], bf16)

    flags_loaded = sem("slots_flags_loaded")
    v = sem("slots_vector_step")
    summed = sem("slots_carry_summed")
    turned = sem("slots_turned")
    ring_ready = sem("slots_index_ready")
    gathered = sem("slots_edges_gathered")
    keys_made = sem("slots_keys_made")
    keys_turned = sem("slots_keys_turned")
    keys_kept = sem("slots_keys_kept")
    scat_ready = sem("slots_info_ready")
    scattered = sem("slots_info_scattered")
    row_made = sem("slots_first_row_made")
    row_stored = sem("slots_first_row_stored")
    steps = [0]

    def link(ins):
        steps[0] += 1
        ins.then_inc(v, 1)
        nc.vector.wait_ge(v, steps[0])
        return steps[0]

    marks = {}

    with nc.Block() as block:
        @block.vector
        def _(dve):
            nc.vector.memset(ones[:], 1.0)
            nc.vector.memset(first_row[:], 0).then_inc(row_made, 1)
            nc.vector.memset(S.key_hi[:, SLOTS:], 0.0)
            nc.vector.memset(S.key_lo[:, SLOTS:], 0.0)
            dve.wait_ge(flags_loaded, 32)
            link(nc.vector.tensor_copy(flags_f[:], flags[:]))
            link(nc.vector.tensor_tensor_scan(out=run[:], data0=ones[:], data1=flags_f[:, 0, :], initial=0.0,
                                              op0=ALU.mult, op1=ALU.add))
            dve.wait_ge(summed, 1)
            link(nc.vector.tensor_scalar(whole[:], run[:], p_a[0:C, 0:1], None, ALU.add))
            dve.wait_ge(turned, 1)
            link(nc.vector.tensor_copy(tile_of[:], p_a[:, 128:128 + C]))
            link(nc.vector.tensor_copy(going[:], p_a[:, 256:256 + C]))
            link(nc.vector.tensor_tensor(node_of[:], S.slot_id[:], tile_of[:], ALU.subtract))
            link(nc.vector.tensor_copy(tile_idx[:], tile_of[:]))
            base = steps[0]
            with dve.Fori(0, N_BATCHES) as i:
                at = bass.ds(i * B, B)
                dve.wait_ge(gathered, i * 16 * B)
                nc.vector.tensor_copy(idx_ring[:], tile_idx[:, at]).then_inc(ring_ready, 1)
                dve.wait_ge(gathered, (i + 1) * 16 * B)
                dve.wait_ge(keys_turned, 2 * i)
                nc.vector.tensor_tensor(match[:], edges[:, :, P:2 * P],
                                        node_of[:, at].unsqueeze(2).to_broadcast([P, B, P]), ALU.is_equal)
                nc.vector.tensor_scalar(hi[:], edges[:, :, 0:P], 7, None,
                                        ALU.logical_shift_right).then_inc(v, 1)
                dve.wait_ge(v, base + 3 * i + 1)
                nc.vector.tensor_reduce(count[:, at], match[:], AX.X, ALU.add)
                nc.vector.scalar_tensor_tensor(key_hi[:], hi[:], 1.0, match[:], ALU.add, ALU.mult).then_inc(v, 1)
                dve.wait_ge(v, base + 3 * i + 2)
                nc.vector.tensor_scalar(hi[:], edges[:, :, 0:P], 127, None, ALU.bitwise_and).then_inc(v, 1)
                dve.wait_ge(v, base + 3 * i + 3)
                nc.vector.tensor_copy(key_lo[:], hi[:]).then_inc(keys_made, 1)
                dve.wait_ge(keys_made, i + 1)
            steps[0] = base + 3 * N_BATCHES
            link(nc.vector.tensor_copy(tile_of[:], count[:]))
            marks["count"] = steps[0]
            dve.wait_ge(turned, 2)
            link(nc.vector.tensor_tensor_scan(out=run[:], data0=ones[:], data1=p_a[0:C, 0:P], initial=0.0,
                                              op0=ALU.mult, op1=ALU.add))
            marks["run2"] = steps[0]
            dve.wait_ge(summed, 2)
            link(nc.vector.tensor_scalar(whole[:], run[:], p_a[0:C, 128:129], None, ALU.add))
            marks["whole2"] = steps[0]
            dve.wait_ge(turned, 3)
            link(nc.vector.tensor_copy(info[:, :, 1], p_a[:, 256:256 + C]))
            link(nc.vector.tensor_copy(info[:, :, 0], S.slot_id[:]))
            link(nc.vector.tensor_tensor(info_f[:], S.slot_id[:], node_of[:], ALU.subtract))
            link(nc.vector.tensor_scalar(info_f[:], info_f[:], float(INFO_SPARE - 1), None, ALU.add))
            link(nc.vector.tensor_tensor(info_f[:], info_f[:], going[:], ALU.mult))
            link(nc.vector.tensor_tensor(info_f[:], info_f[:], node_of[:], ALU.add))
            link(nc.vector.tensor_scalar(info_f[:], info_f[:], 1.0, None, ALU.add))
            link(nc.vector.tensor_copy(info_idx[:], info_f[:]))
            with dve.Fori(0, N_BATCHES) as i:
                at = bass.ds(i * B, B)
                dve.wait_ge(scattered, i * 16 * B)
                nc.vector.tensor_copy(idx_ring[:], info_idx[:, at])
                nc.vector.tensor_copy(info_ring[:], info[:, at, :]).then_inc(scat_ready, 1)

        @block.tensor
        def _(pe):
            pe.wait_ge(v, 2)
            nc.tensor.matmul(p_a[0:C, 0:1], S.before[0:C, 0:C], run[:, P - 1:P], start=True, stop=True).then_inc(summed, 1)
            pe.wait_ge(v, 3)
            nc.tensor.transpose(p_a[:, 128:128 + C], whole[:], S.ident[0:C, 0:C])
            nc.tensor.transpose(p_a[:, 256:256 + C], flags_f[:, 1, :], S.ident[0:C, 0:C]).then_inc(turned, 1)
            with pe.Fori(0, N_BATCHES) as i:
                for n, key in enumerate((key_hi, key_lo)):
                    pe.wait_ge(keys_kept, 2 * i + n)
                    pe.wait_ge(keys_made, i + 1)
                    for j in range(B):
                        last = nc.tensor.transpose(p_keys[:, j // 8, (j % 8) * P:(j % 8) * P + P],
                                                   key[:, j, :], S.ident_bf[:])
                    last.then_inc(keys_turned, 1)
            pe.wait_ge(v, marks["count"])
            nc.tensor.transpose(p_a[0:C, 0:P], count[:], S.ident[:]).then_inc(turned, 1)
            pe.wait_ge(v, marks["run2"])
            nc.tensor.matmul(p_a[0:C, 128:129], S.before[0:C, 0:C], run[:, P - 1:P], start=True, stop=True).then_inc(summed, 1)
            pe.wait_ge(v, marks["whole2"])
            nc.tensor.transpose(p_a[:, 256:256 + C], whole[:], S.ident[0:C, 0:C]).then_inc(turned, 1)

        @block.scalar
        def _(act):
            with act.Fori(0, N_BATCHES) as i:
                for n, key in enumerate((S.key_hi, S.key_lo)):
                    act.wait_ge(keys_turned, 2 * i + n + 1)
                    nc.scalar.copy(key[:, bass.ds(i * B * P, B * P)],
                                   p_keys[:].rearrange("p b e -> p (b e)")[:, 0:B * P]).then_inc(keys_kept, 1)

        @block.sync
        def _(sp):
            slot_rows = D.slot_flags[:].rearrange("v o -> (v o)")
            sp.dma_start(flags[:, 0, :], slot_rows[0:SLOTS].rearrange("(c p) -> c p", p=P)).then_inc(flags_loaded, 16)
            sp.dma_start(flags[:, 1, :], slot_rows[1:SLOTS + 1].rearrange("(c p) -> c p", p=P)).then_inc(flags_loaded, 16)
            sp.wait_ge(row_made, 1)
            sp.dma_start(D.info[0:1, :], first_row[:]).then_inc(row_stored, 16)
            sp.wait_ge(row_stored, 16)

        @block.gpsimd
        def _(pool):
            with pool.Fori(1, N_BATCHES + 1) as batch:
                pool.wait_ge(flags_loaded, 32)
                pool.wait_ge(ring_ready, batch)
                for j in range(B):
                    nc.gpsimd.indirect_dma_start(out=edges[:, j, :], out_offset=None, in_=D.edge_table[:, :],
                                                 in_offset=rows_of(idx_ring[:, j:j + 1])).then_inc(gathered, 16)
            with pool.Fori(1, N_BATCHES + 1) as batch:
                pool.wait_ge(flags_loaded, 32)
                pool.wait_ge(scat_ready, batch)
                for j in range(B):
                    nc.gpsimd.indirect_dma_start(out=D.info[:, :], out_offset=rows_of(idx_ring[:, j:j + 1]),
                                                 in_=info_ring[:, j, :], in_offset=None).then_inc(scattered, 16)
            pool.wait_ge(scattered, 16 * C)


def prepare_ends(nc, sb, sem, pb, D, S):
    own = sb("own", [P, NH, 2], i32)
    prev = sb("prev", [P, NH, 2], i32)
    end = sb("end", [P, NH], f32)
    begin = sb("begin", [P, NH], f32)
    deg = sb("deg", [P, NH], f32)
    tmp = sb("tmp", [P, NH], f32)

    loaded = sem("ends_info_loaded")
    v = sem("ends_vector_step")
    rooted = sem("ends_root_taken")
    steps = [0]

    def link(ins):
        steps[0] += 1
        ins.then_inc(v, 1)
        nc.vector.wait_ge(v, steps[0])
        return steps[0]

    with nc.Block() as block:
        @block.sync
        def _(sp):
            with nc.allow_non_contiguous_dma(reason="one row of two numbers per node, once"):
                sp.dma_start(own[:], D.info[1:1 + N_PAD, :].rearrange("(h p) c -> p h c", p=P)).then_inc(loaded, 16)
                sp.dma_start(prev[:], D.info[0:N_PAD, :].rearrange("(h p) c -> p h c", p=P)).then_inc(loaded, 16)

        @block.vector
        def _(dve):
            dve.wait_ge(loaded, 32)
            link(nc.vector.tensor_copy(S.last_slot[:], own[:, :, 0]))
            link(nc.vector.tensor_copy(end[:], own[:, :, 1]))
            link(nc.vector.tensor_copy(begin[:], prev[:, :, 1]))
            link(nc.vector.tensor_tensor(deg[:], end[:], begin[:], ALU.subtract))
            link(nc.vector.tensor_scalar(S.has_edges[:], deg[:], 0.0, None, ALU.is_gt))
            link(nc.vector.tensor_scalar(tmp[:], end[:], -1.0, 0.0, ALU.add, ALU.max))
            link(nc.vector.tensor_copy(S.last_edge[:], tmp[:]))
            link(nc.vector.tensor_scalar(tmp[:], S.node_id[:], float(E_PAD), None, ALU.add))
            link(nc.vector.tensor_tensor(begin[:], begin[:], tmp[:], ALU.subtract))
            link(nc.vector.tensor_tensor(begin[:], begin[:], S.has_edges[:], ALU.mult))
            link(nc.vector.tensor_tensor(begin[:], begin[:], tmp[:], ALU.add))
            link(nc.vector.tensor_copy(S.first_edge[:], begin[:]))
            ready = link(nc.vector.tensor_scalar(tmp[:], deg[:], 1.0, None, ALU.max))
            link(nc.vector.reciprocal(S.mean_scale[:], tmp[:]))
            dve.wait_ge(rooted, 1)
            link(nc.vector.reciprocal(deg[:], end[:]))
            link(nc.vector.tensor_tensor(S.norm_scale[:], deg[:], S.has_edges[:], ALU.mult))
            nc.vector.memset(S.one_scale[:], 1.0).then_inc(S.tables_done, 1)
            S.root_at = ready

        @block.scalar
        def _(act):
            act.wait_ge(v, S.root_at)
            nc.scalar.activation(end[:], tmp[:], ACT.Sqrt).then_inc(rooted, 1)


def build_matrix(nc, sb, sem, pb, D, S):
    QUARTERS, SLOTS_Q = 4, SUB // 4
    key2_hi = sb("key2_hi", [P, 2, SUB, 2], bf16)
    key2_lo = sb("key2_lo", [P, 2, SUB, 2], bf16)
    hot_hi = sb("hot_hi", [P, 2, SUB, NH], bf16)
    hot_lo = sb("hot_lo", [P, 2, SUB, P], bf16)
    stage = sb("stage", [P, 2, NH, SUB], bf16)
    counts = pb("counts", [P, 2, 2, 512], f32)

    paired = sem("matrix_keys_paired")
    hot = sem("matrix_one_hots_made")
    counted = [sem(f"matrix_sub{u}_quarters_counted") for u in range(2)]
    staged = [sem(f"matrix_half{u}_staged") for u in range(2)]
    stored = [sem(f"matrix_sub{u}_stored") for u in range(2)]

    def pair_keys(first, u):
        for two, key in ((key2_hi, S.key_hi), (key2_lo, S.key_lo)):
            nc.scalar.copy(two[:, u], key[:, bass.ds(first, SUB)].unsqueeze(2).to_broadcast([P, SUB, 2])).then_inc(paired, 1)

    with nc.Block() as block:
        @block.scalar
        def _(act):
            pair_keys(0, 0)
            with act.Fori(0, N_SUBS // 2) as i:
                for u in range(2):
                    s = i * 2 + u
                    act.wait_ge(hot, s * 2)
                    pair_keys(s * SUB + SUB, 1 - u)
                    act.wait_ge(stored[u], i * 32)
                    for r in range(QUARTERS):
                        act.wait_ge(counted[u], i * QUARTERS + (r + 1))
                        nc.scalar.copy(
                            stage[:, u, :, r * SLOTS_Q:(r + 1) * SLOTS_Q].rearrange("p h (b v) -> p h b v", b=2),
                            counts[:, r % 2, :, 0:4 * NH].rearrange("p b (v h) -> p h b v", h=NH)).then_inc(staged[r % 2], 1)

        @block.vector
        def _(dve):
            with dve.Fori(0, N_SUBS // 2) as i:
                for u in range(2):
                    dve.wait_ge(paired, i * 4 + (2 * u + 2))
                    dve.wait_ge(counted[u], i * QUARTERS)
                    for out, ramp, two, n in ((hot_hi, S.ramp_hi, key2_hi, NH), (hot_lo, S.ramp_lo, key2_lo, P)):
                        nc.vector.tensor_tensor(
                            out[:, u].rearrange("p v (h t) -> p v h t", t=2),
                            ramp[:].rearrange("p (h t) -> p h t", t=2).unsqueeze(1).to_broadcast([P, SUB, n // 2, 2]),
                            two[:, u].unsqueeze(2).to_broadcast([P, SUB, n // 2, 2]), ALU.is_equal).then_inc(hot, 1)

        @block.tensor
        def _(pe):
            with pe.Fori(0, N_SUBS // 2) as i:
                for u in range(2):
                    pe.wait_ge(hot, i * 4 + (2 * u + 2))
                    for r in range(QUARTERS):
                        pe.wait_ge(staged[r % 2], i * 4 + (2 * u + r // 2))
                        for n in range(SLOTS_Q):
                            slot = r * SLOTS_Q + n
                            last = nc.tensor.matmul(counts[:, r % 2, n // 4, NH * (n % 4):NH * (n % 4) + NH],
                                                    hot_lo[:, u, slot, :], hot_hi[:, u, slot, :],
                                                    start=True, stop=True)
                        last.then_inc(counted[u], 1)

        @block.sync
        def _(sp):
            with sp.Fori(0, N_SUBS // 2) as i:
                for u in range(2):
                    for half in range(2):
                        sp.wait_ge(staged[half], i * 4 + (2 * u + 2))
                    for rows, parts in zip(D.matrix, MATRIX_PARTS):
                        sp.dma_start(rows[bass.ds(i * 2 + u, 1), :, :, :].rearrange("s q p x -> p (s q) x"),
                                     stage[:, u].rearrange("p (q h) v -> p q (h v)", q=N_PARTS)[:, parts]).then_inc(stored[u], 16)
            for u in range(2):
                sp.wait_ge(stored[u], 32 * (N_SUBS // 2))


def attend_edges(nc, sb, sem, pb, D, S):
    EACH = GROUPS * LANES
    ring = sb("ring", [P, 2, GROUPS, LANES], i32)
    rows = sb("rows", [P, 2, GROUPS, LANES, 2 * FEAT], f32)
    pack = sb("pack", [P, 2, LANES, 2, GROUPS, FEAT], f32)
    neg = sb("neg0", [P, 2, CHUNK], bf16)
    peak = sb("peak", [P, 2, CHUNK + 1], f32)
    args = sb("args", [P, 2, 2, CHUNK], f32)
    weight = sb("weight", [P, 2, 2, CHUNK], f32)
    value = sb("value", [P, CHUNK], f32)
    num = sb("num", [P, 2, CHUNK], f32)
    den = sb("den", [P, 2, CHUNK], f32)
    out = sb("out", [P, 2, GROUPS, LANES, Y0_ROW], f32)
    p_val = pb("p_val", [P, CHUNK], f32)
    p_score = pb("p_score", [P, CHUNK], f32)
    p_num = pb("p_num", [P, LANES, P], f32)
    p_stat = pb("p_stat", [P, 2, LANES, GROUPS], f32)

    first_listed = sem("attend_first_sources_listed")
    listed = [sem(f"attend_sources{u}_listed") for u in range(2)]
    gathered = [sem(f"attend_rows{u}_gathered") for u in range(2)]
    packed = [sem(f"attend_rows{u}_packed") for u in range(2)]
    flagged = [sem(f"attend_flags{u}_loaded") for u in range(2)]
    turned = [sem(f"attend_rows{u}_turned") for u in range(2)]
    begun = sem("attend_first_states_made")
    v = sem("attend_vector_step")
    exponents = sem("attend_exponents_made")
    weighed = sem("attend_weighed")
    used = [sem(f"attend_rows{u}_used") for u in range(2)]
    scanned = sem("attend_scanned")
    back = [sem(f"attend_sums{u}_turned_back") for u in range(2)]
    emptied = sem("attend_emptied")
    stored = [sem(f"attend_out{u}_stored") for u in range(2)]
    V = 3
    STEPS = GROUP_CHUNKS

    with nc.Block() as block:
        @block.gpsimd
        def _(pool):
            with pool.Fori(0, STEPS // 2) as i:
                for u in range(2):
                    pool.wait_ge(first_listed, 2)
                    pool.wait_ge(packed[u], i)
                    pool.wait_ge(listed[u], i)
                    for g in range(GROUPS):
                        for j in range(LANES):
                            nc.gpsimd.indirect_dma_start(out=rows[:, u, g, j, :], out_offset=None, in_=D.table0[:, :],
                                                         in_offset=rows_of(ring[:, u, g, j:j + 1])).then_inc(gathered[u], 16)

        @block.tensor
        def _(pe):
            with pe.Fori(0, STEPS // 2) as i:
                for u in range(2):
                    c = i * 2 + u
                    pe.wait_ge(used[1 - u], i + u)
                    pe.wait_ge(packed[u], i + 1)
                    for j in range(LANES):
                        for p_out, w in ((p_val, 0), (p_score, 1)):
                            last = nc.tensor.transpose(p_out[:, j::LANES], pack[:, u, j, w].rearrange("p g f -> p (g f)"), S.ident[:])
                    last.then_inc(turned[u], 1)
                    pe.wait_ge(emptied, c * 2)
                    pe.wait_ge(scanned, c * 2 + 2)
                    for j in range(LANES):
                        nc.tensor.transpose(p_num[:, j, :], num[:, u, j::LANES], S.ident[:])
                    for j in range(LANES):
                        nc.tensor.matmul(p_stat[:, 0, j, :], den[:, u, j::LANES], S.group_pick[:], start=True, stop=True)
                        last = nc.tensor.matmul(p_stat[:, 1, j, :], peak[:, u, 1 + j::LANES], S.group_pick[:], start=True, stop=True)
                    last.then_inc(back[u], 1)

        @block.vector
        def _(dve):
            nc.vector.memset(peak[:, 0, 0:1], NEG)
            nc.vector.memset(num[:, 1, CHUNK - 1:CHUNK], 0.0)
            nc.vector.memset(den[:, 1, CHUNK - 1:CHUNK], 0.0).then_inc(begun, 1)
            dve.wait_ge(begun, 1)
            with dve.Fori(0, STEPS // 2) as i:
                for u in range(2):
                    c = i * 2 + u
                    dve.wait_ge(v, c * V)
                    dve.wait_ge(scanned, c * 2)
                    dve.wait_ge(back[u], i)
                    dve.wait_ge(flagged[u], i * 64 + 64)
                    dve.wait_ge(turned[u], i + 1)
                    nc.vector.tensor_tensor_scan(out=peak[:, u, 1:], data0=neg[:, u], data1=p_score[:],
                                                 initial=peak[:, u, 0:1], op0=ALU.add, op1=ALU.max).then_inc(v, 1)
                    dve.wait_ge(v, c * V + 1)
                    nc.vector.tensor_tensor(args[:, u, 0], peak[:, u, 0:CHUNK], neg[:, u], ALU.add).then_inc(v, 1)
                    nc.vector.tensor_tensor(args[:, u, 1], p_score[:], peak[:, u, 1:], ALU.subtract)
                    dve.wait_ge(v, c * V + 2)
                    nc.vector.tensor_tensor(args[:, u, 0], args[:, u, 0], peak[:, u, 1:], ALU.subtract).then_inc(exponents, 1)
                    nc.vector.tensor_copy(peak[:, 1 - u, 0:1], peak[:, u, CHUNK:]).then_inc(v, 1)
                    dve.wait_ge(weighed, c + 1)
                    nc.vector.tensor_tensor(value[:], weight[:, u, 1], p_val[:], ALU.mult).then_inc(used[u], 1)
                    nc.vector.tensor_tensor_scan(out=den[:, u], data0=weight[:, u, 0], data1=weight[:, u, 1],
                                                 initial=den[:, 1 - u, CHUNK - 1:], op0=ALU.mult, op1=ALU.add).then_inc(scanned, 1)
                    dve.wait_ge(used[u], i + 1)
                    nc.vector.tensor_tensor_scan(out=num[:, u], data0=weight[:, u, 0], data1=value[:],
                                                 initial=num[:, 1 - u, CHUNK - 1:], op0=ALU.mult, op1=ALU.add).then_inc(scanned, 1)

        @block.scalar
        def _(act):
            src_of = S.src_all[:, 0:E_PAD // P].rearrange("p (g c j) -> p g c j", g=GROUPS, j=LANES)
            src_after = S.src_all[:, 2 * LANES:2 * LANES + E_PAD // P].rearrange("p (g c j) -> p g c j", g=GROUPS, j=LANES)
            for u in range(2):
                nc.scalar.copy(ring[:, u], src_of[:, :, u, :]).then_inc(first_listed, 1)
            with act.Fori(0, STEPS // 2) as i:
                for u in range(2):
                    c = i * 2 + u
                    act.wait_ge(turned[u], i)
                    act.wait_ge(gathered[u], i * (16 * EACH) + 16 * EACH)
                    for w in range(2):
                        last = nc.scalar.copy(pack[:, u, :, w].rearrange("p j g f -> p g j f"),
                                              rows[:, u, :, :, FEAT * w:FEAT * (w + 1)])
                    last.then_inc(packed[u], 1)
                    nc.scalar.copy(ring[:, u].unsqueeze(2), src_after[:, :, bass.ds(c, 1), :]).then_inc(listed[u], 1)
                    act.wait_ge(exponents, c + 1)
                    nc.scalar.activation(weight[:, u], args[:, u], ACT.Exp).then_inc(weighed, 1)
                    act.wait_ge(stored[u], i * 16 * GROUPS)
                    act.wait_ge(back[u], i + 1)
                    nc.scalar.copy(out[:, u, :, :, 0:FEAT],
                                   p_num[:].rearrange("p j (g f) -> p g j f", g=GROUPS)).then_inc(emptied, 1)
                    nc.scalar.copy(out[:, u, :, :, FEAT:Y0_ROW],
                                   p_stat[:].rearrange("p w j g -> p g j w")).then_inc(emptied, 1)

        @block.sync
        def _(sp):
            with sp.Fori(0, STEPS // 2) as i:
                for u in range(2):
                    c = i * 2 + u
                    sp.wait_ge(used[u], i)
                    for g in range(GROUPS):
                        first = c * CHUNK + g * GROUP_EDGES
                        sp.dma_start(neg[FEAT * g:FEAT * (g + 1), u],
                                     D.neg[bass.ds(first, CHUNK)].unsqueeze(0).to_broadcast([FEAT, CHUNK])).then_inc(flagged[u], 16)
                    sp.wait_ge(emptied, c * 2 + 2)
                    for g in range(GROUPS):
                        first = c * CHUNK + g * GROUP_EDGES
                        sp.dma_start(D.scan0[bass.ds(first, CHUNK), :].rearrange("(p j) w -> p (j w)", j=LANES),
                                     out[:, u, g].rearrange("p j w -> p (j w)")).then_inc(stored[u], 16)
            for u in range(2):
                sp.wait_ge(stored[u], 16 * GROUPS * (STEPS // 2))


def normalize(nc, dve, act_done, act_go, link, T, S, out):
    link(nc.vector.tensor_reduce(S.stat[:, 0], T[:], AX.X, ALU.add))
    link(nc.vector.tensor_scalar(S.stat[:, 0], S.stat[:, 0], 1.0 / FEAT, None, ALU.mult))
    link(nc.vector.tensor_tensor(T[:], T[:], over_features(S.stat[:, 0]), ALU.subtract))
    link(nc.vector.tensor_tensor(S.square[:], T[:], T[:], ALU.mult))
    link(nc.vector.tensor_reduce(S.stat[:, 1], S.square[:], AX.X, ALU.add))
    nc.vector.tensor_scalar(S.stat[:, 1], S.stat[:, 1], 1.0 / FEAT, EPS, ALU.mult, ALU.add).then_inc(act_go, 1)
    dve.wait_ge(act_done, 1)
    link(nc.vector.reciprocal(S.stat[:, 0], S.stat[:, 1]))
    return link(nc.vector.tensor_tensor(out[:], T[:], over_features(S.stat[:, 0]), ALU.mult))


def finish_attention(nc, sb, sem, pb, D, S):
    S.square = sb("square_finish_attention", [P, NH, FEAT], f32)
    last = sb("last", [P, NH, Y0_ROW], f32)
    cut = sb("cut", [P, GROUPS - 1, Y0_ROW], f32)
    cut_dst = sb("cut_dst", [P, GROUPS - 1, 2], i32)
    cut_dst_f = sb("cut_dst_f", [P, GROUPS - 1, 2], f32)
    top = sb("top", [P, NH], f32)
    side = sb("side", [P, GROUPS, NH], f32)
    other = sb("other", [P, NH], f32)
    total = sb("total", [P, NH], f32)
    part = sb("part", [P, NH, FEAT], f32)

    cuts = sem("finish0_cuts_loaded")
    gathered = sem("finish0_ends_gathered")
    v = sem("finish0_vector_step")
    weighed = sem("finish0_weighed")
    root_go, root_done = sem("finish0_variance_made"), sem("finish0_root_taken")
    steps, at = [0], {}

    def link(ins):
        steps[0] += 1
        ins.then_inc(v, 1)
        nc.vector.wait_ge(v, steps[0])
        return steps[0]

    with nc.Block() as block:
        @block.sync
        def _(sp):
            for g in range(GROUPS - 1):
                e = (g + 1) * GROUP_EDGES - 1
                sp.dma_start(cut[:, g, :], D.scan0[e:e + 1, :].to_broadcast([P, Y0_ROW])).then_inc(cuts, 16)
                sp.dma_start(cut_dst[:, g, :], D.dst[e:e + 2].unsqueeze(0).to_broadcast([P, 2])).then_inc(cuts, 16)

        @block.gpsimd
        def _(pool):
            for h in range(NH):
                nc.gpsimd.indirect_dma_start(out=last[:, h, :], out_offset=None, in_=D.scan0[:, :],
                                             in_offset=rows_of(S.last_edge[:, h:h + 1])).then_inc(gathered, 16)

        @block.vector
        def _(dve):
            dve.wait_ge(cuts, 32 * (GROUPS - 1))
            link(nc.vector.tensor_copy(cut_dst_f[:], cut_dst[:]))
            dve.wait_ge(gathered, 16 * NH)
            link(nc.vector.tensor_copy(top[:], last[:, :, FEAT + 1]))
            for g in range(GROUPS - 1):
                link(nc.vector.tensor_scalar(other[:], S.node_id[:], cut_dst_f[:, g, 0:1], None, ALU.is_equal))
                link(nc.vector.tensor_scalar(side[:, g], S.node_id[:], cut_dst_f[:, g, 1:2], None, ALU.is_equal))
                link(nc.vector.tensor_tensor(other[:], other[:], side[:, g], ALU.mult))
                link(nc.vector.tensor_scalar(other[:], other[:], 1.0, -NEG, ALU.subtract, ALU.mult))
                link(nc.vector.tensor_scalar(side[:, g], other[:], cut[:, g, FEAT + 1:FEAT + 2], None, ALU.add))
                link(nc.vector.tensor_tensor(top[:], top[:], side[:, g], ALU.max))
            link(nc.vector.tensor_copy(side[:, GROUPS - 1], last[:, :, FEAT + 1]))
            at["side"] = link(nc.vector.tensor_tensor(side[:], side[:], top[:].unsqueeze(1).to_broadcast([P, GROUPS, NH]), ALU.subtract))
            dve.wait_ge(weighed, 1)
            own = side[:, GROUPS - 1]
            link(nc.vector.tensor_tensor(total[:], last[:, :, FEAT], own, ALU.mult))
            link(nc.vector.tensor_tensor(S.work[:], last[:, :, 0:FEAT], over_features(own), ALU.mult))
            for g in range(GROUPS - 1):
                link(nc.vector.scalar_tensor_tensor(total[:], side[:, g], cut[:, g, FEAT:FEAT + 1], total[:], ALU.mult, ALU.add))
                link(nc.vector.tensor_tensor(part[:], over_features(side[:, g]),
                                             cut[:, g, 0:FEAT].unsqueeze(1).to_broadcast([P, NH, FEAT]), ALU.mult))
                link(nc.vector.tensor_tensor(S.work[:], S.work[:], part[:], ALU.add))
            link(nc.vector.reciprocal(other[:], total[:]))
            link(nc.vector.tensor_tensor(other[:], other[:], S.has_edges[:], ALU.mult))
            link(nc.vector.tensor_tensor(S.work[:], S.work[:], over_features(other[:]), ALU.mult))
            link(nc.vector.tensor_tensor(S.work[:], S.work[:], S.base[:], ALU.add))
            normalize(nc, dve, root_done, root_go, link, S.work, S, S.x)

        @block.scalar
        def _(act):
            act.wait_ge(v, at["side"])
            nc.scalar.activation(side[:], side[:], ACT.Exp).then_inc(weighed, 1)
            act.wait_ge(root_go, 1)
            nc.scalar.activation(S.stat[:, 1], S.stat[:, 1], ACT.Sqrt).then_inc(root_done, 1)


def propagate(nc, sb, sem, pb, D, S, name, turn, before, after):
    ROUNDS = 3
    SUBS = BLOCK // SUB
    split = sb("split", [P, NH, 3, FEAT], bf16)
    part = sb("part", [P, N_PARTS, SUBS, HI_PART * SUB], bf16)
    scaled = S.square = sb("scaled", [P, NH, FEAT], f32)
    sums = sb("sums", [P, NH, FEAT], f32)
    keep = sb("keep", [3 * FEAT, BLOCK], i32)
    slot_sum = sb("slot_sum", [3 * FEAT, BLOCK], f32)
    carry = sb("carry", [3 * FEAT, 1], f32)
    out = sb("out", [P, LANES, FEAT], f32)
    p_dense = pb("p_dense", [3 * FEAT, BLOCK], f32)
    p_out = pb("p_out", [P, LANES, FEAT], f32)

    loaded, used = S.part_loaded, S.part_multiplied
    splitted, flagged, scanned, carried, back, emptied, stored, gathered = S.block_sems
    first = turn * ROUNDS
    v = sem(name + "_vector_step")
    root_go, root_done = sem(name + "_variance_made"), sem(name + "_root_taken")
    steps = [0]
    V = 6

    def link(ins):
        steps[0] += 1
        ins.then_inc(v, 1)
        nc.vector.wait_ge(v, steps[0])

    with nc.Block() as block:
        @block.sync
        def _(sp):
            with sp.Fori(first, first + ROUNDS) as k:
                with sp.Fori(0, N_BLOCKS) as b:
                    for q in range(N_PARTS):
                        sp.wait_ge(used[q], k * N_BLOCKS + b)
                        rows = D.matrix[0] if q < MATRIX_PARTS[0].stop else D.matrix[1]
                        sp.dma_start(part[:, q], rows[bass.ds(b * SUBS, SUBS), q % MATRIX_PARTS[0].stop, :, :]
                                     .rearrange("s p x -> p s x")).then_inc(loaded[q], 16)

        @block.scalar
        def _(act):
            with act.Fori(first, first + ROUNDS) as k:
                with act.Fori(0, N_BLOCKS) as b:
                    n = k * N_BLOCKS + b
                    act.wait_ge(scanned, n)
                    act.dma_start(keep[:], D.slot_flags[bass.ds(b * BLOCK, BLOCK), :].rearrange("v o -> o v")
                                  .to_broadcast([3 * FEAT, BLOCK])).then_inc(flagged, 16)
                    act.wait_ge(stored, n * 16)
                    act.wait_ge(back, n + 1)
                    nc.scalar.copy(out[:], p_out[:]).then_inc(emptied, 1)
                    act.wait_ge(emptied, n + 1)
                    act.dma_start(D.slot_sums[bass.ds(b * BLOCK, BLOCK), :].rearrange("(p j) f -> p (j f)", j=LANES),
                                  out[:].rearrange("p j f -> p (j f)")).then_inc(stored, 16)
            act.wait_ge(root_go, 1)
            nc.scalar.activation(S.stat[:, 1], S.stat[:, 1], ACT.Sqrt).then_inc(root_done, 1)

        @block.tensor
        def _(pe):
            with pe.Fori(first, first + ROUNDS) as k:
                with pe.Fori(0, N_BLOCKS) as b:
                    n = k * N_BLOCKS + b
                    pe.wait_ge(splitted, k + 1)
                    pe.wait_ge(scanned, n)
                    for q in range(N_PARTS):
                        pe.wait_ge(loaded[q], n * 16 + 16)
                        here = part[:, q].rearrange("p s (h v) -> p s h v", v=SUB)
                        for m in range(HI_PART):
                            h = q * HI_PART + m
                            last = nc.tensor.matmul(p_dense[:], split[:, h].rearrange("p c f -> p (c f)"), here[:, :, m, :],
                                                    start=(h == 0), stop=(h == NH - 1))
                            if m == HI_PART - 1:
                                last.then_inc(used[q], 1)
                    pe.wait_ge(emptied, n)
                    pe.wait_ge(scanned, n + 1)
                    for j in range(LANES):
                        last = nc.tensor.matmul(p_out[:, j, :], slot_sum[:, j::LANES], S.part_sum[:], start=True, stop=True)
                    last.then_inc(back, 1)

        @block.vector
        def _(dve):
            nc.vector.memset(carry[:], 0.0)
            link(nc.vector.tensor_scalar(S.work[:], S.x[:], 1.25, None, ALU.mult))
            link(nc.vector.tensor_tensor(scaled[:], S.x[:], over_features(before[:]), ALU.mult))
            base = steps[0]
            with dve.Fori(first, first + ROUNDS) as k:
                def step(ins, nth):
                    ins.then_inc(v, 1)
                    dve.wait_ge(v, k * V + (base + nth - first * V))

                step(nc.vector.tensor_copy(split[:, :, 0, :], scaled[:]), 1)
                step(nc.vector.tensor_tensor(scaled[:], scaled[:], split[:, :, 0, :], ALU.subtract), 2)
                step(nc.vector.tensor_copy(split[:, :, 1, :], scaled[:]), 3)
                step(nc.vector.tensor_tensor(scaled[:], scaled[:], split[:, :, 1, :], ALU.subtract), 4)
                nc.vector.tensor_copy(split[:, :, 2, :], scaled[:]).then_inc(splitted, 1)
                with dve.Fori(0, N_BLOCKS) as b:
                    n = k * N_BLOCKS + b
                    dve.wait_ge(flagged, n * 16 + 16)
                    dve.wait_ge(carried, n)
                    dve.wait_ge(back, n)
                    dve.wait_ge(used[N_PARTS - 1], n + 1)
                    nc.vector.tensor_tensor_scan(out=slot_sum[:], data0=keep[:], data1=p_dense[:], initial=carry[:, 0:1],
                                                 op0=ALU.mult, op1=ALU.add).then_inc(scanned, 1)
                    dve.wait_ge(scanned, n + 1)
                    nc.vector.tensor_copy(carry[:], slot_sum[:, BLOCK - 1:]).then_inc(carried, 1)
                dve.wait_ge(gathered, (k + 1) * 16 * NH)
                dve.wait_ge(splitted, k + 1)
                step(nc.vector.tensor_tensor(sums[:], sums[:], over_features(after[:]), ALU.mult), 5)
                nc.vector.tensor_tensor(scaled[:], sums[:], over_features(before[:]), ALU.mult)
                step(nc.vector.scalar_tensor_tensor(S.work[:], sums[:], 0.25, S.work[:], ALU.mult, ALU.add), 6)
            steps[0] = base + ROUNDS * V
            normalize(nc, dve, root_done, root_go, link, S.work, S, S.x)

        @block.gpsimd
        def _(pool):
            with pool.Fori((first + 1) * 16 * N_BLOCKS, (first + ROUNDS + 1) * 16 * N_BLOCKS, 16 * N_BLOCKS) as blocks_stored:
                pool.wait_ge(S.tables_done, 1)
                pool.wait_ge(stored, blocks_stored)
                for h in range(NH):
                    nc.gpsimd.indirect_dma_start(out=sums[:, h, :], out_offset=None, in_=D.slot_sums[:, :],
                                                 in_offset=rows_of(S.last_slot[:, h:h + 1])).then_inc(gathered, 16)


def spread_nodes(nc, sb, sem, pb, D, S):
    stored = sem("spread_table_stored")
    placed = sem("spread_rows_placed")
    with nc.Block() as block:
        @block.sync
        def _(sp):
            sp.dma_start(D.table2[:, :].rearrange("(h p) f -> p h f", p=P), S.x[:]).then_inc(stored, 16)
            sp.wait_ge(stored, 16)

        @block.gpsimd
        def _(pool):
            for h in range(NH):
                nc.gpsimd.indirect_dma_start(out=D.inject[:, :], out_offset=rows_of(S.first_edge[:, h:h + 1]),
                                             in_=S.x[:, h, :], in_offset=None).then_inc(placed, 16)
            pool.wait_ge(placed, 16 * NH)


def judge_edges(nc, sb, sem, pb, D, S):
    WIDE = 3 * FEAT
    ring = sb("ring2", [P, 2, LANES], i32)
    rows = sb("rows2", [P, 2, LANES, WIDE], f32)
    flags = sb("flags2", [WIDE, 2, CHUNK], bf16)
    feat = sb("feat2", [WIDE, 2, CHUNK], f32)
    hidden = sb("hidden2", [HID, 2, CHUNK], f32)
    best = sb("best2", [FEAT, 2, CHUNK], f32)
    out = sb("out2", [P, 2, LANES, FEAT], f32)
    w1 = sb("w1_2", [WIDE, HID], f32)
    w2 = sb("w2_2", [HID, P], f32)
    b1 = sb("b1_2", [HID, 1], f32)
    p_feat = pb("p_feat", [WIDE, 2, CHUNK], f32)
    p_hid = pb("p_hid", [HID, CHUNK], f32)
    p_msg = pb("p_msg", [P, 2, CHUNK], f32)
    p_back = pb("p_back", [P, LANES, FEAT], f32)

    def pair_of(what):
        return [sem(f"judge_{what}_{u}") for u in range(2)]

    begun = sem("judge_first_states_made")
    w_loaded = sem("judge_weights_loaded")
    first_listed = sem("judge_first_sources_listed")
    listed, gathered, loaded, turned = pair_of("sources_listed"), pair_of("rows_gathered"), pair_of("rows_loaded"), pair_of("rows_turned")
    copied, held, lifted, rectified = pair_of("features_copied"), pair_of("dst_held"), pair_of("hidden_multiplied"), pair_of("hidden_rectified")
    sent, topped, back = pair_of("messages_multiplied"), pair_of("maxima_scanned"), pair_of("maxima_turned_back")
    emptied, stored, flagged = pair_of("out_emptied"), pair_of("out_stored"), pair_of("neg_flags_loaded")
    STEPS = CHUNKS
    assert STEPS % 2 == 0
    last_edges = N_EDGES - (STEPS - 1) * CHUNK

    def skewed(eng, stage):
        with eng.Fori(0, STEPS // 2 - 1) as i:
            stage(i * 2 + 1, 1, i)
            stage(i * 2 + 2, 0, i + 1)
        stage(STEPS - 1, 1, STEPS // 2 - 1)

    def before(u, n):
        return (0, n) if u else (1, n - 1)

    with nc.Block() as block:
        @block.gpsimd
        def _(pool):
            with pool.Fori(0, STEPS // 2) as i:
                for u in range(2):
                    pool.wait_ge(first_listed, 2)
                    pool.wait_ge(turned[u], i)
                    pool.wait_ge(listed[u], i)
                    for j in range(LANES):
                        nc.gpsimd.indirect_dma_start(out=rows[:, u, j, 0:FEAT], out_offset=None, in_=D.table2[:, :],
                                                     in_offset=rows_of(ring[:, u, j:j + 1])).then_inc(gathered[u], 16)

        @block.sync
        def _(sp):
            sp.wait_ge(begun, 1)
            sp.dma_start(w1[0:FEAT, :], D.W1[0:FEAT, :]).then_inc(w_loaded, 16)
            sp.dma_start(w1[FEAT:2 * FEAT, :], D.W1[2 * FEAT:3 * FEAT, :]).then_inc(w_loaded, 16)
            sp.dma_start(w1[2 * FEAT:3 * FEAT, :], D.W1[FEAT:2 * FEAT, :]).then_inc(w_loaded, 16)
            sp.dma_start(w2[:, 0:FEAT], D.W2[:, :]).then_inc(w_loaded, 16)
            sp.dma_start(b1[:], D.b1[:].unsqueeze(1), allow_slow_non_contiguous=True).then_inc(w_loaded, 16)

            def load(k, u, n, before_last):
                at = bass.ds(k * CHUNK, CHUNK)
                sp.wait_ge(turned[u], before_last)
                sp.wait_ge(held[u], before_last)
                sp.dma_start(rows[0:n // LANES, u, :, FEAT:2 * FEAT],
                             D.attr[bass.ds(k * CHUNK, n), :].rearrange("(p j) f -> p j f", j=LANES)).then_inc(loaded[u], 16)
                sp.dma_start(rows[:, u, :, 2 * FEAT:WIDE],
                             D.inject[at, :].rearrange("(p j) f -> p j f", j=LANES)).then_inc(loaded[u], 16)
                sp.dma_start(flags[2 * FEAT:WIDE, u], D.keep[at].unsqueeze(0).to_broadcast([FEAT, CHUNK])).then_inc(loaded[u], 16)
                sp.wait_ge(begun, 1)
                sp.wait_ge(topped[u], before_last)
                sp.dma_start(flags[0:FEAT, u], D.neg[at].unsqueeze(0).to_broadcast([FEAT, CHUNK])).then_inc(flagged[u], 16)

            with sp.Fori(0, STEPS // 2 - 1) as i:
                for u in range(2):
                    load(i * 2 + u, u, CHUNK, i)
            for u in range(2):
                load(STEPS - 2 + u, u, last_edges if u else CHUNK, STEPS // 2 - 1)

        @block.tensor
        def _(pe):
            def turn(u, n):
                pe.wait_ge(copied[u], n)
                pe.wait_ge(held[u], n)
                pe.wait_ge(loaded[u], n * 48 + 48)
                pe.wait_ge(gathered[u], n * (16 * LANES) + 16 * LANES)
                for j in range(LANES):
                    last = nc.tensor.transpose(p_feat[:, u, j::LANES], rows[:, u, j, :], S.ident[:])
                last.then_inc(turned[u], 1)

            def lift(u, n):
                pe.wait_ge(rectified[1 - u], n if u == 0 else n + 1)
                pe.wait_ge(copied[u], n + 1)
                pe.wait_ge(held[u], n + 1)
                nc.tensor.matmul(p_hid[:], w1[:], feat[:, u], start=True, stop=True).then_inc(lifted[u], 1)

            def send(u, n):
                pe.wait_ge(topped[u], n)
                pe.wait_ge(rectified[u], n + 1)
                nc.tensor.matmul(p_msg[:, u], w2[:], hidden[:, u], start=True, stop=True).then_inc(sent[u], 1)

            def turn_back(u, n):
                pe.wait_ge(w_loaded, 80)
                pe.wait_ge(emptied[1 - u], n if u == 0 else n + 1)
                pe.wait_ge(topped[u], n + 1)
                for j in range(LANES):
                    last = nc.tensor.transpose(p_back[:, j, :], best[:, u, j::LANES], S.ident[0:FEAT, 0:FEAT])
                last.then_inc(back[u], 1)

            def stage(k, u, n):
                turn(u, n)
                send(*before(u, n))
                lift(u, n)
                turn_back(*before(u, n))

            pe.wait_ge(w_loaded, 80)
            turn(0, 0)
            lift(0, 0)
            skewed(pe, stage)
            send(1, STEPS // 2 - 1)
            turn_back(1, STEPS // 2 - 1)

        @block.vector
        def _(dve):
            nc.vector.memset(rows[:, 1, :, FEAT:2 * FEAT], 0.0)
            nc.vector.memset(w2[:], 0.0)
            nc.vector.memset(feat[2 * FEAT:WIDE, 1, CHUNK - 1:], 0.0)
            nc.vector.memset(best[:, 1, CHUNK - 1:], NEG).then_inc(begun, 1)
            dve.wait_ge(begun, 1)

            def hold(u, n):
                dve.wait_ge(lifted[u], n)
                dve.wait_ge(held[1 - u], n if u == 0 else n + 1)
                dve.wait_ge(loaded[u], n * 48 + 48)
                dve.wait_ge(turned[u], n + 1)
                nc.vector.tensor_tensor_scan(out=feat[2 * FEAT:WIDE, u], data0=flags[2 * FEAT:WIDE, u],
                                             data1=p_feat[2 * FEAT:WIDE, u],
                                             initial=feat[2 * FEAT:WIDE, 1 - u, CHUNK - 1:],
                                             op0=ALU.mult, op1=ALU.add).then_inc(held[u], 1)

            def top(u, n):
                dve.wait_ge(back[u], n)
                dve.wait_ge(topped[1 - u], n if u == 0 else n + 1)
                dve.wait_ge(flagged[u], n * 16 + 16)
                dve.wait_ge(sent[u], n + 1)
                nc.vector.tensor_tensor_scan(out=best[:, u], data0=flags[0:FEAT, u], data1=p_msg[0:FEAT, u],
                                             initial=best[:, 1 - u, CHUNK - 1:],
                                             op0=ALU.add, op1=ALU.max).then_inc(topped[u], 1)

            def stage(k, u, n):
                hold(u, n)
                top(*before(u, n))

            hold(0, 0)
            skewed(dve, stage)
            top(1, STEPS // 2 - 1)

        @block.scalar
        def _(act):
            for u in range(2):
                nc.scalar.copy(ring[:, u], S.src_all[:, u * LANES:(u + 1) * LANES]).then_inc(first_listed, 1)
            act.wait_ge(w_loaded, 80)

            def copy(k, u, n):
                act.wait_ge(gathered[u], n * (16 * LANES) + 16 * LANES)
                nc.scalar.copy(ring[:, u], S.src_all[:, bass.ds(k * LANES + 2 * LANES, LANES)]).then_inc(listed[u], 1)
                act.wait_ge(lifted[u], n)
                act.wait_ge(turned[u], n + 1)
                nc.scalar.copy(feat[0:2 * FEAT, u], p_feat[0:2 * FEAT, u]).then_inc(copied[u], 1)

            def rectify(u, n):
                act.wait_ge(sent[u], n)
                act.wait_ge(lifted[u], n + 1)
                nc.scalar.activation(hidden[:, u], p_hid[:], ACT.Relu, bias=b1[:, 0:1]).then_inc(rectified[u], 1)

            def put_out(k, u, n):
                act.wait_ge(stored[u], n * 16)
                act.wait_ge(back[u], n + 1)
                nc.scalar.copy(out[:, u], p_back[:]).then_inc(emptied[u], 1)
                act.wait_ge(emptied[u], n + 1)
                act.dma_start(D.scan2[bass.ds(k * CHUNK, CHUNK), :].rearrange("(p j) f -> p (j f)", j=LANES),
                              out[:, u].rearrange("p j f -> p (j f)")).then_inc(stored[u], 16)

            def stage(k, u, n):
                copy(k, u, n)
                rectify(u, n)
                put_out(k - 1, *before(u, n))

            copy(0, 0, 0)
            rectify(0, 0)
            skewed(act, stage)
            put_out(STEPS - 1, 1, STEPS // 2 - 1)
            for u in range(2):
                act.wait_ge(stored[u], 16 * (STEPS // 2))


def finish_judging(nc, sb, sem, pb, D, S):
    S.square = sb("square_finish_judging", [P, NH, FEAT], f32)
    best = sb("best_node", [P, NH, FEAT], f32)
    b2 = sb("b2_all", [P, FEAT], f32)
    none = sb("none", [P, NH], f32)
    b2_loaded = sem("finish2_b2_loaded")
    gathered = sem("finish2_ends_gathered")
    v = sem("finish2_vector_step")
    root_go, root_done = sem("finish2_variance_made"), sem("finish2_root_taken")
    steps = [0]

    def link(ins):
        steps[0] += 1
        ins.then_inc(v, 1)
        nc.vector.wait_ge(v, steps[0])
        return steps[0]

    with nc.Block() as block:
        @block.sync
        def _(sp):
            sp.dma_start(b2[:], D.b2[:].unsqueeze(0).to_broadcast([P, FEAT])).then_inc(b2_loaded, 16)

        @block.gpsimd
        def _(pool):
            for h in range(NH):
                nc.gpsimd.indirect_dma_start(out=best[:, h, :], out_offset=None, in_=D.scan2[:, :],
                                             in_offset=rows_of(S.last_edge[:, h:h + 1])).then_inc(gathered, 16)

        @block.vector
        def _(dve):
            link(nc.vector.tensor_scalar(none[:], S.has_edges[:], 1.0, -2.0 * NEG, ALU.subtract, ALU.mult))
            dve.wait_ge(b2_loaded, 16)
            dve.wait_ge(gathered, 16 * NH)
            link(nc.vector.tensor_tensor(best[:], best[:], b2[:].unsqueeze(1).to_broadcast([P, NH, FEAT]), ALU.add))
            link(nc.vector.tensor_tensor(best[:], best[:], over_features(none[:]), ALU.add))
            link(nc.vector.tensor_tensor(best[:], best[:], S.x[:], ALU.max))
            link(nc.vector.tensor_tensor(S.work[:], best[:], S.x[:], ALU.add))
            normalize(nc, dve, root_done, root_go, link, S.work, S, S.x)

        @block.scalar
        def _(act):
            act.wait_ge(root_go, 1)
            nc.scalar.activation(S.stat[:, 1], S.stat[:, 1], ACT.Sqrt).then_inc(root_done, 1)


def write_out(nc, sem, D, S):
    stored = sem("output_stored")
    full = N_NODES // P
    with nc.Block() as block:
        @block.sync
        def _(sp):
            sp.dma_start(D.out[0:full * P, :].rearrange("(h p) f -> p h f", p=P), S.x[:, 0:full, :]).then_inc(stored, 16)
            sp.dma_start(D.out[full * P:N_NODES, :], S.x[0:N_NODES - full * P, full, :]).then_inc(stored, 16)
            sp.wait_ge(stored, 32)


def graph_layers(nc, x, src, dst, attr, w1_W, w1_b, w2_W, w2_b, a, W1, b1, W2, b2, out, upto=99, only=None):
    D = Names()
    D.x, D.src, D.dst, D.attr, D.out = x, src, dst, attr, out
    D.w1_W, D.w1_b, D.w2_W, D.w2_b, D.a = w1_W, w1_b, w2_W, w2_b, a
    D.W1, D.b1, D.W2, D.b2 = W1, b1, W2, b2

    def dram(name, shape, dt):
        return nc.dram_tensor(name, shape, dt, kind="Internal").ap()

    D.slot_flags = dram("slot_flags", [SLOTS + P, 1], i32)
    D.edge_table = dram("edge_table", [TILES, 2 * P], i32)
    D.keep = dram("keep_flags", [E_PAD], bf16)
    D.neg = dram("neg_flags", [E_PAD], bf16)
    D.inject = dram("inject", [E_PAD + N_PAD, FEAT], f32)
    D.table0 = dram("table0", [N_PAD, 2 * FEAT], f32)
    D.table2 = dram("table2", [N_PAD, FEAT], f32)
    D.info = dram("info", [INFO_SPARE + SLOTS, 2], i32)
    D.matrix = [dram(f"matrix{n}", [N_SUBS, parts.stop - parts.start, P, HI_PART * SUB], bf16)
                for n, parts in enumerate(MATRIX_PARTS)]
    D.scan0 = dram("scan0", [E_PAD, Y0_ROW], f32)
    D.scan2 = dram("scan2", [CHUNKS * CHUNK, FEAT], f32)
    D.slot_sums = dram("slot_sums", [SLOTS, FEAT], f32)

    with ExitStack() as whole:
        def keeper(stack, alloc, prefix=""):
            return lambda name, *spec: stack.enter_context(alloc(prefix + name, *spec))

        sb = keeper(whole, nc.sbuf_tensor)
        sem = keeper(whole, nc.semaphore)
        S = Names()
        S.tables_done = sem("tables_done")
        S.part_loaded = [sem(f"propagate_part{q}_loaded") for q in range(N_PARTS)]
        S.part_multiplied = [sem(f"propagate_part{q}_multiplied") for q in range(N_PARTS)]
        S.block_sems = [sem("propagate_" + what) for what in (
            "x_split", "flags_loaded", "block_scanned", "carry_kept", "block_turned_back", "block_emptied",
            "block_stored", "sums_gathered")]
        S.x = sb("x_sb", [P, NH, FEAT], f32)
        S.base = sb("base", [P, NH, FEAT], f32)
        S.work = sb("work", [P, NH, FEAT], f32)
        S.stat = sb("stat", [P, 2, NH], f32)
        S.ident = sb("ident", [P, P], f32)
        S.ident_bf = sb("ident_bf", [P, P], bf16)
        S.before = sb("before", [P, P], f32)
        S.group_pick = sb("group_pick", [P, GROUPS], f32)
        S.part_sum = sb("part_sum", [3 * FEAT, FEAT], f32)
        S.ramp_hi = sb("ramp_hi", [P, NH], bf16)
        S.ramp_lo = sb("ramp_lo", [P, P], bf16)
        S.slot_id = sb("slot_id", [P, SLOT_COLS], f32)
        S.node_id = sb("node_id", [P, NH], f32)
        S.src_all = sb("src_all", [P, E_PAD // P + 2 * LANES], i32)
        S.has_edges, S.mean_scale, S.norm_scale, S.one_scale = (
            sb(name, [P, NH], f32) for name in ("has_edges", "mean_scale", "norm_scale", "one_scale"))
        S.last_slot, S.last_edge, S.first_edge = (
            sb(name, [P, NH], i32) for name in ("last_slot", "last_edge", "first_edge"))

        def stage(build, *more):
            if only and build.__name__ not in only:
                return
            with ExitStack() as local:
                prefix = "_".join([build.__name__, *more[:1], ""])
                build(nc, keeper(local, nc.sbuf_tensor, prefix), sem, keeper(local, nc.psum_tensor, prefix), D, S, *more)

        stages = [lambda: stage(prepare_constants), lambda: stage(prepare_nodes)]

        def matrix():
            with ExitStack() as local:
                S.key_hi = keeper(local, nc.sbuf_tensor)("key_hi_all", [P, SLOTS + SUB], bf16)
                S.key_lo = keeper(local, nc.sbuf_tensor)("key_lo_all", [P, SLOTS + SUB], bf16)
                stage(prepare_slots)
                stage(prepare_ends)
                stage(build_matrix)
        stages += [matrix, lambda: stage(attend_edges), lambda: stage(finish_attention),
                   lambda: stage(propagate, "mean", 0, S.one_scale, S.mean_scale),
                   lambda: stage(spread_nodes), lambda: stage(judge_edges), lambda: stage(finish_judging),
                   lambda: stage(propagate, "norm", 1, S.norm_scale, S.norm_scale)]
        for run in stages[:upto]:
            run()
        write_out(nc, sem, D, S)


_INS = ["x", "src", "dst", "edge_attr_32", "L0_gnn_w1_W", "L0_gnn_w1_b", "L0_gnn_w2_W", "L0_gnn_w2_b", "L0_gnn_a",
        "L2_gnn_W1", "L2_gnn_b1", "L2_gnn_W2", "L2_gnn_b2"]


def kernel(**inputs):
    import numpy as _np
    import concourse.bacc as _bacc
    from concourse import mybir as _mybir
    from concourse.bass_utils import run_bass_kernel_spmd as _run

    nc = _bacc.Bacc("TRN2", target_bir_lowering=False, num_devices=1)
    arrays, args = {}, []
    for name in _INS:
        a = _np.ascontiguousarray(inputs[name])
        arrays[f"in_{name}_dram"] = a
        args.append(nc.dram_tensor(f"in_{name}_dram", a.shape, _mybir.dt.from_np(a.dtype), kind="ExternalInput").ap())
    args.append(nc.dram_tensor("out_dram", (N_NODES, FEAT), _mybir.dt.float32, kind="ExternalOutput").ap())
    graph_layers(nc, *args)
    r = _run(nc, [arrays], core_ids=[0])
    return r.results[0]["out_dram"]
```

```python
import concourse.bass as bass
from concourse import mybir
from contextlib import ExitStack

P = 128
N_NODES, N_EDGES, FEAT, HID = 12500, 400000, 32, 64
NH = -(-N_NODES // P)
N_PAD = NH * P
TILES = N_EDGES // P
SUB = 32
BLOCK = 512
N_BLOCKS = -(-(TILES + N_NODES - 1) // BLOCK)
SLOTS = N_BLOCKS * BLOCK
SLOT_COLS = SLOTS // P
HI_PART = 14
N_PARTS = NH // HI_PART
PAIR = 2 * SUB
CHUNK = 512
LANES = CHUNK // P
GROUPS = 4
CHUNKS = -(-N_EDGES // CHUNK)
GROUP_CHUNKS = -(-CHUNKS // GROUPS)
GROUP_EDGES = GROUP_CHUNKS * CHUNK
E_PAD = GROUPS * GROUP_EDGES
ATTEND_STEPS, COUNT_SUBS = 4, 10
COUNTED_PAIRS = GROUP_CHUNKS // ATTEND_STEPS * COUNT_SUBS // 2
STAGES = 3
PLACES = 4
SCALAR_PARTS, VECTOR_PARTS = (0, 1, 3), (2, 4, 5, 6)
SLOT_BATCH = 31
N_BATCHES = SLOT_COLS // SLOT_BATCH
INFO_SPARE = 13056
NEG = -1.0e30
EPS = 1e-5
Y0_ROW = FEAT + 2

f32, bf16, i32, u8 = mybir.dt.float32, mybir.dt.bfloat16, mybir.dt.int32, mybir.dt.uint8
ALU = mybir.AluOpType
ACT = mybir.ActivationFunctionType
AX = mybir.AxisListType


class Names:
    pass


def rows_of(ap):
    return bass.IndirectOffsetOnAxis(ap=ap, axis=0)


def over_features(ap):
    return ap.unsqueeze(2).to_broadcast([P, NH, FEAT])


def prepare_constants(nc, sb, sem, pb, D, S):
    zeros = sb("zeros", [P, 7168], f32)
    ones_i = sb("ones_i", [P, 1], i32)
    theta = sb("theta", [P, 25], i32)
    theta_t = sb("theta_t", [P, 25], i32)
    tile_head_cols = -(-(TILES - 1) // P)
    src_pad = sb("src_pad", [P, LANES], i32)
    dst_run = TILES
    dst_sb = sb("dst_sb", [P, dst_run + 1], i32)
    keep = sb("keep", [P, dst_run], bf16)
    neg = sb("neg", [P, dst_run], bf16)
    zero_bf = sb("zero_bf", [P, 128], bf16)

    made = sem("const_made")
    zeroed = sem("const_zeros_made")
    flags_zero = sem("const_slot_flags_zeroed")
    inject_zero = sem("const_inject_zeroed")
    rest_zero = sem("const_matrix_rest_zeroed")
    heads_loaded = sem("const_tile_heads_loaded")
    heads_added = sem("const_tile_heads_added")
    flags_set = sem("const_slot_flags_set")
    table_copied = sem("const_edge_table_copied")
    dst_loaded = sem("const_dst_loaded")
    dst_edge = sem("const_dst_edge_made")
    keep_made = sem("const_keep_made")
    neg_made = sem("const_neg_made")
    flags_stored = sem("const_scan_flags_stored")
    src_zero = sem("const_src_index_zeroed")
    src_loaded = sem("const_src_index_loaded")

    with nc.Block() as block:
        @block.sync
        def _(sp):
            heads = D.dst[:].rearrange("(t e) -> t e", e=P)[1:TILES, 0:1]
            full = (tile_head_cols - 1) * P
            sp.dma_start(theta[:, 0:tile_head_cols - 1],
                         heads[0:full].rearrange("(r p) o -> p (r o)", p=P),
                         allow_slow_non_contiguous=True).then_inc(heads_loaded, 16)
            sp.dma_start(theta[0:TILES - 1 - full, tile_head_cols - 1:tile_head_cols],
                         heads[full:TILES - 1],
                         allow_slow_non_contiguous=True).then_inc(heads_loaded, 16)
            sp.dma_start(D.edge_table[:, 0:P], D.src[:].rearrange("(t e) -> t e", e=P)).then_inc(table_copied, 16)
            sp.dma_start(D.edge_table[:, P:2 * P], D.dst[:].rearrange("(t e) -> t e", e=P)).then_inc(table_copied, 16)
            runs = D.dst[:].rearrange("(p i) -> p i", p=P)
            sp.wait_ge(dst_edge, 1)
            sp.dma_start(dst_sb[:, 1:dst_run + 1], runs).then_inc(dst_loaded, 16)
            sp.dma_start(dst_sb[1:P, 0:1], runs[0:P - 1, dst_run - 1:dst_run],
                         allow_slow_non_contiguous=True).then_inc(dst_loaded, 16)
            sp.wait_ge(src_zero, 1)
            whole = N_EDGES // CHUNK
            sp.dma_start(S.src_all[:, 0:whole * LANES].rearrange("p (k j) -> p k j", j=LANES),
                         D.src[0:whole * CHUNK].rearrange("(k p j) -> p k j", p=P, j=LANES)).then_inc(src_loaded, 16)
            rest = (N_EDGES - whole * CHUNK) // LANES
            sp.dma_start(S.src_all[0:rest, whole * LANES:(whole + 1) * LANES],
                         D.src[whole * CHUNK:N_EDGES].rearrange("(p j) -> p j", j=LANES)).then_inc(src_loaded, 16)
            sp.wait_ge(keep_made, 1)
            sp.dma_start(D.keep[0:N_EDGES].rearrange("(p i) -> p i", p=P), keep[:]).then_inc(flags_stored, 16)
            sp.wait_ge(neg_made, 1)
            sp.dma_start(D.neg[0:N_EDGES].rearrange("(p i) -> p i", p=P), neg[:]).then_inc(flags_stored, 16)
            pad = (E_PAD - N_EDGES) // P
            sp.dma_start(D.keep[N_EDGES:E_PAD].rearrange("(p i) -> p i", p=P), zero_bf[:, 0:pad]).then_inc(flags_stored, 16)
            sp.dma_start(D.neg[N_EDGES:E_PAD].rearrange("(p i) -> p i", p=P), zero_bf[:, 0:pad]).then_inc(flags_stored, 16)
            sp.wait_ge(table_copied, 32)
            sp.wait_ge(src_loaded, 32)
            sp.wait_ge(flags_stored, 64)

        @block.scalar
        def _(act):
            act.wait_ge(zeroed, 1)
            act.dma_start(D.slot_flags[:].rearrange("(p i) o -> p (i o)", p=P),
                          zeros[:, 0:(SLOTS + P) // P].bitcast(i32)).then_inc(flags_zero, 16)
            per = P * 7168 // FEAT
            for r in range(E_PAD // per):
                act.dma_start(D.inject[r * per:(r + 1) * per, :].rearrange("(p i) f -> p (i f)", p=P),
                              zeros[:]).then_inc(inject_zero, 16)
            act.wait_ge(inject_zero, 16 * (E_PAD // per))
            for s in range(COUNTED_PAIRS, SLOTS // PAIR):
                act.dma_start(D.matrix[s].rearrange("q p x -> p q x"),
                              zeros[:].bitcast(u8)[:, 0:NH * PAIR].rearrange("p (q x) -> p q x", q=N_PARTS)).then_inc(rest_zero, 16)
            act.wait_ge(rest_zero, 16 * (SLOTS // PAIR - COUNTED_PAIRS))

        @block.gpsimd
        def _(pool):
            pg = nc.gpsimd
            pg.iota(S.ramp_hi[:], pattern=[[1, NH]], base=1, channel_multiplier=0,
                    allow_small_or_imprecise_dtypes=True)
            pg.iota(S.ramp_lo[:], pattern=[[1, P]], base=0, channel_multiplier=0,
                    allow_small_or_imprecise_dtypes=True)
            pg.iota(S.slot_id[:], pattern=[[P, SLOT_COLS]], base=0, channel_multiplier=1,
                    allow_small_or_imprecise_dtypes=True)
            pg.iota(S.node_id[:], pattern=[[P, NH]], base=0, channel_multiplier=1,
                    allow_small_or_imprecise_dtypes=True)
            pg.iota(theta_t[:], pattern=[[P, 25]], base=1, channel_multiplier=1)
            pg.memset(ones_i[:], 1)
            pg.memset(S.ident[:], 1.0)
            pg.memset(S.before[:], 1.0)
            pg.memset(S.group_pick[:], 0.0)
            pg.memset(S.part_sum[:], 0.0).then_inc(made, 1)
            pool.wait_ge(made, 1)
            pg.affine_select(out=S.ident[:], in_=S.ident[:], compare_op=ALU.is_equal, fill=0.0,
                             base=0, pattern=[[-1, P]], channel_multiplier=1)
            pg.affine_select(out=S.before[:], in_=S.before[:], compare_op=ALU.is_gt, fill=0.0,
                             base=0, pattern=[[1, P]], channel_multiplier=-1)
            pg.affine_select(out=S.group_pick[:], in_=S.group_pick[:], compare_op=ALU.not_equal, fill=1.0,
                             base=0, pattern=[[-FEAT, GROUPS]], channel_multiplier=1).then_inc(made, 1)
            for part in range(3):
                pool.wait_ge(made, 2 + part)
                pg.affine_select(out=S.part_sum[:], in_=S.part_sum[:], compare_op=ALU.not_equal, fill=1.0,
                                 base=-FEAT * part, pattern=[[-1, FEAT]], channel_multiplier=1).then_inc(made, 1)
            pool.wait_ge(heads_loaded, 32)
            full = tile_head_cols - 1
            last = TILES - 1 - full * P
            pg.tensor_tensor(theta[:, 0:full], theta[:, 0:full], theta_t[:, 0:full], ALU.add)
            pg.tensor_tensor(theta[0:last, full:], theta[0:last, full:], theta_t[0:last, full:], ALU.add).then_inc(heads_added, 1)
            pool.wait_ge(heads_added, 1)
            pool.wait_ge(flags_zero, 16)
            for r in range(tile_head_cols):
                n = P if r < full else last
                pg.indirect_dma_start(out=D.slot_flags[:], out_offset=rows_of(theta[0:n, r:r + 1]),
                                      in_=ones_i[0:n, :], in_offset=None).then_inc(flags_set, 16)
            pool.wait_ge(flags_set, 16 * tile_head_cols)

        @block.vector
        def _(dve):
            nc.vector.memset(zeros[:], 0.0)
            nc.vector.memset(zero_bf[:], 0.0).then_inc(zeroed, 1)
            nc.vector.memset(dst_sb[:, 0:1], -1).then_inc(dst_edge, 1)
            nc.vector.memset(S.src_all[:], 0).then_inc(src_zero, 1)
            dve.wait_ge(dst_loaded, 32)
            nc.vector.tensor_tensor(keep[:], dst_sb[:, 1:dst_run + 1], dst_sb[:, 0:dst_run],
                                    ALU.is_equal).then_inc(keep_made, 1)
            dve.wait_ge(keep_made, 1)
            nc.vector.tensor_scalar(neg[:], keep[:], 1.0, -NEG, ALU.subtract, ALU.mult).then_inc(neg_made, 1)
            dve.wait_ge(made, 2)
            nc.vector.tensor_copy(S.ident_bf[:], S.ident[:])


def prepare_nodes(nc, sb, sem, pb, D, S):
    STEP = 7
    w_nat = sb("w_nat", [FEAT, 2, FEAT], f32)
    a_col = sb("a_col", [FEAT, 1], f32)
    a_neg = sb("a_neg", [FEAT, FEAT], f32)
    w_all = sb("w_all", [FEAT + 1, 3, FEAT], f32)
    x_step = sb("x_step", [P, STEP, FEAT], f32)
    xt = sb("xt", [FEAT + 1, STEP * P], f32)
    table = sb("table", [P, NH, 2 * FEAT], f32)
    p_w = pb("p_w", [FEAT, 3, FEAT], f32)
    p_xt = pb("p_xt", [FEAT, 1024], f32)
    p_lin = pb("p_lin", [P, 2, 512], f32)

    pad_zero = sem("nodes_pad_zeroed")
    x_loaded = sem("nodes_x_loaded")
    w_loaded = sem("nodes_w_loaded")
    a_made = sem("nodes_a_negated")
    w_turned = sem("nodes_w_turned")
    w_made = sem("nodes_w_made")
    x_staged = sem("nodes_x_staged")
    x_turned = sem("nodes_x_turned")
    xt_made = sem("nodes_xt_made")
    multiplied = sem("nodes_multiplied")
    emptied = sem("nodes_emptied")
    stored = sem("nodes_table_stored")
    full = N_NODES // P

    with nc.Block() as block:
        @block.sync
        def _(sp):
            sp.wait_ge(pad_zero, 1)
            sp.dma_start(S.x[:, 0:full, :], D.x[0:full * P, :].rearrange("(h p) f -> p h f", p=P)).then_inc(x_loaded, 16)
            sp.dma_start(S.x[0:N_NODES - full * P, full, :], D.x[full * P:N_NODES, :]).then_inc(x_loaded, 16)
            sp.dma_start(w_nat[:, 0, :], D.w2_W[:, :]).then_inc(w_loaded, 16)
            sp.dma_start(w_nat[:, 1, :], D.w1_W[:, :]).then_inc(w_loaded, 16)
            sp.dma_start(a_col[:], D.a[:, :].rearrange("o k -> k o"), allow_slow_non_contiguous=True).then_inc(w_loaded, 16)
            sp.dma_start(w_all[FEAT:FEAT + 1, 0, :], D.w2_b[:].unsqueeze(0)).then_inc(w_loaded, 16)
            sp.dma_start(w_all[FEAT:FEAT + 1, 2, :], D.w1_b[:].unsqueeze(0)).then_inc(w_loaded, 16)
            sp.wait_ge(emptied, 4 * (NH // STEP))
            sp.dma_start(D.table0[:, :].rearrange("(h p) f -> p h f", p=P), table[:]).then_inc(stored, 16)
            sp.wait_ge(stored, 16)

        @block.vector
        def _(dve):
            nc.vector.memset(S.x[:, full, :], 0.0).then_inc(pad_zero, 1)
            nc.vector.memset(xt[FEAT:FEAT + 1, :], 1.0)
            nc.vector.memset(w_all[FEAT:FEAT + 1, 1, :], 0.0)
            dve.wait_ge(w_loaded, 80)
            nc.vector.tensor_scalar(a_neg[:], a_col[:].to_broadcast([FEAT, FEAT]), -1.0, None, ALU.mult).then_inc(a_made, 1)
            dve.wait_ge(w_turned, 1)
            nc.vector.tensor_copy(w_all[0:FEAT], p_w[:]).then_inc(w_made, 1)
            dve.wait_ge(x_loaded, 32)
            with dve.Fori(0, NH // STEP) as i:
                dve.wait_ge(x_turned, i)
                nc.vector.tensor_copy(x_step[:], S.x[:, bass.ds(i * STEP, STEP), :]).then_inc(x_staged, 1)
                dve.wait_ge(x_turned, i + 1)
                dve.wait_ge(multiplied, i)
                nc.vector.tensor_copy(xt[0:FEAT, :], p_xt[:, 0:STEP * P]).then_inc(xt_made, 1)
                dve.wait_ge(multiplied, i + 1)
                for bank, n in ((0, 4), (1, 3)):
                    lin = p_lin[:, bank, 0:n * 96].rearrange("p (j c) -> p j c", c=96)
                    at = bass.ds(i * STEP + 4 * bank, n)
                    nc.vector.tensor_copy(table[:, at, :], lin[:, :, 0:2 * FEAT]).then_inc(emptied, 1)
                    nc.vector.tensor_tensor(S.base[:, at, :], x_step[:, 4 * bank:4 * bank + n, :],
                                            lin[:, :, 2 * FEAT:3 * FEAT], ALU.add).then_inc(emptied, 1)
                dve.wait_ge(emptied, 4 * i + 4)

        @block.tensor
        def _(pe):
            pe.wait_ge(w_loaded, 80)
            pe.wait_ge(a_made, 1)
            nc.tensor.transpose(p_w[:, 0, :], w_nat[:, 0, :], S.ident[0:FEAT, 0:FEAT])
            nc.tensor.matmul(p_w[:, 1, :], w_nat[:, 0, :], a_neg[:], start=True, stop=True)
            nc.tensor.transpose(p_w[:, 2, :], w_nat[:, 1, :], S.ident[0:FEAT, 0:FEAT]).then_inc(w_turned, 1)
            with pe.Fori(0, NH // STEP) as i:
                pe.wait_ge(xt_made, i)
                pe.wait_ge(x_staged, i + 1)
                for j in range(STEP):
                    last = nc.tensor.transpose(p_xt[:, j * P:(j + 1) * P], x_step[:, j, :], S.ident[:])
                last.then_inc(x_turned, 1)
                pe.wait_ge(emptied, 4 * i)
                pe.wait_ge(w_made, 1)
                pe.wait_ge(xt_made, i + 1)
                for j in range(STEP):
                    last = nc.tensor.matmul(p_lin[:, j // 4, 96 * (j % 4):96 * (j % 4) + 96],
                                            xt[:, j * P:(j + 1) * P], w_all[:].rearrange("k b f -> k (b f)"),
                                            start=True, stop=True)
                last.then_inc(multiplied, 1)


def prepare_slots(nc, sb, sem, pb, D, S):
    C, B = SLOT_COLS, SLOT_BATCH
    flags = sb("flags", [C, 2, P], i32)
    flags_f = sb("flags_f", [C, 2, P], f32)
    ones = sb("ones", [C, P], f32)
    run = sb("run", [C, P], f32)
    whole = sb("whole", [C, P], f32)
    tile_of = sb("tile_of", [P, C], f32)
    going = sb("going", [P, C], f32)
    node_of = sb("node_of", [P, C], f32)
    tile_idx = sb("tile_idx", [P, C], i32)
    idx_ring = sb("idx_ring", [P, B], i32)
    edges = sb("edges", [P, B, 2 * P], i32)
    match = sb("match", [P, B, P], bf16)
    hi = sb("hi", [P, B, P], i32)
    key_hi = sb("key_hi", [P, B, P], bf16)
    key_lo = sb("key_lo", [P, B, P], bf16)
    count = sb("count", [P, C], f32)
    info = sb("info_sb", [P, C, 2], i32)
    info_idx = sb("info_idx", [P, C], i32)
    info_f = sb("info_f", [P, C], f32)
    info_ring = sb("info_ring", [P, B, 2], i32)
    first_row = sb("first_row", [1, 2], i32)
    p_a = pb("p_a", [P, 512], f32)
    p_keys = pb("p_keys", [P, 4, 1024], bf16)

    flags_loaded = sem("slots_flags_loaded")
    v = sem("slots_vector_step")
    summed = sem("slots_carry_summed")
    turned = sem("slots_turned")
    ring_ready = sem("slots_index_ready")
    gathered = sem("slots_edges_gathered")
    keys_made = sem("slots_keys_made")
    keys_turned = sem("slots_keys_turned")
    keys_kept = sem("slots_keys_kept")
    scat_ready = sem("slots_info_ready")
    scattered = sem("slots_info_scattered")
    row_made = sem("slots_first_row_made")
    row_stored = sem("slots_first_row_stored")
    steps = [0]

    def link(ins):
        steps[0] += 1
        ins.then_inc(v, 1)
        nc.vector.wait_ge(v, steps[0])
        return steps[0]

    marks = {}

    with nc.Block() as block:
        @block.vector
        def _(dve):
            nc.vector.memset(ones[:], 1.0)
            nc.vector.memset(first_row[:], 0).then_inc(row_made, 1)
            nc.vector.memset(S.key_hi[:, SLOTS:], 0.0)
            nc.vector.memset(S.key_lo[:, SLOTS:], 0.0)
            dve.wait_ge(flags_loaded, 32)
            link(nc.vector.tensor_copy(flags_f[:], flags[:]))
            link(nc.vector.tensor_tensor_scan(out=run[:], data0=ones[:], data1=flags_f[:, 0, :], initial=0.0,
                                              op0=ALU.mult, op1=ALU.add))
            dve.wait_ge(summed, 1)
            link(nc.vector.tensor_scalar(whole[:], run[:], p_a[0:C, 0:1], None, ALU.add))
            dve.wait_ge(turned, 1)
            link(nc.vector.tensor_copy(tile_of[:], p_a[:, 128:128 + C]))
            link(nc.vector.tensor_copy(going[:], p_a[:, 256:256 + C]))
            link(nc.vector.tensor_tensor(node_of[:], S.slot_id[:], tile_of[:], ALU.subtract))
            link(nc.vector.tensor_copy(tile_idx[:], tile_of[:]))
            base = steps[0]
            with dve.Fori(0, N_BATCHES) as i:
                at = bass.ds(i * B, B)
                dve.wait_ge(gathered, i * 16 * B)
                nc.vector.tensor_copy(idx_ring[:], tile_idx[:, at]).then_inc(ring_ready, 1)
                dve.wait_ge(gathered, (i + 1) * 16 * B)
                dve.wait_ge(keys_turned, 2 * i)
                nc.vector.tensor_tensor(match[:], edges[:, :, P:2 * P],
                                        node_of[:, at].unsqueeze(2).to_broadcast([P, B, P]), ALU.is_equal)
                nc.vector.tensor_scalar(hi[:], edges[:, :, 0:P], 7, None,
                                        ALU.logical_shift_right).then_inc(v, 1)
                dve.wait_ge(v, base + 3 * i + 1)
                nc.vector.tensor_reduce(count[:, at], match[:], AX.X, ALU.add)
                nc.vector.scalar_tensor_tensor(key_hi[:], hi[:], 1.0, match[:], ALU.add, ALU.mult).then_inc(v, 1)
                dve.wait_ge(v, base + 3 * i + 2)
                nc.vector.tensor_scalar(hi[:], edges[:, :, 0:P], 127, None, ALU.bitwise_and).then_inc(v, 1)
                dve.wait_ge(v, base + 3 * i + 3)
                nc.vector.tensor_copy(key_lo[:], hi[:]).then_inc(keys_made, 1)
                dve.wait_ge(keys_made, i + 1)
            steps[0] = base + 3 * N_BATCHES
            link(nc.vector.tensor_copy(tile_of[:], count[:]))
            marks["count"] = steps[0]
            dve.wait_ge(turned, 2)
            link(nc.vector.tensor_tensor_scan(out=run[:], data0=ones[:], data1=p_a[0:C, 0:P], initial=0.0,
                                              op0=ALU.mult, op1=ALU.add))
            marks["run2"] = steps[0]
            dve.wait_ge(summed, 2)
            link(nc.vector.tensor_scalar(whole[:], run[:], p_a[0:C, 128:129], None, ALU.add))
            marks["whole2"] = steps[0]
            dve.wait_ge(turned, 3)
            link(nc.vector.tensor_copy(info[:, :, 1], p_a[:, 256:256 + C]))
            link(nc.vector.tensor_copy(info[:, :, 0], S.slot_id[:]))
            link(nc.vector.tensor_tensor(info_f[:], S.slot_id[:], node_of[:], ALU.subtract))
            link(nc.vector.tensor_scalar(info_f[:], info_f[:], float(INFO_SPARE - 1), None, ALU.add))
            link(nc.vector.tensor_tensor(info_f[:], info_f[:], going[:], ALU.mult))
            link(nc.vector.tensor_tensor(info_f[:], info_f[:], node_of[:], ALU.add))
            link(nc.vector.tensor_scalar(info_f[:], info_f[:], 1.0, None, ALU.add))
            link(nc.vector.tensor_copy(info_idx[:], info_f[:]))
            with dve.Fori(0, N_BATCHES) as i:
                at = bass.ds(i * B, B)
                dve.wait_ge(scattered, i * 16 * B)
                nc.vector.tensor_copy(idx_ring[:], info_idx[:, at])
                nc.vector.tensor_copy(info_ring[:], info[:, at, :]).then_inc(scat_ready, 1)

        @block.tensor
        def _(pe):
            pe.wait_ge(v, 2)
            nc.tensor.matmul(p_a[0:C, 0:1], S.before[0:C, 0:C], run[:, P - 1:P], start=True, stop=True).then_inc(summed, 1)
            pe.wait_ge(v, 3)
            nc.tensor.transpose(p_a[:, 128:128 + C], whole[:], S.ident[0:C, 0:C])
            nc.tensor.transpose(p_a[:, 256:256 + C], flags_f[:, 1, :], S.ident[0:C, 0:C]).then_inc(turned, 1)
            with pe.Fori(0, N_BATCHES) as i:
                for n, key in enumerate((key_hi, key_lo)):
                    pe.wait_ge(keys_kept, 2 * i + n)
                    pe.wait_ge(keys_made, i + 1)
                    for j in range(B):
                        last = nc.tensor.transpose(p_keys[:, j // 8, (j % 8) * P:(j % 8) * P + P],
                                                   key[:, j, :], S.ident_bf[:])
                    last.then_inc(keys_turned, 1)
            pe.wait_ge(v, marks["count"])
            nc.tensor.transpose(p_a[0:C, 0:P], count[:], S.ident[:]).then_inc(turned, 1)
            pe.wait_ge(v, marks["run2"])
            nc.tensor.matmul(p_a[0:C, 128:129], S.before[0:C, 0:C], run[:, P - 1:P], start=True, stop=True).then_inc(summed, 1)
            pe.wait_ge(v, marks["whole2"])
            nc.tensor.transpose(p_a[:, 256:256 + C], whole[:], S.ident[0:C, 0:C]).then_inc(turned, 1)

        @block.scalar
        def _(act):
            with act.Fori(0, N_BATCHES) as i:
                for n, key in enumerate((S.key_hi, S.key_lo)):
                    act.wait_ge(keys_turned, 2 * i + n + 1)
                    nc.scalar.copy(key[:, bass.ds(i * B * P, B * P)],
                                   p_keys[:].rearrange("p b e -> p (b e)")[:, 0:B * P]).then_inc(keys_kept, 1)

        @block.sync
        def _(sp):
            slot_rows = D.slot_flags[:].rearrange("v o -> (v o)")
            sp.dma_start(flags[:, 0, :], slot_rows[0:SLOTS].rearrange("(c p) -> c p", p=P)).then_inc(flags_loaded, 16)
            sp.dma_start(flags[:, 1, :], slot_rows[1:SLOTS + 1].rearrange("(c p) -> c p", p=P)).then_inc(flags_loaded, 16)
            sp.wait_ge(row_made, 1)
            sp.dma_start(D.info[0:1, :], first_row[:]).then_inc(row_stored, 16)
            sp.wait_ge(row_stored, 16)

        @block.gpsimd
        def _(pool):
            with pool.Fori(1, N_BATCHES + 1) as batch:
                pool.wait_ge(flags_loaded, 32)
                pool.wait_ge(ring_ready, batch)
                for j in range(B):
                    nc.gpsimd.indirect_dma_start(out=edges[:, j, :], out_offset=None, in_=D.edge_table[:, :],
                                                 in_offset=rows_of(idx_ring[:, j:j + 1])).then_inc(gathered, 16)
            with pool.Fori(1, N_BATCHES + 1) as batch:
                pool.wait_ge(flags_loaded, 32)
                pool.wait_ge(scat_ready, batch)
                for j in range(B):
                    nc.gpsimd.indirect_dma_start(out=D.info[:, :], out_offset=rows_of(idx_ring[:, j:j + 1]),
                                                 in_=info_ring[:, j, :], in_offset=None).then_inc(scattered, 16)
            pool.wait_ge(scattered, 16 * C)


def prepare_ends(nc, sb, sem, pb, D, S):
    own = sb("own", [P, NH, 2], i32)
    prev = sb("prev", [P, NH, 2], i32)
    end = sb("end", [P, NH], f32)
    begin = sb("begin", [P, NH], f32)
    deg = sb("deg", [P, NH], f32)
    tmp = sb("tmp", [P, NH], f32)

    loaded = sem("ends_info_loaded")
    v = sem("ends_vector_step")
    rooted = sem("ends_root_taken")
    steps = [0]

    def link(ins):
        steps[0] += 1
        ins.then_inc(v, 1)
        nc.vector.wait_ge(v, steps[0])
        return steps[0]

    with nc.Block() as block:
        @block.sync
        def _(sp):
            with nc.allow_non_contiguous_dma(reason="one row of two numbers per node, once"):
                sp.dma_start(own[:], D.info[1:1 + N_PAD, :].rearrange("(h p) c -> p h c", p=P)).then_inc(loaded, 16)
                sp.dma_start(prev[:], D.info[0:N_PAD, :].rearrange("(h p) c -> p h c", p=P)).then_inc(loaded, 16)

        @block.vector
        def _(dve):
            dve.wait_ge(loaded, 32)
            link(nc.vector.tensor_copy(S.last_slot[:], own[:, :, 0]))
            link(nc.vector.tensor_copy(end[:], own[:, :, 1]))
            link(nc.vector.tensor_copy(begin[:], prev[:, :, 1]))
            link(nc.vector.tensor_tensor(deg[:], end[:], begin[:], ALU.subtract))
            link(nc.vector.tensor_scalar(S.has_edges[:], deg[:], 0.0, None, ALU.is_gt))
            link(nc.vector.tensor_scalar(tmp[:], end[:], -1.0, 0.0, ALU.add, ALU.max))
            link(nc.vector.tensor_copy(S.last_edge[:], tmp[:]))
            link(nc.vector.tensor_scalar(tmp[:], S.node_id[:], float(E_PAD), None, ALU.add))
            link(nc.vector.tensor_tensor(begin[:], begin[:], tmp[:], ALU.subtract))
            link(nc.vector.tensor_tensor(begin[:], begin[:], S.has_edges[:], ALU.mult))
            link(nc.vector.tensor_tensor(begin[:], begin[:], tmp[:], ALU.add))
            link(nc.vector.tensor_copy(S.first_edge[:], begin[:]))
            ready = link(nc.vector.tensor_scalar(tmp[:], deg[:], 1.0, None, ALU.max))
            link(nc.vector.reciprocal(S.mean_scale[:], tmp[:]))
            dve.wait_ge(rooted, 1)
            link(nc.vector.reciprocal(deg[:], end[:]))
            link(nc.vector.tensor_tensor(S.norm_scale[:], deg[:], S.has_edges[:], ALU.mult))
            nc.vector.memset(S.one_scale[:], 1.0).then_inc(S.tables_done, 1)
            S.root_at = ready

        @block.scalar
        def _(act):
            act.wait_ge(v, S.root_at)
            nc.scalar.activation(end[:], tmp[:], ACT.Sqrt).then_inc(rooted, 1)


def attend_and_count(nc, sb, sem, pb, D, S):
    EACH = GROUPS * LANES
    QUARTERS, SLOTS_Q = 4, SUB // 4
    ring = sb("ring", [P, 2, GROUPS, LANES], i32)
    rows = sb("rows", [P, 2, GROUPS, LANES, 2 * FEAT], f32)
    pack = sb("pack", [P, 2, LANES, 2, GROUPS, FEAT], f32)
    neg = sb("neg0", [P, 2, CHUNK], bf16)
    peak = sb("peak", [P, 2, CHUNK + 1], f32)
    args = sb("args", [P, 2, 2, CHUNK], f32)
    weight = sb("weight", [P, 2, 2, CHUNK], f32)
    value = sb("value", [P, CHUNK], f32)
    num = sb("num", [P, 2, CHUNK], f32)
    den = sb("den", [P, 2, CHUNK], f32)
    out = sb("out", [P, 2, GROUPS, LANES, Y0_ROW], f32)
    key2_hi = sb("key2_hi", [P, 2, SUB, 2], bf16)
    key2_lo = sb("key2_lo", [P, 2, SUB, 2], bf16)
    hot_hi = sb("hot_hi", [P, 2, SUB, NH], bf16)
    hot_lo = sb("hot_lo", [P, 2, SUB, P], bf16)
    stage = sb("stage", [P, STAGES, NH, PAIR], u8)
    p_val = pb("p_val", [P, CHUNK], f32)
    p_score = pb("p_score", [P, CHUNK], f32)
    p_num = pb("p_num", [P, LANES, P], f32)
    p_stat = pb("p_stat", [P, 2, LANES, GROUPS], f32)
    counts = pb("counts", [P, 2, 2, 512], f32)

    first_listed = sem("attend_first_sources_listed")
    listed = [sem(f"attend_sources{u}_listed") for u in range(2)]
    gathered = [sem(f"attend_rows{u}_gathered") for u in range(2)]
    packed = [sem(f"attend_rows{u}_packed") for u in range(2)]
    flagged = [sem(f"attend_flags{u}_loaded") for u in range(2)]
    turned = [sem(f"attend_rows{u}_turned") for u in range(2)]
    begun = sem("attend_first_states_made")
    v = sem("attend_vector_step")
    exponents = sem("attend_exponents_made")
    weighed = sem("attend_weighed")
    used = [sem(f"attend_rows{u}_used") for u in range(2)]
    scanned = sem("attend_scanned")
    back = [sem(f"attend_sums{u}_turned_back") for u in range(2)]
    emptied = sem("attend_emptied")
    out_stored = [sem(f"attend_out{u}_stored") for u in range(2)]
    paired = sem("matrix_keys_paired")
    hot = sem("matrix_one_hots_made")
    counted = [sem(f"matrix_sub{u}_quarters_counted") for u in range(2)]
    staged = [sem(f"matrix_half{u}_staged") for u in range(2)]
    pair_stored = [sem(f"matrix_stage{w}_stored") for w in range(STAGES)]
    V = 3
    TURNS = GROUP_CHUNKS // ATTEND_STEPS
    SHARE = [range(t * COUNT_SUBS // ATTEND_STEPS, (t + 1) * COUNT_SUBS // ATTEND_STEPS) for t in range(ATTEND_STEPS)]
    PAIRS = COUNT_SUBS // 2
    pairs_on = [len(range(w, PAIRS, STAGES)) for w in range(STAGES)]

    def step_of(i, t):
        return i * ATTEND_STEPS + t, t % 2, i * (ATTEND_STEPS // 2) + t // 2

    def sub_of(i, m):
        return i * COUNT_SUBS + m, m % 2, i * (COUNT_SUBS // 2) + m // 2

    def after(i, t):
        return (i, t + 1) if t + 1 < ATTEND_STEPS else (i + 1, 0)

    def over_steps(eng, one):
        with eng.Fori(0, TURNS - 1) as i:
            for t in range(ATTEND_STEPS):
                one(i, t, False)
        for t in range(ATTEND_STEPS):
            one(TURNS - 1, t, t + 1 == ATTEND_STEPS)

    with nc.Block() as block:
        @block.gpsimd
        def _(pool):
            with pool.Fori(0, TURNS) as i:
                for t in range(ATTEND_STEPS):
                    _, u, n = step_of(i, t)
                    before = pool.snap(pool.to_reg(n))
                    pool.wait_ge(first_listed, 2)
                    pool.wait_ge(packed[u], before)
                    pool.wait_ge(listed[u], before)
                    for g in range(GROUPS):
                        for j in range(LANES):
                            nc.gpsimd.indirect_dma_start(out=rows[:, u, g, j, :], out_offset=None, in_=D.table0[:, :],
                                                         in_offset=rows_of(ring[:, u, g, j:j + 1])).then_inc(gathered[u], 16)

        @block.tensor
        def _(pe):
            def turn(i, t):
                c, u, n = step_of(i, t)
                pe.wait_ge(used[1 - u], n + u)
                pe.wait_ge(packed[u], n + 1)
                for j in range(LANES):
                    for p_out, w in ((p_val, 0), (p_score, 1)):
                        last = nc.tensor.transpose(p_out[:, j::LANES], pack[:, u, j, w].rearrange("p g f -> p (g f)"), S.ident[:])
                last.then_inc(turned[u], 1)

            def turn_back(i, t):
                c, u, n = step_of(i, t)
                pe.wait_ge(emptied, c * 2)
                pe.wait_ge(scanned, c * 2 + 2)
                for j in range(LANES):
                    nc.tensor.transpose(p_num[:, j, :], num[:, u, j::LANES], S.ident[:])
                for j in range(LANES):
                    nc.tensor.matmul(p_stat[:, 0, j, :], den[:, u, j::LANES], S.group_pick[:], start=True, stop=True)
                    last = nc.tensor.matmul(p_stat[:, 1, j, :], peak[:, u, 1 + j::LANES], S.group_pick[:], start=True, stop=True)
                last.then_inc(back[u], 1)

            def count(i, m):
                s, u, n = sub_of(i, m)
                pe.wait_ge(hot, s * 2 + 2)
                for r in range(QUARTERS):
                    pe.wait_ge(staged[r % 2], s * 2 + r // 2)
                    for k in range(SLOTS_Q):
                        slot = r * SLOTS_Q + k
                        last = nc.tensor.matmul(counts[:, r % 2, k // 4, NH * (k % 4):NH * (k % 4) + NH],
                                                hot_lo[:, u, slot, :], hot_hi[:, u, slot, :], start=True, stop=True)
                    last.then_inc(counted[u], 1)

            def one(i, t, is_last):
                for m in SHARE[t]:
                    count(i, m)
                if not is_last:
                    turn(*after(i, t))
                turn_back(i, t)

            turn(0, 0)
            over_steps(pe, one)

        @block.vector
        def _(dve):
            nc.vector.memset(peak[:, 0, 0:1], NEG)
            nc.vector.memset(num[:, 1, CHUNK - 1:CHUNK], 0.0)
            nc.vector.memset(den[:, 1, CHUNK - 1:CHUNK], 0.0).then_inc(begun, 1)
            dve.wait_ge(begun, 1)

            def compare(i, m):
                s, u, n = sub_of(i, m)
                dve.wait_ge(paired, s * 2 + 2)
                dve.wait_ge(counted[u], n * QUARTERS)
                for hots, ramp, two, width in ((hot_hi, S.ramp_hi, key2_hi, NH), (hot_lo, S.ramp_lo, key2_lo, P)):
                    nc.vector.tensor_tensor(
                        hots[:, u].rearrange("p v (h t) -> p v h t", t=2),
                        ramp[:].rearrange("p (h t) -> p h t", t=2).unsqueeze(1).to_broadcast([P, SUB, width // 2, 2]),
                        two[:, u].unsqueeze(2).to_broadcast([P, SUB, width // 2, 2]), ALU.is_equal).then_inc(hot, 1)

            def scan_scores(i, t):
                c, u, n = step_of(i, t)
                dve.wait_ge(v, c * V)
                dve.wait_ge(back[u], n)
                dve.wait_ge(flagged[u], n * 64 + 64)
                dve.wait_ge(turned[u], n + 1)
                nc.vector.tensor_tensor_scan(out=peak[:, u, 1:], data0=neg[:, u], data1=p_score[:],
                                             initial=peak[:, u, 0:1], op0=ALU.add, op1=ALU.max).then_inc(v, 1)
                dve.wait_ge(v, c * V + 1)
                nc.vector.tensor_tensor(args[:, u, 0], peak[:, u, 0:CHUNK], neg[:, u], ALU.add).then_inc(v, 1)
                nc.vector.tensor_tensor(args[:, u, 1], p_score[:], peak[:, u, 1:], ALU.subtract)
                dve.wait_ge(v, c * V + 2)
                nc.vector.tensor_tensor(args[:, u, 0], args[:, u, 0], peak[:, u, 1:], ALU.subtract).then_inc(exponents, 1)
                nc.vector.tensor_copy(peak[:, 1 - u, 0:1], peak[:, u, CHUNK:]).then_inc(v, 1)

            def scan_sums(i, t):
                c, u, n = step_of(i, t)
                dve.wait_ge(scanned, c * 2)
                dve.wait_ge(weighed, c + 1)
                nc.vector.tensor_tensor(value[:], weight[:, u, 1], p_val[:], ALU.mult).then_inc(used[u], 1)
                nc.vector.tensor_tensor_scan(out=den[:, u], data0=weight[:, u, 0], data1=weight[:, u, 1],
                                             initial=den[:, 1 - u, CHUNK - 1:], op0=ALU.mult, op1=ALU.add).then_inc(scanned, 1)
                dve.wait_ge(used[u], n + 1)
                nc.vector.tensor_tensor_scan(out=num[:, u], data0=weight[:, u, 0], data1=value[:],
                                             initial=num[:, 1 - u, CHUNK - 1:], op0=ALU.mult, op1=ALU.add).then_inc(scanned, 1)

            def one(i, t, is_last):
                for m in SHARE[t][:-1]:
                    compare(i, m)
                scan_scores(i, t)
                compare(i, SHARE[t][-1])
                scan_sums(i, t)

            over_steps(dve, one)

        @block.scalar
        def _(act):
            src_of = S.src_all[:, 0:E_PAD // P].rearrange("p (g c j) -> p g c j", g=GROUPS, j=LANES)
            src_after = S.src_all[:, 2 * LANES:2 * LANES + E_PAD // P].rearrange("p (g c j) -> p g c j", g=GROUPS, j=LANES)

            def pair_keys(first, u):
                for two, key in ((key2_hi, S.key_hi), (key2_lo, S.key_lo)):
                    nc.scalar.copy(two[:, u], key[:, bass.ds(first, SUB)].unsqueeze(2).to_broadcast([P, SUB, 2])).then_inc(paired, 1)

            def load_flags(i, t):
                c, u, n = step_of(i, t)
                act.wait_ge(used[u], n)
                for g in range(GROUPS):
                    first = c * CHUNK + g * GROUP_EDGES
                    act.dma_start(neg[FEAT * g:FEAT * (g + 1), u],
                                  D.neg[bass.ds(first, CHUNK)].unsqueeze(0).to_broadcast([FEAT, CHUNK])).then_inc(flagged[u], 16)

            def pack_rows(i, t):
                c, u, n = step_of(i, t)
                act.wait_ge(turned[u], n)
                act.wait_ge(gathered[u], n * (16 * EACH) + 16 * EACH)
                for w in range(2):
                    last = nc.scalar.copy(pack[:, u, :, w].rearrange("p j g f -> p g j f"),
                                          rows[:, u, :, :, FEAT * w:FEAT * (w + 1)])
                last.then_inc(packed[u], 1)
                nc.scalar.copy(ring[:, u].unsqueeze(2), src_after[:, :, bass.ds(c, 1), :]).then_inc(listed[u], 1)

            def keep_counts(i, m):
                s, u, n = sub_of(i, m)
                act.wait_ge(hot, s * 2)
                pair_keys(s * SUB + SUB, 1 - u)
                w = m // 2 % STAGES
                act.wait_ge(pair_stored[w], (i * pairs_on[w] + m // 2 // STAGES) * 16)
                for r in range(QUARTERS):
                    act.wait_ge(counted[u], n * QUARTERS + (r + 1))
                    at = u * SUB + r * SLOTS_Q
                    nc.scalar.copy(stage[:, w, :, at:at + SLOTS_Q].rearrange("p h (b v) -> p h b v", b=2),
                                   counts[:, r % 2, :, 0:4 * NH].rearrange("p b (v h) -> p h b v", h=NH)).then_inc(staged[r % 2], 1)

            def weigh(i, t):
                c, u, n = step_of(i, t)
                act.wait_ge(exponents, c + 1)
                nc.scalar.activation(weight[:, u], args[:, u], ACT.Exp).then_inc(weighed, 1)

            def put_out(i, t):
                c, u, n = step_of(i, t)
                act.wait_ge(out_stored[u], n * 16 * GROUPS)
                act.wait_ge(back[u], n + 1)
                nc.scalar.copy(out[:, u, :, :, 0:FEAT],
                               p_num[:].rearrange("p j (g f) -> p g j f", g=GROUPS)).then_inc(emptied, 1)
                nc.scalar.copy(out[:, u, :, :, FEAT:Y0_ROW],
                               p_stat[:].rearrange("p w j g -> p g j w")).then_inc(emptied, 1)

            for u in range(2):
                nc.scalar.copy(ring[:, u], src_of[:, :, u, :]).then_inc(first_listed, 1)
            def one(i, t, is_last):
                for m in SHARE[t][:-1]:
                    keep_counts(i, m)
                weigh(i, t)
                if not is_last:
                    load_flags(*after(i, t))
                    pack_rows(*after(i, t))
                keep_counts(i, SHARE[t][-1])
                put_out(i, t)

            load_flags(0, 0)
            pack_rows(0, 0)
            pair_keys(0, 0)
            over_steps(act, one)

        @block.sync
        def _(sp):
            with sp.Fori(0, TURNS) as i:
                for t in range(ATTEND_STEPS):
                    for m in SHARE[t]:
                        if m % 2:
                            w = m // 2 % STAGES
                            for half in range(2):
                                sp.wait_ge(staged[half], (i * COUNT_SUBS + m) * 2 + 2)
                            sp.dma_start(D.matrix[bass.ds(i * PAIRS + m // 2, 1), :, :, :].rearrange("s q p x -> p (s q) x"),
                                         stage[:, w].rearrange("p (q h) v -> p q (h v)", q=N_PARTS)).then_inc(pair_stored[w], 16)
                    c, u, n = step_of(i, t)
                    sp.wait_ge(emptied, c * 2 + 2)
                    for g in range(GROUPS):
                        first = c * CHUNK + g * GROUP_EDGES
                        sp.dma_start(D.scan0[bass.ds(first, CHUNK), :].rearrange("(p j) w -> p (j w)", j=LANES),
                                     out[:, u, g].rearrange("p j w -> p (j w)")).then_inc(out_stored[u], 16)
            for w in range(STAGES):
                sp.wait_ge(pair_stored[w], 16 * pairs_on[w] * TURNS)
            for u in range(2):
                sp.wait_ge(out_stored[u], 16 * GROUPS * (GROUP_CHUNKS // 2))


def normalize(nc, dve, act_done, act_go, link, T, S, out):
    link(nc.vector.tensor_reduce(S.stat[:, 0], T[:], AX.X, ALU.add))
    link(nc.vector.tensor_scalar(S.stat[:, 0], S.stat[:, 0], 1.0 / FEAT, None, ALU.mult))
    link(nc.vector.tensor_tensor(T[:], T[:], over_features(S.stat[:, 0]), ALU.subtract))
    link(nc.vector.tensor_tensor(S.square[:], T[:], T[:], ALU.mult))
    link(nc.vector.tensor_reduce(S.stat[:, 1], S.square[:], AX.X, ALU.add))
    nc.vector.tensor_scalar(S.stat[:, 1], S.stat[:, 1], 1.0 / FEAT, EPS, ALU.mult, ALU.add).then_inc(act_go, 1)
    dve.wait_ge(act_done, 1)
    link(nc.vector.reciprocal(S.stat[:, 0], S.stat[:, 1]))
    return link(nc.vector.tensor_tensor(out[:], T[:], over_features(S.stat[:, 0]), ALU.mult))


def finish_attention(nc, sb, sem, pb, D, S):
    S.square = sb("square_finish_attention", [P, NH, FEAT], f32)
    last = sb("last", [P, NH, Y0_ROW], f32)
    cut = sb("cut", [P, GROUPS - 1, Y0_ROW], f32)
    cut_dst = sb("cut_dst", [P, GROUPS - 1, 2], i32)
    cut_dst_f = sb("cut_dst_f", [P, GROUPS - 1, 2], f32)
    top = sb("top", [P, NH], f32)
    side = sb("side", [P, GROUPS, NH], f32)
    other = sb("other", [P, NH], f32)
    total = sb("total", [P, NH], f32)
    part = sb("part", [P, NH, FEAT], f32)

    cuts = sem("finish0_cuts_loaded")
    gathered = sem("finish0_ends_gathered")
    v = sem("finish0_vector_step")
    weighed = sem("finish0_weighed")
    root_go, root_done = sem("finish0_variance_made"), sem("finish0_root_taken")
    steps, at = [0], {}

    def link(ins):
        steps[0] += 1
        ins.then_inc(v, 1)
        nc.vector.wait_ge(v, steps[0])
        return steps[0]

    with nc.Block() as block:
        @block.sync
        def _(sp):
            for g in range(GROUPS - 1):
                e = (g + 1) * GROUP_EDGES - 1
                sp.dma_start(cut[:, g, :], D.scan0[e:e + 1, :].to_broadcast([P, Y0_ROW])).then_inc(cuts, 16)
                sp.dma_start(cut_dst[:, g, :], D.dst[e:e + 2].unsqueeze(0).to_broadcast([P, 2])).then_inc(cuts, 16)

        @block.gpsimd
        def _(pool):
            for h in range(NH):
                nc.gpsimd.indirect_dma_start(out=last[:, h, :], out_offset=None, in_=D.scan0[:, :],
                                             in_offset=rows_of(S.last_edge[:, h:h + 1])).then_inc(gathered, 16)

        @block.vector
        def _(dve):
            dve.wait_ge(cuts, 32 * (GROUPS - 1))
            link(nc.vector.tensor_copy(cut_dst_f[:], cut_dst[:]))
            dve.wait_ge(gathered, 16 * NH)
            link(nc.vector.tensor_copy(top[:], last[:, :, FEAT + 1]))
            for g in range(GROUPS - 1):
                link(nc.vector.tensor_scalar(other[:], S.node_id[:], cut_dst_f[:, g, 0:1], None, ALU.is_equal))
                link(nc.vector.tensor_scalar(side[:, g], S.node_id[:], cut_dst_f[:, g, 1:2], None, ALU.is_equal))
                link(nc.vector.tensor_tensor(other[:], other[:], side[:, g], ALU.mult))
                link(nc.vector.tensor_scalar(other[:], other[:], 1.0, -NEG, ALU.subtract, ALU.mult))
                link(nc.vector.tensor_scalar(side[:, g], other[:], cut[:, g, FEAT + 1:FEAT + 2], None, ALU.add))
                link(nc.vector.tensor_tensor(top[:], top[:], side[:, g], ALU.max))
            link(nc.vector.tensor_copy(side[:, GROUPS - 1], last[:, :, FEAT + 1]))
            at["side"] = link(nc.vector.tensor_tensor(side[:], side[:], top[:].unsqueeze(1).to_broadcast([P, GROUPS, NH]), ALU.subtract))
            dve.wait_ge(weighed, 1)
            own = side[:, GROUPS - 1]
            link(nc.vector.tensor_tensor(total[:], last[:, :, FEAT], own, ALU.mult))
            link(nc.vector.tensor_tensor(S.work[:], last[:, :, 0:FEAT], over_features(own), ALU.mult))
            for g in range(GROUPS - 1):
                link(nc.vector.scalar_tensor_tensor(total[:], side[:, g], cut[:, g, FEAT:FEAT + 1], total[:], ALU.mult, ALU.add))
                link(nc.vector.tensor_tensor(part[:], over_features(side[:, g]),
                                             cut[:, g, 0:FEAT].unsqueeze(1).to_broadcast([P, NH, FEAT]), ALU.mult))
                link(nc.vector.tensor_tensor(S.work[:], S.work[:], part[:], ALU.add))
            link(nc.vector.reciprocal(other[:], total[:]))
            link(nc.vector.tensor_tensor(other[:], other[:], S.has_edges[:], ALU.mult))
            link(nc.vector.tensor_tensor(S.work[:], S.work[:], over_features(other[:]), ALU.mult))
            link(nc.vector.tensor_tensor(S.work[:], S.work[:], S.base[:], ALU.add))
            normalize(nc, dve, root_done, root_go, link, S.work, S, S.x)

        @block.scalar
        def _(act):
            act.wait_ge(v, at["side"])
            nc.scalar.activation(side[:], side[:], ACT.Exp).then_inc(weighed, 1)
            act.wait_ge(root_go, 1)
            nc.scalar.activation(S.stat[:, 1], S.stat[:, 1], ACT.Sqrt).then_inc(root_done, 1)


def propagate(nc, sb, sem, pb, D, S, name, turn, before, after):
    ROUNDS = 3
    PAIRS = BLOCK // PAIR
    split = sb("split", [P, NH, 3, FEAT], bf16)
    raw = sb("raw", [P, PLACES, PAIRS, HI_PART * PAIR], u8)
    part = sb("part", [P, PLACES, PAIRS, HI_PART * PAIR], bf16)
    scaled = S.square = sb("scaled", [P, NH, FEAT], f32)
    sums = sb("sums", [P, NH, FEAT], f32)
    keep = sb("keep", [3 * FEAT, BLOCK], i32)
    slot_sum = sb("slot_sum", [3 * FEAT, BLOCK], f32)
    carry = sb("carry", [3 * FEAT, 1], f32)
    out = sb("out", [P, LANES, FEAT], f32)
    p_dense = pb("p_dense", [3 * FEAT, 2, BLOCK], f32)
    p_out = pb("p_out", [P, LANES, FEAT], f32)

    loaded, widened, multiplied = S.place_loaded, S.place_widened, S.place_multiplied
    splitted, flagged, scanned, carried, back, emptied, stored, gathered = S.block_sems
    first = turn * ROUNDS
    v = sem(name + "_vector_step")
    root_go, root_done = sem(name + "_variance_made"), sem(name + "_root_taken")
    steps = [0]
    V = 6
    parts_on = [len(range(w, N_PARTS, PLACES)) for w in range(PLACES)]

    def place_of(n, q):
        return q % PLACES, n * parts_on[q % PLACES] + q // PLACES

    def widen(eng, copy, n, q):
        w, uses = place_of(n, q)
        eng.wait_ge(multiplied[w], uses)
        eng.wait_ge(loaded[w], uses * 16 + 16)
        copy(part[:, w], raw[:, w]).then_inc(widened[w], 1)

    def over_blocks(eng, k, block):
        block(k * N_BLOCKS, 0, 0, True)
        with eng.Fori(0, N_BLOCKS // 2) as i:
            for u in range(2):
                block(k * N_BLOCKS + i * 2 + (u + 1), i * 2 + (u + 1), 1 - u, False)

    def link(ins):
        steps[0] += 1
        ins.then_inc(v, 1)
        nc.vector.wait_ge(v, steps[0])

    with nc.Block() as block:
        @block.sync
        def _(sp):
            with sp.Fori(first, first + ROUNDS) as k:
                with sp.Fori(0, N_BLOCKS) as b:
                    for q in range(N_PARTS):
                        w, uses = place_of(k * N_BLOCKS + b, q)
                        uses = sp.snap(sp.to_reg(uses))
                        sp.wait_ge(S.tables_done, 1)
                        sp.wait_ge(widened[w], uses)
                        sp.dma_start(raw[:, w], D.matrix[bass.ds(b * PAIRS, PAIRS), q, :, :]
                                     .rearrange("s p x -> p s x")).then_inc(loaded[w], 16)

        @block.scalar
        def _(act):
            def put_out(n, b):
                act.wait_ge(stored, n * 16)
                act.wait_ge(back, n + 1)
                nc.scalar.copy(out[:], p_out[:]).then_inc(emptied, 1)
                act.wait_ge(emptied, n + 1)
                act.dma_start(D.slot_sums[bass.ds(b * BLOCK, BLOCK), :].rearrange("(p j) f -> p (j f)", j=LANES),
                              out[:].rearrange("p j f -> p (j f)")).then_inc(stored, 16)

            def one(n, b, bank, leads):
                for q in SCALAR_PARTS[:2]:
                    widen(act, nc.scalar.copy, n, q)
                act.wait_ge(scanned, n)
                act.dma_start(keep[:], D.slot_flags[bass.ds(b * BLOCK, BLOCK), :].rearrange("v o -> o v")
                              .to_broadcast([3 * FEAT, BLOCK])).then_inc(flagged, 16)
                if not leads:
                    put_out(n - 1, b - 1)
                for q in SCALAR_PARTS[2:]:
                    widen(act, nc.scalar.copy, n, q)

            with act.Fori(first, first + ROUNDS) as k:
                over_blocks(act, k, one)
                put_out(k * N_BLOCKS + (N_BLOCKS - 1), N_BLOCKS - 1)
            act.wait_ge(root_go, 1)
            nc.scalar.activation(S.stat[:, 1], S.stat[:, 1], ACT.Sqrt).then_inc(root_done, 1)

        @block.tensor
        def _(pe):
            def turn_back(n):
                pe.wait_ge(emptied, n)
                pe.wait_ge(scanned, n + 1)
                for j in range(LANES):
                    last = nc.tensor.matmul(p_out[:, j, :], slot_sum[:, j::LANES], S.part_sum[:], start=True, stop=True)
                last.then_inc(back, 1)

            def one(n, b, bank, leads):
                if not leads:
                    pe.wait_ge(scanned, n - 1)
                for q in range(N_PARTS):
                    w, uses = place_of(n, q)
                    pe.wait_ge(widened[w], uses + 1)
                    here = part[:, w].rearrange("p s (h v) -> p s h v", v=PAIR)
                    for m in range(HI_PART):
                        h = q * HI_PART + m
                        last = nc.tensor.matmul(p_dense[:, bank], split[:, h].rearrange("p c f -> p (c f)"), here[:, :, m, :],
                                                start=(h == 0), stop=(h == NH - 1))
                    last.then_inc(multiplied[w], 1)
                    if q == 0 and not leads:
                        turn_back(n - 1)

            with pe.Fori(first, first + ROUNDS) as k:
                pe.wait_ge(splitted, k + 1)
                over_blocks(pe, k, one)
                turn_back(k * N_BLOCKS + (N_BLOCKS - 1))

        @block.vector
        def _(dve):
            nc.vector.memset(carry[:], 0.0)
            link(nc.vector.tensor_scalar(S.work[:], S.x[:], 1.25, None, ALU.mult))
            link(nc.vector.tensor_tensor(scaled[:], S.x[:], over_features(before[:]), ALU.mult))
            base = steps[0]

            def one(n, b, bank, leads):
                for q in VECTOR_PARTS:
                    widen(dve, nc.vector.tensor_copy, n, q)
                w, uses = place_of(n, N_PARTS - 1)
                dve.wait_ge(flagged, n * 16 + 16)
                dve.wait_ge(carried, n)
                dve.wait_ge(back, n)
                dve.wait_ge(multiplied[w], uses + 1)
                nc.vector.tensor_tensor_scan(out=slot_sum[:], data0=keep[:], data1=p_dense[:, bank], initial=carry[:, 0:1],
                                             op0=ALU.mult, op1=ALU.add).then_inc(scanned, 1)
                dve.wait_ge(scanned, n + 1)
                nc.vector.tensor_copy(carry[:], slot_sum[:, BLOCK - 1:]).then_inc(carried, 1)

            with dve.Fori(first, first + ROUNDS) as k:
                def step(ins, nth):
                    ins.then_inc(v, 1)
                    dve.wait_ge(v, k * V + (base + nth - first * V))

                step(nc.vector.tensor_copy(split[:, :, 0, :], scaled[:]), 1)
                step(nc.vector.tensor_tensor(scaled[:], scaled[:], split[:, :, 0, :], ALU.subtract), 2)
                step(nc.vector.tensor_copy(split[:, :, 1, :], scaled[:]), 3)
                step(nc.vector.tensor_tensor(scaled[:], scaled[:], split[:, :, 1, :], ALU.subtract), 4)
                nc.vector.tensor_copy(split[:, :, 2, :], scaled[:]).then_inc(splitted, 1)
                over_blocks(dve, k, one)
                dve.wait_ge(gathered, (k + 1) * 16 * NH)
                dve.wait_ge(splitted, k + 1)
                step(nc.vector.tensor_tensor(sums[:], sums[:], over_features(after[:]), ALU.mult), 5)
                nc.vector.tensor_tensor(scaled[:], sums[:], over_features(before[:]), ALU.mult)
                step(nc.vector.scalar_tensor_tensor(S.work[:], sums[:], 0.25, S.work[:], ALU.mult, ALU.add), 6)
            steps[0] = base + ROUNDS * V
            normalize(nc, dve, root_done, root_go, link, S.work, S, S.x)

        @block.gpsimd
        def _(pool):
            ready = [min(N_BLOCKS, -(-(TILES + P * (h + 1)) // BLOCK)) for h in range(NH)]
            with pool.Fori(first, first + ROUNDS) as k:
                for blocks in sorted(set(ready)):
                    blocks_stored = pool.snap(pool.to_reg((k * N_BLOCKS + blocks) * 16))
                    pool.wait_ge(S.tables_done, 1)
                    pool.wait_ge(stored, blocks_stored)
                    for h in range(NH):
                        if ready[h] == blocks:
                            nc.gpsimd.indirect_dma_start(out=sums[:, h, :], out_offset=None, in_=D.slot_sums[0:blocks * BLOCK, :],
                                                         in_offset=rows_of(S.last_slot[:, h:h + 1])).then_inc(gathered, 16)


def spread_nodes(nc, sb, sem, pb, D, S):
    stored = sem("spread_table_stored")
    placed = sem("spread_rows_placed")
    with nc.Block() as block:
        @block.sync
        def _(sp):
            sp.dma_start(D.table2[:, :].rearrange("(h p) f -> p h f", p=P), S.x[:]).then_inc(stored, 16)
            sp.wait_ge(stored, 16)

        @block.gpsimd
        def _(pool):
            for h in range(NH):
                nc.gpsimd.indirect_dma_start(out=D.inject[:, :], out_offset=rows_of(S.first_edge[:, h:h + 1]),
                                             in_=S.x[:, h, :], in_offset=None).then_inc(placed, 16)
            pool.wait_ge(placed, 16 * NH)


def judge_edges(nc, sb, sem, pb, D, S):
    WIDE = 3 * FEAT
    ring = sb("ring2", [P, 2, LANES], i32)
    rows = sb("rows2", [P, 2, LANES, WIDE], f32)
    flags = sb("flags2", [WIDE, 2, CHUNK], bf16)
    feat = sb("feat2", [WIDE, 2, CHUNK], f32)
    hidden = sb("hidden2", [HID, 2, CHUNK], f32)
    best = sb("best2", [FEAT, 2, CHUNK], f32)
    out = sb("out2", [P, 2, LANES, FEAT], f32)
    w1 = sb("w1_2", [WIDE, HID], f32)
    w2 = sb("w2_2", [HID, P], f32)
    b1 = sb("b1_2", [HID, 1], f32)
    p_feat = pb("p_feat", [WIDE, 2, CHUNK], f32)
    p_hid = pb("p_hid", [HID, CHUNK], f32)
    p_msg = pb("p_msg", [P, 2, CHUNK], f32)
    p_back = pb("p_back", [P, LANES, FEAT], f32)

    def pair_of(what):
        return [sem(f"judge_{what}_{u}") for u in range(2)]

    begun = sem("judge_first_states_made")
    w_loaded = sem("judge_weights_loaded")
    first_listed = sem("judge_first_sources_listed")
    listed, gathered, loaded, turned = pair_of("sources_listed"), pair_of("rows_gathered"), pair_of("rows_loaded"), pair_of("rows_turned")
    copied, held, lifted, rectified = pair_of("features_copied"), pair_of("dst_held"), pair_of("hidden_multiplied"), pair_of("hidden_rectified")
    sent, topped, back = pair_of("messages_multiplied"), pair_of("maxima_scanned"), pair_of("maxima_turned_back")
    emptied, stored, flagged = pair_of("out_emptied"), pair_of("out_stored"), pair_of("neg_flags_loaded")
    STEPS = CHUNKS
    assert STEPS % 2 == 0
    last_edges = N_EDGES - (STEPS - 1) * CHUNK

    def skewed(eng, stage):
        with eng.Fori(0, STEPS // 2 - 1) as i:
            stage(i * 2 + 1, 1, i)
            stage(i * 2 + 2, 0, i + 1)
        stage(STEPS - 1, 1, STEPS // 2 - 1)

    def before(u, n):
        return (0, n) if u else (1, n - 1)

    with nc.Block() as block:
        @block.gpsimd
        def _(pool):
            with pool.Fori(0, STEPS // 2) as i:
                for u in range(2):
                    pool.wait_ge(first_listed, 2)
                    pool.wait_ge(turned[u], i)
                    pool.wait_ge(listed[u], i)
                    for j in range(LANES):
                        nc.gpsimd.indirect_dma_start(out=rows[:, u, j, 0:FEAT], out_offset=None, in_=D.table2[:, :],
                                                     in_offset=rows_of(ring[:, u, j:j + 1])).then_inc(gathered[u], 16)

        @block.sync
        def _(sp):
            sp.wait_ge(begun, 1)
            sp.dma_start(w1[0:FEAT, :], D.W1[0:FEAT, :]).then_inc(w_loaded, 16)
            sp.dma_start(w1[FEAT:2 * FEAT, :], D.W1[2 * FEAT:3 * FEAT, :]).then_inc(w_loaded, 16)
            sp.dma_start(w1[2 * FEAT:3 * FEAT, :], D.W1[FEAT:2 * FEAT, :]).then_inc(w_loaded, 16)
            sp.dma_start(w2[:, 0:FEAT], D.W2[:, :]).then_inc(w_loaded, 16)
            sp.dma_start(b1[:], D.b1[:].unsqueeze(1), allow_slow_non_contiguous=True).then_inc(w_loaded, 16)

            def load(k, u, n, before_last):
                at = bass.ds(k * CHUNK, CHUNK)
                sp.wait_ge(turned[u], before_last)
                sp.wait_ge(held[u], before_last)
                sp.dma_start(rows[0:n // LANES, u, :, FEAT:2 * FEAT],
                             D.attr[bass.ds(k * CHUNK, n), :].rearrange("(p j) f -> p j f", j=LANES)).then_inc(loaded[u], 16)
                sp.dma_start(rows[:, u, :, 2 * FEAT:WIDE],
                             D.inject[at, :].rearrange("(p j) f -> p j f", j=LANES)).then_inc(loaded[u], 16)
                sp.dma_start(flags[2 * FEAT:WIDE, u], D.keep[at].unsqueeze(0).to_broadcast([FEAT, CHUNK])).then_inc(loaded[u], 16)
                sp.wait_ge(begun, 1)
                sp.wait_ge(topped[u], before_last)
                sp.dma_start(flags[0:FEAT, u], D.neg[at].unsqueeze(0).to_broadcast([FEAT, CHUNK])).then_inc(flagged[u], 16)

            with sp.Fori(0, STEPS // 2 - 1) as i:
                for u in range(2):
                    load(i * 2 + u, u, CHUNK, i)
            for u in range(2):
                load(STEPS - 2 + u, u, last_edges if u else CHUNK, STEPS // 2 - 1)

        @block.tensor
        def _(pe):
            def turn(u, n):
                pe.wait_ge(copied[u], n)
                pe.wait_ge(held[u], n)
                pe.wait_ge(loaded[u], n * 48 + 48)
                pe.wait_ge(gathered[u], n * (16 * LANES) + 16 * LANES)
                for j in range(LANES):
                    last = nc.tensor.transpose(p_feat[:, u, j::LANES], rows[:, u, j, :], S.ident[:])
                last.then_inc(turned[u], 1)

            def lift(u, n):
                pe.wait_ge(rectified[1 - u], n if u == 0 else n + 1)
                pe.wait_ge(copied[u], n + 1)
                pe.wait_ge(held[u], n + 1)
                nc.tensor.matmul(p_hid[:], w1[:], feat[:, u], start=True, stop=True).then_inc(lifted[u], 1)

            def send(u, n):
                pe.wait_ge(topped[u], n)
                pe.wait_ge(rectified[u], n + 1)
                nc.tensor.matmul(p_msg[:, u], w2[:], hidden[:, u], start=True, stop=True).then_inc(sent[u], 1)

            def turn_back(u, n):
                pe.wait_ge(w_loaded, 80)
                pe.wait_ge(emptied[1 - u], n if u == 0 else n + 1)
                pe.wait_ge(topped[u], n + 1)
                for j in range(LANES):
                    last = nc.tensor.transpose(p_back[:, j, :], best[:, u, j::LANES], S.ident[0:FEAT, 0:FEAT])
                last.then_inc(back[u], 1)

            def stage(k, u, n):
                turn(u, n)
                send(*before(u, n))
                lift(u, n)
                turn_back(*before(u, n))

            pe.wait_ge(w_loaded, 80)
            turn(0, 0)
            lift(0, 0)
            skewed(pe, stage)
            send(1, STEPS // 2 - 1)
            turn_back(1, STEPS // 2 - 1)

        @block.vector
        def _(dve):
            nc.vector.memset(rows[:, 1, :, FEAT:2 * FEAT], 0.0)
            nc.vector.memset(w2[:], 0.0)
            nc.vector.memset(feat[2 * FEAT:WIDE, 1, CHUNK - 1:], 0.0)
            nc.vector.memset(best[:, 1, CHUNK - 1:], NEG).then_inc(begun, 1)
            dve.wait_ge(begun, 1)

            def hold(u, n):
                dve.wait_ge(lifted[u], n)
                dve.wait_ge(held[1 - u], n if u == 0 else n + 1)
                dve.wait_ge(loaded[u], n * 48 + 48)
                dve.wait_ge(turned[u], n + 1)
                nc.vector.tensor_tensor_scan(out=feat[2 * FEAT:WIDE, u], data0=flags[2 * FEAT:WIDE, u],
                                             data1=p_feat[2 * FEAT:WIDE, u],
                                             initial=feat[2 * FEAT:WIDE, 1 - u, CHUNK - 1:],
                                             op0=ALU.mult, op1=ALU.add).then_inc(held[u], 1)

            def top(u, n):
                dve.wait_ge(back[u], n)
                dve.wait_ge(topped[1 - u], n if u == 0 else n + 1)
                dve.wait_ge(flagged[u], n * 16 + 16)
                dve.wait_ge(sent[u], n + 1)
                nc.vector.tensor_tensor_scan(out=best[:, u], data0=flags[0:FEAT, u], data1=p_msg[0:FEAT, u],
                                             initial=best[:, 1 - u, CHUNK - 1:],
                                             op0=ALU.add, op1=ALU.max).then_inc(topped[u], 1)

            def stage(k, u, n):
                hold(u, n)
                top(*before(u, n))

            hold(0, 0)
            skewed(dve, stage)
            top(1, STEPS // 2 - 1)

        @block.scalar
        def _(act):
            for u in range(2):
                nc.scalar.copy(ring[:, u], S.src_all[:, u * LANES:(u + 1) * LANES]).then_inc(first_listed, 1)
            act.wait_ge(w_loaded, 80)

            def copy(k, u, n):
                act.wait_ge(gathered[u], n * (16 * LANES) + 16 * LANES)
                nc.scalar.copy(ring[:, u], S.src_all[:, bass.ds(k * LANES + 2 * LANES, LANES)]).then_inc(listed[u], 1)
                act.wait_ge(lifted[u], n)
                act.wait_ge(turned[u], n + 1)
                nc.scalar.copy(feat[0:2 * FEAT, u], p_feat[0:2 * FEAT, u]).then_inc(copied[u], 1)

            def rectify(u, n):
                act.wait_ge(sent[u], n)
                act.wait_ge(lifted[u], n + 1)
                nc.scalar.activation(hidden[:, u], p_hid[:], ACT.Relu, bias=b1[:, 0:1]).then_inc(rectified[u], 1)

            def put_out(k, u, n):
                act.wait_ge(stored[u], n * 16)
                act.wait_ge(back[u], n + 1)
                nc.scalar.copy(out[:, u], p_back[:]).then_inc(emptied[u], 1)
                act.wait_ge(emptied[u], n + 1)
                act.dma_start(D.scan2[bass.ds(k * CHUNK, CHUNK), :].rearrange("(p j) f -> p (j f)", j=LANES),
                              out[:, u].rearrange("p j f -> p (j f)")).then_inc(stored[u], 16)

            def stage(k, u, n):
                copy(k, u, n)
                rectify(u, n)
                put_out(k - 1, *before(u, n))

            copy(0, 0, 0)
            rectify(0, 0)
            skewed(act, stage)
            put_out(STEPS - 1, 1, STEPS // 2 - 1)
            for u in range(2):
                act.wait_ge(stored[u], 16 * (STEPS // 2))


def finish_judging(nc, sb, sem, pb, D, S):
    S.square = sb("square_finish_judging", [P, NH, FEAT], f32)
    best = sb("best_node", [P, NH, FEAT], f32)
    b2 = sb("b2_all", [P, FEAT], f32)
    none = sb("none", [P, NH], f32)
    b2_loaded = sem("finish2_b2_loaded")
    gathered = sem("finish2_ends_gathered")
    v = sem("finish2_vector_step")
    root_go, root_done = sem("finish2_variance_made"), sem("finish2_root_taken")
    steps = [0]

    def link(ins):
        steps[0] += 1
        ins.then_inc(v, 1)
        nc.vector.wait_ge(v, steps[0])
        return steps[0]

    with nc.Block() as block:
        @block.sync
        def _(sp):
            sp.dma_start(b2[:], D.b2[:].unsqueeze(0).to_broadcast([P, FEAT])).then_inc(b2_loaded, 16)

        @block.gpsimd
        def _(pool):
            for h in range(NH):
                nc.gpsimd.indirect_dma_start(out=best[:, h, :], out_offset=None, in_=D.scan2[:, :],
                                             in_offset=rows_of(S.last_edge[:, h:h + 1])).then_inc(gathered, 16)

        @block.vector
        def _(dve):
            link(nc.vector.tensor_scalar(none[:], S.has_edges[:], 1.0, -2.0 * NEG, ALU.subtract, ALU.mult))
            dve.wait_ge(b2_loaded, 16)
            dve.wait_ge(gathered, 16 * NH)
            link(nc.vector.tensor_tensor(best[:], best[:], b2[:].unsqueeze(1).to_broadcast([P, NH, FEAT]), ALU.add))
            link(nc.vector.tensor_tensor(best[:], best[:], over_features(none[:]), ALU.add))
            link(nc.vector.tensor_tensor(best[:], best[:], S.x[:], ALU.max))
            link(nc.vector.tensor_tensor(S.work[:], best[:], S.x[:], ALU.add))
            normalize(nc, dve, root_done, root_go, link, S.work, S, S.x)

        @block.scalar
        def _(act):
            act.wait_ge(root_go, 1)
            nc.scalar.activation(S.stat[:, 1], S.stat[:, 1], ACT.Sqrt).then_inc(root_done, 1)


def write_out(nc, sem, D, S):
    stored = sem("output_stored")
    full = N_NODES // P
    with nc.Block() as block:
        @block.sync
        def _(sp):
            sp.dma_start(D.out[0:full * P, :].rearrange("(h p) f -> p h f", p=P), S.x[:, 0:full, :]).then_inc(stored, 16)
            sp.dma_start(D.out[full * P:N_NODES, :], S.x[0:N_NODES - full * P, full, :]).then_inc(stored, 16)
            sp.wait_ge(stored, 32)


def graph_layers(nc, x, src, dst, attr, w1_W, w1_b, w2_W, w2_b, a, W1, b1, W2, b2, out, upto=99, only=None):
    D = Names()
    D.x, D.src, D.dst, D.attr, D.out = x, src, dst, attr, out
    D.w1_W, D.w1_b, D.w2_W, D.w2_b, D.a = w1_W, w1_b, w2_W, w2_b, a
    D.W1, D.b1, D.W2, D.b2 = W1, b1, W2, b2

    def dram(name, shape, dt):
        return nc.dram_tensor(name, shape, dt, kind="Internal").ap()

    D.slot_flags = dram("slot_flags", [SLOTS + P, 1], i32)
    D.edge_table = dram("edge_table", [TILES, 2 * P], i32)
    D.keep = dram("keep_flags", [E_PAD], bf16)
    D.neg = dram("neg_flags", [E_PAD], bf16)
    D.inject = dram("inject", [E_PAD + N_PAD, FEAT], f32)
    D.table0 = dram("table0", [N_PAD, 2 * FEAT], f32)
    D.table2 = dram("table2", [N_PAD, FEAT], f32)
    D.info = dram("info", [INFO_SPARE + SLOTS, 2], i32)
    D.matrix = dram("matrix", [SLOTS // PAIR, N_PARTS, P, HI_PART * PAIR], u8)
    D.scan0 = dram("scan0", [E_PAD, Y0_ROW], f32)
    D.scan2 = dram("scan2", [CHUNKS * CHUNK, FEAT], f32)
    D.slot_sums = dram("slot_sums", [SLOTS, FEAT], f32)

    with ExitStack() as whole:
        def keeper(stack, alloc, prefix=""):
            return lambda name, *spec: stack.enter_context(alloc(prefix + name, *spec))

        sb = keeper(whole, nc.sbuf_tensor)
        sem = keeper(whole, nc.semaphore)
        S = Names()
        S.tables_done = sem("tables_done")
        S.place_loaded = [sem(f"propagate_place{w}_loaded") for w in range(PLACES)]
        S.place_widened = [sem(f"propagate_place{w}_widened") for w in range(PLACES)]
        S.place_multiplied = [sem(f"propagate_place{w}_multiplied") for w in range(PLACES)]
        S.block_sems = [sem("propagate_" + what) for what in (
            "x_split", "flags_loaded", "block_scanned", "carry_kept", "block_turned_back", "block_emptied",
            "block_stored", "sums_gathered")]
        S.x = sb("x_sb", [P, NH, FEAT], f32)
        S.base = sb("base", [P, NH, FEAT], f32)
        S.stat = sb("stat", [P, 2, NH], f32)
        S.ident = sb("ident", [P, P], f32)
        S.ident_bf = sb("ident_bf", [P, P], bf16)
        S.before = sb("before", [P, P], f32)
        S.group_pick = sb("group_pick", [P, GROUPS], f32)
        S.part_sum = sb("part_sum", [3 * FEAT, FEAT], f32)
        S.ramp_hi = sb("ramp_hi", [P, NH], bf16)
        S.ramp_lo = sb("ramp_lo", [P, P], bf16)
        S.slot_id = sb("slot_id", [P, SLOT_COLS], f32)
        S.node_id = sb("node_id", [P, NH], f32)
        S.src_all = sb("src_all", [P, E_PAD // P + 2 * LANES], i32)
        S.has_edges, S.mean_scale, S.norm_scale, S.one_scale = (
            sb(name, [P, NH], f32) for name in ("has_edges", "mean_scale", "norm_scale", "one_scale"))
        S.last_slot, S.last_edge, S.first_edge = (
            sb(name, [P, NH], i32) for name in ("last_slot", "last_edge", "first_edge"))

        def stage(build, *more):
            if only and build.__name__ not in only:
                return
            with ExitStack() as local:
                prefix = "_".join([build.__name__, *more[:1], ""])
                build(nc, keeper(local, nc.sbuf_tensor, prefix), sem, keeper(local, nc.psum_tensor, prefix), D, S, *more)

        stages = [lambda: stage(prepare_constants), lambda: stage(prepare_nodes)]

        def matrix():
            with ExitStack() as local:
                S.key_hi = keeper(local, nc.sbuf_tensor)("key_hi_all", [P, SLOTS + SUB], bf16)
                S.key_lo = keeper(local, nc.sbuf_tensor)("key_lo_all", [P, SLOTS + SUB], bf16)
                stage(prepare_slots)
                stage(prepare_ends)
                stage(attend_and_count)
            S.work = sb("work", [P, NH, FEAT], f32)
        stages += [matrix, lambda: stage(finish_attention),
                   lambda: stage(propagate, "mean", 0, S.one_scale, S.mean_scale),
                   lambda: stage(spread_nodes), lambda: stage(judge_edges), lambda: stage(finish_judging),
                   lambda: stage(propagate, "norm", 1, S.norm_scale, S.norm_scale)]
        for run in stages[:upto]:
            run()
        write_out(nc, sem, D, S)


_INS = ["x", "src", "dst", "edge_attr_32", "L0_gnn_w1_W", "L0_gnn_w1_b", "L0_gnn_w2_W", "L0_gnn_w2_b", "L0_gnn_a",
        "L2_gnn_W1", "L2_gnn_b1", "L2_gnn_W2", "L2_gnn_b2"]


def kernel(**inputs):
    import numpy as _np
    import concourse.bacc as _bacc
    from concourse import mybir as _mybir
    from concourse.bass_utils import run_bass_kernel_spmd as _run

    nc = _bacc.Bacc("TRN2", target_bir_lowering=False, num_devices=1)
    arrays, args = {}, []
    for name in _INS:
        a = _np.ascontiguousarray(inputs[name])
        arrays[f"in_{name}_dram"] = a
        args.append(nc.dram_tensor(f"in_{name}_dram", a.shape, _mybir.dt.from_np(a.dtype), kind="ExternalInput").ap())
    args.append(nc.dram_tensor("out_dram", (N_NODES, FEAT), _mybir.dt.float32, kind="ExternalOutput").ap())
    graph_layers(nc, *args)
    r = _run(nc, [arrays], core_ids=[0])
    return r.results[0]["out_dram"]
```

```python
import concourse.bass as bass
from concourse import mybir
from contextlib import ExitStack

P = 128
N_NODES, N_EDGES, FEAT, HID = 12500, 400000, 32, 64
NH = -(-N_NODES // P)
N_PAD = NH * P
TILES = N_EDGES // P
SUB = 32
BLOCK = 512
N_BLOCKS = -(-(TILES + N_NODES - 1) // BLOCK)
SLOTS = N_BLOCKS * BLOCK
SLOT_COLS = SLOTS // P
HI_PART = 14
N_PARTS = NH // HI_PART
PAIR = 2 * SUB
CHUNK = 512
LANES = CHUNK // P
GROUPS = 4
CHUNKS = -(-N_EDGES // CHUNK)
GROUP_CHUNKS = -(-CHUNKS // GROUPS)
GROUP_EDGES = GROUP_CHUNKS * CHUNK
E_PAD = GROUPS * GROUP_EDGES
ATTEND_STEPS, COUNT_SUBS = 4, 10
COUNTED_PAIRS = GROUP_CHUNKS // ATTEND_STEPS * COUNT_SUBS // 2
HALF_CHUNKS = CHUNKS // 2
HALF_EDGES = HALF_CHUNKS * CHUNK
STAGES = 3
PLACE = (0, 1, 2, 3, 4, 2, 3)
PLACES = 5
SPLIT_PART = 4
SRC_PIECES = 11
SLOT_BATCH = 31
N_BATCHES = SLOT_COLS // SLOT_BATCH
INFO_SPARE = 13056
SLICE = 14
SLICES = [slice(first, first + SLICE) for first in range(0, NH, SLICE)]
NEG = -1.0e30
EPS = 1e-5
Y0_ROW = FEAT + 2

f32, bf16, i32, u8 = mybir.dt.float32, mybir.dt.bfloat16, mybir.dt.int32, mybir.dt.uint8
ALU = mybir.AluOpType
ACT = mybir.ActivationFunctionType
AX = mybir.AxisListType


class Names:
    pass


def rows_of(ap):
    return bass.IndirectOffsetOnAxis(ap=ap, axis=0)


def over_features(ap):
    return ap.unsqueeze(2).to_broadcast([P, ap.shape[1], FEAT])


def prepare_constants(nc, sb, sem, pb, D, S):
    zeros = sb("zeros", [P, NH * PAIR // 4], f32)
    ones_i = sb("ones_i", [P, 1], i32)
    theta = sb("theta", [P, 25], i32)
    theta_t = sb("theta_t", [P, 25], i32)
    tile_head_cols = -(-(TILES - 1) // P)
    src_pad = sb("src_pad", [P, LANES], i32)
    dst_run = TILES
    dst_sb = sb("dst_sb", [P, dst_run + 1], i32)
    keep = sb("keep", [P, dst_run], bf16)
    neg = sb("neg", [P, dst_run], bf16)
    zero_bf = sb("zero_bf", [P, 128], bf16)

    made = sem("const_made")
    zeroed = sem("const_fills_made")
    flags_zero = sem("const_slot_flags_zeroed")
    rest_zero = sem("const_matrix_rest_zeroed")
    heads_loaded = sem("const_tile_heads_loaded")
    heads_added = sem("const_tile_heads_added")
    flags_set = sem("const_slot_flags_set")
    table_copied = sem("const_edge_table_copied")
    dst_loaded = sem("const_dst_loaded")
    keep_made = sem("const_keep_made")
    neg_made = sem("const_neg_made")
    flags_stored = sem("const_scan_flags_stored")

    with nc.Block() as block:
        @block.sync
        def _(sp):
            heads = D.dst[:].rearrange("(t e) -> t e", e=P)[1:TILES, 0:1]
            full = (tile_head_cols - 1) * P
            sp.dma_start(theta[:, 0:tile_head_cols - 1],
                         heads[0:full].rearrange("(r p) o -> p (r o)", p=P),
                         allow_slow_non_contiguous=True).then_inc(heads_loaded, 16)
            sp.dma_start(theta[0:TILES - 1 - full, tile_head_cols - 1:tile_head_cols],
                         heads[full:TILES - 1],
                         allow_slow_non_contiguous=True).then_inc(heads_loaded, 16)
            runs = D.dst[:].rearrange("(p i) -> p i", p=P)
            sp.wait_ge(zeroed, 2)
            sp.dma_start(dst_sb[:, 1:dst_run + 1], runs).then_inc(dst_loaded, 16)
            sp.dma_start(dst_sb[1:P, 0:1], runs[0:P - 1, dst_run - 1:dst_run],
                         allow_slow_non_contiguous=True).then_inc(dst_loaded, 16)
            sp.dma_start(D.edge_table[:, 0:P], D.src[:].rearrange("(t e) -> t e", e=P)).then_inc(table_copied, 16)
            sp.dma_start(D.edge_table[:, P:2 * P], D.dst[:].rearrange("(t e) -> t e", e=P)).then_inc(table_copied, 16)
            sp.wait_ge(keep_made, 1)
            sp.dma_start(D.keep[0:N_EDGES].rearrange("(p i) -> p i", p=P), keep[:]).then_inc(flags_stored, 16)
            sp.wait_ge(neg_made, 1)
            sp.dma_start(D.neg[0:N_EDGES].rearrange("(p i) -> p i", p=P), neg[:]).then_inc(flags_stored, 16)
            pad = (E_PAD - N_EDGES) // P
            sp.dma_start(D.keep[N_EDGES:E_PAD].rearrange("(p i) -> p i", p=P), zero_bf[:, 0:pad]).then_inc(flags_stored, 16)
            sp.dma_start(D.neg[N_EDGES:E_PAD].rearrange("(p i) -> p i", p=P), zero_bf[:, 0:pad]).then_inc(flags_stored, 16)
            sp.wait_ge(table_copied, 32)
            sp.wait_ge(flags_stored, 64)

        @block.scalar
        def _(act):
            act.wait_ge(zeroed, 1)
            act.dma_start(D.slot_flags[:].rearrange("(p i) o -> p (i o)", p=P),
                          zeros[:, 0:(SLOTS + P) // P].bitcast(i32)).then_inc(flags_zero, 16)
            for s in range(COUNTED_PAIRS, SLOTS // PAIR):
                act.dma_start(D.matrix[s].rearrange("q p x -> p q x"),
                              zeros[:].bitcast(u8)[:, 0:NH * PAIR].rearrange("p (q x) -> p q x", q=N_PARTS)).then_inc(rest_zero, 16)
            act.wait_ge(rest_zero, 16 * (SLOTS // PAIR - COUNTED_PAIRS))

        @block.gpsimd
        def _(pool):
            pg = nc.gpsimd
            pg.iota(S.ramp_hi[:], pattern=[[1, NH]], base=1, channel_multiplier=0,
                    allow_small_or_imprecise_dtypes=True)
            pg.iota(S.ramp_lo[:], pattern=[[1, P]], base=0, channel_multiplier=0,
                    allow_small_or_imprecise_dtypes=True)
            pg.iota(S.slot_id[:], pattern=[[P, SLOT_COLS]], base=0, channel_multiplier=1,
                    allow_small_or_imprecise_dtypes=True)
            pg.iota(S.node_id[:], pattern=[[P, NH]], base=0, channel_multiplier=1,
                    allow_small_or_imprecise_dtypes=True)
            pg.iota(theta_t[:], pattern=[[P, 25]], base=1, channel_multiplier=1)
            pg.memset(ones_i[:], 1)
            pg.memset(S.ident[:], 1.0)
            pg.memset(S.before[:], 1.0)
            pg.memset(S.group_pick[:], 0.0).then_inc(made, 1)
            pool.wait_ge(made, 1)
            pg.affine_select(out=S.ident[:], in_=S.ident[:], compare_op=ALU.is_equal, fill=0.0,
                             base=0, pattern=[[-1, P]], channel_multiplier=1)
            pg.affine_select(out=S.before[:], in_=S.before[:], compare_op=ALU.is_gt, fill=0.0,
                             base=0, pattern=[[1, P]], channel_multiplier=-1)
            pg.affine_select(out=S.group_pick[:], in_=S.group_pick[:], compare_op=ALU.not_equal, fill=1.0,
                             base=0, pattern=[[-FEAT, GROUPS]], channel_multiplier=1).then_inc(made, 1)
            pool.wait_ge(heads_loaded, 32)
            full = tile_head_cols - 1
            last = TILES - 1 - full * P
            pg.tensor_tensor(theta[:, 0:full], theta[:, 0:full], theta_t[:, 0:full], ALU.add)
            pg.tensor_tensor(theta[0:last, full:], theta[0:last, full:], theta_t[0:last, full:], ALU.add).then_inc(heads_added, 1)
            pool.wait_ge(heads_added, 1)
            pool.wait_ge(flags_zero, 16)
            for r in range(tile_head_cols):
                n = P if r < full else last
                pg.indirect_dma_start(out=D.slot_flags[:], out_offset=rows_of(theta[0:n, r:r + 1]),
                                      in_=ones_i[0:n, :], in_offset=None).then_inc(flags_set, 16)
            pool.wait_ge(flags_set, 16 * tile_head_cols)

        @block.vector
        def _(dve):
            nc.vector.memset(zeros[:], 0.0)
            nc.vector.memset(zero_bf[:], 0.0).then_inc(zeroed, 1)
            nc.vector.memset(dst_sb[:, 0:1], -1).then_inc(zeroed, 1)
            nc.vector.memset(S.src_all[:], 0).then_inc(zeroed, 1)
            dve.wait_ge(dst_loaded, 32)
            nc.vector.tensor_tensor(keep[:], dst_sb[:, 1:dst_run + 1], dst_sb[:, 0:dst_run],
                                    ALU.is_equal).then_inc(keep_made, 1)
            dve.wait_ge(keep_made, 1)
            nc.vector.tensor_scalar(neg[:], keep[:], 1.0, -NEG, ALU.subtract, ALU.mult).then_inc(neg_made, 1)
            dve.wait_ge(made, 2)
            nc.vector.tensor_copy(S.ident_bf[:], S.ident[:])


def prepare_slots_and_nodes(nc, sb, sem, pb, D, S):
    C, B = SLOT_COLS, SLOT_BATCH
    STEP = 7
    NODE_STEPS = NH // STEP
    AT_FIRST, BESIDE = 2, 1
    EARLY = AT_FIRST + N_BATCHES * BESIDE
    full = N_NODES // P
    w_nat = sb("w_nat", [FEAT, 2, FEAT], f32)
    a_col = sb("a_col", [FEAT, 1], f32)
    a_neg = sb("a_neg", [FEAT, FEAT], f32)
    w_all = sb("w_all", [FEAT + 1, 3, FEAT], f32)
    x_step = sb("x_step", [P, STEP, FEAT], f32)
    xt = sb("xt", [FEAT + 1, STEP * P], f32)
    table = sb("table", [P, STEP, 2 * FEAT], f32)
    flags = sb("flags", [C, 2, P], i32)
    flags_f = sb("flags_f", [C, 2, P], f32)
    ones = sb("ones", [C, P], f32)
    run = sb("run", [C, P], f32)
    whole = sb("whole", [C, P], f32)
    tile_of = sb("tile_of", [P, C], f32)
    going = sb("going", [P, C], f32)
    node_of = sb("node_of", [P, C], f32)
    tile_idx = sb("tile_idx", [P, C], i32)
    edges = sb("edges", [P, 2, B, 2 * P], i32)
    match = sb("match", [P, B, P], bf16)
    key_hi = sb("key_hi", [P, B, P], bf16)
    key_lo = sb("key_lo", [P, B, P], bf16)
    count = sb("count", [P, C], f32)
    info = sb("info_sb", [P, C, 2], i32)
    info_idx = sb("info_idx", [P, C], i32)
    info_f = sb("info_f", [P, C], f32)
    first_row = sb("first_row", [1, 2], i32)
    p_a = pb("p_a", [P, 512], f32)
    p_keys = pb("p_keys", [P, 4, 1024], bf16)
    p_x = pb("p_x", [P, 2, 512], f32)
    p_w = p_a[0:FEAT, 384:384 + 3 * FEAT].rearrange("k (b f) -> k b f", f=FEAT)

    pad_zero = sem("nodes_pad_zeroed")
    x_loaded = sem("nodes_x_loaded")
    w_loaded = sem("nodes_w_loaded")
    a_made = sem("nodes_a_negated")
    w_turned = sem("nodes_w_turned")
    w_made = sem("nodes_w_made")
    x_staged = sem("nodes_x_staged")
    x_turned = sem("nodes_x_turned")
    xt_made = sem("nodes_xt_made")
    multiplied = sem("nodes_multiplied")
    emptied = sem("nodes_emptied")
    table_stored = sem("nodes_table_stored")
    flags_loaded = sem("slots_flags_loaded")
    v = sem("slots_vector_step")
    summed = sem("slots_carry_summed")
    turned = sem("slots_turned")
    gathered = [sem(f"slots_edges{u}_gathered") for u in range(2)]
    keys_made = sem("slots_keys_made")
    keys_turned = sem("slots_keys_turned")
    keys_kept = sem("slots_keys_kept")
    scattered = sem("slots_info_scattered")
    src_loaded = sem("slots_src_index_loaded")
    row_made = sem("slots_first_row_made")
    row_stored = sem("slots_first_row_stored")
    steps = [0]

    def link(ins):
        steps[0] += 1
        ins.then_inc(v, 1)
        nc.vector.wait_ge(v, steps[0])
        return steps[0]

    marks = {}

    with nc.Block() as block:
        @block.vector
        def _(dve):
            nc.vector.memset(S.x[:, full, :], 0.0).then_inc(pad_zero, 1)
            nc.vector.memset(ones[:], 1.0)
            nc.vector.memset(first_row[:], 0).then_inc(row_made, 1)
            nc.vector.memset(xt[FEAT:FEAT + 1, :], 1.0)
            nc.vector.memset(w_all[FEAT:FEAT + 1, 1, :], 0.0)
            dve.wait_ge(w_loaded, 80)
            nc.vector.tensor_scalar(a_neg[:], a_col[:].to_broadcast([FEAT, FEAT]), -1.0, None, ALU.mult).then_inc(a_made, 1)
            dve.wait_ge(w_turned, 1)
            nc.vector.tensor_copy(w_all[0:FEAT, 0:2], p_w[:, 0:2]).then_inc(w_made, 1)
            nc.vector.tensor_tensor(w_all[0:FEAT, 2], p_w[:, 2], S.ident[0:FEAT, 0:FEAT], ALU.add).then_inc(w_made, 1)
            nc.vector.memset(S.key_hi[:, SLOTS:], 0.0)
            nc.vector.memset(S.key_lo[:, SLOTS:], 0.0)
            dve.wait_ge(flags_loaded, 32)
            link(nc.vector.tensor_copy(flags_f[:], flags[:]))
            link(nc.vector.tensor_tensor_scan(out=run[:], data0=ones[:], data1=flags_f[:, 0, :], initial=0.0,
                                              op0=ALU.mult, op1=ALU.add))
            dve.wait_ge(summed, 1)
            link(nc.vector.tensor_scalar(whole[:], run[:], p_a[0:C, 0:1], None, ALU.add))
            dve.wait_ge(turned, 1)
            link(nc.vector.tensor_copy(tile_of[:], p_a[:, 128:128 + C]))
            link(nc.vector.tensor_copy(going[:], p_a[:, 256:256 + C]))
            link(nc.vector.tensor_tensor(node_of[:], S.slot_id[:], tile_of[:], ALU.subtract))
            link(nc.vector.tensor_copy(tile_idx[:], tile_of[:]))
            base = steps[0]
            marks["tile_idx"] = base
            with dve.Fori(0, N_BATCHES // 2) as i:
                for u in range(2):
                    batch = i * 2 + u
                    at = bass.ds(batch * B, B)
                    src, dst = edges[:, u, :, 0:P], edges[:, u, :, P:2 * P]
                    dve.wait_ge(gathered[u], (i + 1) * 16 * B)
                    dve.wait_ge(keys_turned, batch * 2)
                    nc.vector.tensor_tensor(match[:], dst, node_of[:, at].unsqueeze(2).to_broadcast([P, B, P]), ALU.is_equal).then_inc(v, 1)
                    dve.wait_ge(v, batch * 4 + (base + 1))
                    nc.vector.tensor_scalar(dst, src, 7, None, ALU.logical_shift_right).then_inc(v, 1)
                    nc.vector.tensor_reduce(count[:, at], match[:], AX.X, ALU.add)
                    dve.wait_ge(v, batch * 4 + (base + 2))
                    nc.vector.scalar_tensor_tensor(key_hi[:], dst, 1.0, match[:], ALU.add, ALU.mult).then_inc(v, 1)
                    nc.vector.tensor_scalar(src, src, 127, None, ALU.bitwise_and).then_inc(v, 1)
                    dve.wait_ge(v, batch * 4 + (base + 4))
                    nc.vector.tensor_copy(key_lo[:], src).then_inc(keys_made, 1)
                    dve.wait_ge(keys_made, batch + 1)
            steps[0] = base + 4 * N_BATCHES
            link(nc.vector.tensor_copy(tile_of[:], count[:]))
            marks["count"] = steps[0]
            dve.wait_ge(turned, 2)
            link(nc.vector.tensor_tensor_scan(out=run[:], data0=ones[:], data1=p_a[0:C, 0:P], initial=0.0,
                                              op0=ALU.mult, op1=ALU.add))
            marks["run2"] = steps[0]
            dve.wait_ge(summed, 2)
            link(nc.vector.tensor_scalar(whole[:], run[:], p_a[0:C, 128:129], None, ALU.add))
            marks["whole2"] = steps[0]
            dve.wait_ge(turned, 3)
            link(nc.vector.tensor_copy(info[:, :, 1], p_a[:, 256:256 + C]))
            link(nc.vector.tensor_copy(info[:, :, 0], S.slot_id[:]))
            link(nc.vector.tensor_tensor(info_f[:], S.slot_id[:], node_of[:], ALU.subtract))
            link(nc.vector.tensor_scalar(info_f[:], info_f[:], float(INFO_SPARE - 1), None, ALU.add))
            link(nc.vector.tensor_tensor(info_f[:], info_f[:], going[:], ALU.mult))
            link(nc.vector.tensor_tensor(info_f[:], info_f[:], node_of[:], ALU.add))
            link(nc.vector.tensor_scalar(info_f[:], info_f[:], 1.0, None, ALU.add))
            marks["info_idx"] = link(nc.vector.tensor_copy(info_idx[:], info_f[:]))

        @block.tensor
        def _(pe):
            def node_step(i):
                pe.wait_ge(emptied, i * 4)
                pe.wait_ge(x_staged, i + 1)
                for j in range(STEP):
                    last = nc.tensor.transpose(p_x[0:FEAT].rearrange("f b e -> f (b e)")[:, j * P:(j + 1) * P], x_step[:, j, :], S.ident[:])
                last.then_inc(x_turned, 1)
                pe.wait_ge(w_made, 2)
                pe.wait_ge(xt_made, i + 1)
                for j in range(STEP):
                    last = nc.tensor.matmul(p_x[:, j // 4, 96 * (j % 4):96 * (j % 4) + 96],
                                            xt[:, j * P:(j + 1) * P], w_all[:].rearrange("k b f -> k (b f)"),
                                            start=True, stop=True)
                last.then_inc(multiplied, 1)

            pe.wait_ge(w_loaded, 80)
            pe.wait_ge(a_made, 1)
            nc.tensor.transpose(p_w[:, 0, :], w_nat[:, 0, :], S.ident[0:FEAT, 0:FEAT])
            nc.tensor.matmul(p_w[:, 1, :], w_nat[:, 0, :], a_neg[:], start=True, stop=True)
            nc.tensor.transpose(p_w[:, 2, :], w_nat[:, 1, :], S.ident[0:FEAT, 0:FEAT]).then_inc(w_turned, 1)
            pe.wait_ge(v, 2)
            nc.tensor.matmul(p_a[0:C, 0:1], S.before[0:C, 0:C], run[:, P - 1:P], start=True, stop=True).then_inc(summed, 1)
            pe.wait_ge(v, 3)
            nc.tensor.transpose(p_a[:, 128:128 + C], whole[:], S.ident[0:C, 0:C])
            nc.tensor.transpose(p_a[:, 256:256 + C], flags_f[:, 1, :], S.ident[0:C, 0:C]).then_inc(turned, 1)
            with pe.Fori(0, AT_FIRST) as i:
                node_step(i)
            with pe.Fori(0, N_BATCHES) as i:
                for n, key in enumerate((key_hi, key_lo)):
                    pe.wait_ge(keys_kept, 2 * i + n)
                    pe.wait_ge(keys_made, i + 1)
                    for j in range(B):
                        last = nc.tensor.transpose(p_keys[:, j // 8, (j % 8) * P:(j % 8) * P + P],
                                                   key[:, j, :], S.ident_bf[:])
                    last.then_inc(keys_turned, 1)
                for n in range(BESIDE):
                    node_step(i * BESIDE + (AT_FIRST + n))
            pe.wait_ge(v, marks["count"])
            nc.tensor.transpose(p_a[0:C, 0:P], count[:], S.ident[:]).then_inc(turned, 1)
            pe.wait_ge(v, marks["run2"])
            nc.tensor.matmul(p_a[0:C, 128:129], S.before[0:C, 0:C], run[:, P - 1:P], start=True, stop=True).then_inc(summed, 1)
            pe.wait_ge(v, marks["whole2"])
            nc.tensor.transpose(p_a[:, 256:256 + C], whole[:], S.ident[0:C, 0:C]).then_inc(turned, 1)
            with pe.Fori(EARLY, NODE_STEPS) as i:
                node_step(i)

        @block.scalar
        def _(act):
            def node_step(i):
                act.wait_ge(x_turned, i)
                nc.scalar.copy(x_step[:], S.x[:, bass.ds(i * STEP, STEP), :]).then_inc(x_staged, 1)
                act.wait_ge(multiplied, i)
                act.wait_ge(x_turned, i + 1)
                nc.scalar.copy(xt[0:FEAT, :], p_x[0:FEAT].rearrange("f b e -> f (b e)")[:, 0:STEP * P]).then_inc(xt_made, 1)
                act.wait_ge(table_stored, i * 16)
                act.wait_ge(multiplied, i + 1)
                for bank, n in ((0, 4), (1, 3)):
                    lin = p_x[:, bank, 0:n * 96].rearrange("p (j c) -> p j c", c=96)
                    nc.scalar.copy(table[:, 4 * bank:4 * bank + n, :], lin[:, :, 0:2 * FEAT]).then_inc(emptied, 1)
                    nc.scalar.copy(S.base[:, bass.ds(i * STEP + 4 * bank, n), :], lin[:, :, 2 * FEAT:3 * FEAT]).then_inc(emptied, 1)
                act.wait_ge(emptied, i * 4 + 4)
                act.dma_start(D.table0[bass.ds(i * (STEP * P), STEP * P), :].rearrange("(j p) f -> p j f", p=P),
                              table[:]).then_inc(table_stored, 16)

            act.wait_ge(x_loaded, 32)
            act.wait_ge(pad_zero, 1)
            with act.Fori(0, AT_FIRST) as i:
                node_step(i)
            with act.Fori(0, N_BATCHES) as i:
                for n, key in enumerate((S.key_hi, S.key_lo)):
                    act.wait_ge(keys_turned, 2 * i + n + 1)
                    nc.scalar.copy(key[:, bass.ds(i * B * P, B * P)],
                                   p_keys[:].rearrange("p b e -> p (b e)")[:, 0:B * P]).then_inc(keys_kept, 1)
                for n in range(BESIDE):
                    node_step(i * BESIDE + (AT_FIRST + n))
            with act.Fori(EARLY, NODE_STEPS) as i:
                node_step(i)
            act.wait_ge(table_stored, 16 * NODE_STEPS)

        @block.sync
        def _(sp):
            sp.dma_start(w_nat[:, 0, :], D.w2_W[:, :]).then_inc(w_loaded, 16)
            sp.dma_start(w_nat[:, 1, :], D.w1_W[:, :]).then_inc(w_loaded, 16)
            sp.dma_start(a_col[:], D.a[:, :].rearrange("o k -> k o"), allow_slow_non_contiguous=True).then_inc(w_loaded, 16)
            sp.dma_start(w_all[FEAT:FEAT + 1, 0, :], D.w2_b[:].unsqueeze(0)).then_inc(w_loaded, 16)
            sp.dma_start(w_all[FEAT:FEAT + 1, 2, :], D.w1_b[:].unsqueeze(0)).then_inc(w_loaded, 16)
            slot_rows = D.slot_flags[:].rearrange("v o -> (v o)")
            sp.dma_start(flags[:, 0, :], slot_rows[0:SLOTS].rearrange("(c p) -> c p", p=P)).then_inc(flags_loaded, 16)
            sp.dma_start(flags[:, 1, :], slot_rows[1:SLOTS + 1].rearrange("(c p) -> c p", p=P)).then_inc(flags_loaded, 16)
            sp.wait_ge(pad_zero, 1)
            sp.dma_start(S.x[:, 0:full, :], D.x[0:full * P, :].rearrange("(h p) f -> p h f", p=P)).then_inc(x_loaded, 16)
            sp.dma_start(S.x[0:N_NODES - full * P, full, :], D.x[full * P:N_NODES, :]).then_inc(x_loaded, 16)
            sp.wait_ge(row_made, 1)
            sp.dma_start(D.info[0:1, :], first_row[:]).then_inc(row_stored, 16)
            sp.wait_ge(row_stored, 16)
            whole = N_EDGES // CHUNK
            piece = whole // SRC_PIECES
            sp.wait_ge(gathered[1], 16 * B * (N_BATCHES // 2))
            with sp.Fori(0, SRC_PIECES) as i:
                sp.dma_start(S.src_all[:, bass.ds(i * (piece * LANES), piece * LANES)].rearrange("p (k j) -> p k j", j=LANES),
                             D.src[bass.ds(i * (piece * CHUNK), piece * CHUNK)].rearrange("(k p j) -> p k j", p=P, j=LANES)).then_inc(src_loaded, 16)
            rest = (N_EDGES - whole * CHUNK) // LANES
            sp.dma_start(S.src_all[0:rest, whole * LANES:(whole + 1) * LANES],
                         D.src[whole * CHUNK:N_EDGES].rearrange("(p j) -> p j", j=LANES)).then_inc(src_loaded, 16)
            sp.wait_ge(src_loaded, 16 * (SRC_PIECES + 1))

        @block.gpsimd
        def _(pool):
            pool.wait_ge(v, marks["tile_idx"])
            for c in range(C):
                batch = c // B
                if batch >= 2 and c % B == 0:
                    pool.wait_ge(keys_made, batch - 1)
                nc.gpsimd.indirect_dma_start(out=edges[:, batch % 2, c % B, :], out_offset=None, in_=D.edge_table[:, :],
                                             in_offset=rows_of(tile_idx[:, c:c + 1])).then_inc(gathered[batch % 2], 16)
            pool.wait_ge(v, marks["info_idx"])
            for c in range(C):
                nc.gpsimd.indirect_dma_start(out=D.info[:, :], out_offset=rows_of(info_idx[:, c:c + 1]),
                                             in_=info[:, c, :], in_offset=None).then_inc(scattered, 16)
            pool.wait_ge(scattered, 16 * C)


def prepare_ends(nc, sb, sem, pb, D, S):
    own = sb("own", [P, NH, 2], i32)
    prev = sb("prev", [P, NH, 2], i32)
    end = sb("end", [P, NH], f32)
    begin = sb("begin", [P, NH], f32)
    deg = sb("deg", [P, NH], f32)
    tmp = sb("tmp", [P, NH], f32)

    loaded = sem("ends_info_loaded")
    v = sem("ends_vector_step")
    rooted = sem("ends_root_taken")
    steps = [0]

    def link(ins):
        steps[0] += 1
        ins.then_inc(v, 1)
        nc.vector.wait_ge(v, steps[0])
        return steps[0]

    with nc.Block() as block:
        @block.sync
        def _(sp):
            with nc.allow_non_contiguous_dma(reason="one row of two numbers per node, once"):
                sp.dma_start(own[:], D.info[1:1 + N_PAD, :].rearrange("(h p) c -> p h c", p=P)).then_inc(loaded, 16)
                sp.dma_start(prev[:], D.info[0:N_PAD, :].rearrange("(h p) c -> p h c", p=P)).then_inc(loaded, 16)

        @block.vector
        def _(dve):
            dve.wait_ge(loaded, 32)
            link(nc.vector.tensor_copy(S.last_slot[:], own[:, :, 0]))
            link(nc.vector.tensor_copy(end[:], own[:, :, 1]))
            link(nc.vector.tensor_copy(begin[:], prev[:, :, 1]))
            link(nc.vector.tensor_tensor(deg[:], end[:], begin[:], ALU.subtract))
            link(nc.vector.tensor_scalar(S.has_edges[:], deg[:], 0.0, None, ALU.is_gt))
            link(nc.vector.tensor_scalar(tmp[:], end[:], -1.0, 0.0, ALU.add, ALU.max))
            link(nc.vector.tensor_copy(S.last_edge[:], tmp[:]))
            link(nc.vector.tensor_scalar(tmp[:], S.node_id[:], float(E_PAD), None, ALU.add))
            link(nc.vector.tensor_tensor(begin[:], begin[:], tmp[:], ALU.subtract))
            link(nc.vector.tensor_tensor(begin[:], begin[:], S.has_edges[:], ALU.mult))
            link(nc.vector.tensor_tensor(begin[:], begin[:], tmp[:], ALU.add))
            link(nc.vector.tensor_copy(S.first_edge[:], begin[:]))
            ready = link(nc.vector.tensor_scalar(tmp[:], deg[:], 1.0, None, ALU.max))
            link(nc.vector.reciprocal(S.mean_scale[:], tmp[:]))
            dve.wait_ge(rooted, 1)
            link(nc.vector.reciprocal(deg[:], end[:]))
            nc.vector.tensor_tensor(S.norm_scale[:], deg[:], S.has_edges[:], ALU.mult).then_inc(S.tables_done, 1)
            S.root_at = ready

        @block.scalar
        def _(act):
            act.wait_ge(v, S.root_at)
            nc.scalar.activation(end[:], tmp[:], ACT.Sqrt).then_inc(rooted, 1)


def attend_and_count(nc, sb, sem, pb, D, S):
    EACH = GROUPS * LANES
    QUARTERS, SLOTS_Q = 4, SUB // 4
    ring = sb("ring", [P, 2, GROUPS, LANES], i32)
    rows = sb("rows", [P, 2, GROUPS, LANES, 2 * FEAT], f32)
    pack = sb("pack", [P, 2, LANES, 2, GROUPS, FEAT], f32)
    neg = sb("neg0", [P, 2, CHUNK], bf16)
    peak = sb("peak", [P, 2, CHUNK + 1], f32)
    args = sb("args", [P, 2, 2, CHUNK], f32)
    weight = sb("weight", [P, 2, 2, CHUNK], f32)
    value = sb("value", [P, CHUNK], f32)
    num = sb("num", [P, 2, CHUNK], f32)
    den = sb("den", [P, 2, CHUNK], f32)
    out = sb("out", [P, 2, GROUPS, LANES, Y0_ROW], f32)
    zeros = sb("zeros", [P, EACH * FEAT], f32)
    key2_hi = sb("key2_hi", [P, 2, SUB, 2], bf16)
    key2_lo = sb("key2_lo", [P, 2, SUB, 2], bf16)
    hot_hi = sb("hot_hi", [P, 2, SUB, NH], bf16)
    hot_lo = sb("hot_lo", [P, 2, SUB, P], bf16)
    stage = sb("stage", [P, STAGES, NH, PAIR], u8)
    p_val = pb("p_val", [P, CHUNK], f32)
    p_score = pb("p_score", [P, CHUNK], f32)
    p_num = pb("p_num", [P, LANES, P], f32)
    p_stat = pb("p_stat", [P, 2, LANES, GROUPS], f32)
    counts = pb("counts", [P, 2, 2, 512], f32)

    first_listed = sem("attend_first_sources_listed")
    listed = [sem(f"attend_sources{u}_listed") for u in range(2)]
    gathered = [sem(f"attend_rows{u}_gathered") for u in range(2)]
    packed = [sem(f"attend_rows{u}_packed") for u in range(2)]
    flagged = [sem(f"attend_flags{u}_loaded") for u in range(2)]
    turned = [sem(f"attend_rows{u}_turned") for u in range(2)]
    begun = sem("attend_first_states_made")
    v = sem("attend_vector_step")
    exponents = sem("attend_exponents_made")
    weighed = sem("attend_weighed")
    used = [sem(f"attend_rows{u}_used") for u in range(2)]
    scanned = sem("attend_scanned")
    back = [sem(f"attend_sums{u}_turned_back") for u in range(2)]
    emptied = sem("attend_emptied")
    out_stored = [sem(f"attend_out{u}_stored") for u in range(2)]
    paired = sem("matrix_keys_paired")
    hot = sem("matrix_one_hots_made")
    counted = [sem(f"matrix_sub{u}_quarters_counted") for u in range(2)]
    staged = [sem(f"matrix_half{u}_staged") for u in range(2)]
    pair_stored = [sem(f"matrix_stage{w}_stored") for w in range(STAGES)]
    inject_zeroed = sem("spread_rows_zeroed")
    V = 3
    TURNS = GROUP_CHUNKS // ATTEND_STEPS
    SHARE = [range(t * COUNT_SUBS // ATTEND_STEPS, (t + 1) * COUNT_SUBS // ATTEND_STEPS) for t in range(ATTEND_STEPS)]
    PAIRS = COUNT_SUBS // 2
    pairs_on = [len(range(w, PAIRS, STAGES)) for w in range(STAGES)]

    def step_of(i, t):
        return i * ATTEND_STEPS + t, t % 2, i * (ATTEND_STEPS // 2) + t // 2

    def sub_of(i, m):
        return i * COUNT_SUBS + m, m % 2, i * (COUNT_SUBS // 2) + m // 2

    def after(i, t):
        return (i, t + 1) if t + 1 < ATTEND_STEPS else (i + 1, 0)

    def over_steps(eng, one):
        with eng.Fori(0, TURNS - 1) as i:
            for t in range(ATTEND_STEPS):
                one(i, t, False)
        for t in range(ATTEND_STEPS):
            one(TURNS - 1, t, t + 1 == ATTEND_STEPS)

    with nc.Block() as block:
        @block.gpsimd
        def _(pool):
            with pool.Fori(0, TURNS) as i:
                for t in range(ATTEND_STEPS):
                    _, u, n = step_of(i, t)
                    before = pool.snap(pool.to_reg(n))
                    pool.wait_ge(first_listed, 2)
                    pool.wait_ge(packed[u], before)
                    pool.wait_ge(listed[u], before)
                    for g in range(GROUPS):
                        for j in range(LANES):
                            nc.gpsimd.indirect_dma_start(out=rows[:, u, g, j, :], out_offset=None, in_=D.table0[:, :],
                                                         in_offset=rows_of(ring[:, u, g, j:j + 1])).then_inc(gathered[u], 16)

        @block.tensor
        def _(pe):
            def turn(i, t):
                c, u, n = step_of(i, t)
                pe.wait_ge(used[1 - u], n + u)
                pe.wait_ge(packed[u], n + 1)
                for j in range(LANES):
                    for p_out, w in ((p_val, 0), (p_score, 1)):
                        last = nc.tensor.transpose(p_out[:, j::LANES], pack[:, u, j, w].rearrange("p g f -> p (g f)"), S.ident[:])
                last.then_inc(turned[u], 1)

            def turn_back(i, t):
                c, u, n = step_of(i, t)
                pe.wait_ge(emptied, c * 2)
                pe.wait_ge(scanned, c * 2 + 2)
                for j in range(LANES):
                    nc.tensor.transpose(p_num[:, j, :], num[:, u, j::LANES], S.ident[:])
                for j in range(LANES):
                    nc.tensor.matmul(p_stat[:, 0, j, :], den[:, u, j::LANES], S.group_pick[:], start=True, stop=True)
                    last = nc.tensor.matmul(p_stat[:, 1, j, :], peak[:, u, 1 + j::LANES], S.group_pick[:], start=True, stop=True)
                last.then_inc(back[u], 1)

            def count(i, m):
                s, u, n = sub_of(i, m)
                pe.wait_ge(hot, s * 2 + 2)
                for r in range(QUARTERS):
                    pe.wait_ge(staged[r % 2], s * 2 + r // 2)
                    for k in range(SLOTS_Q):
                        slot = r * SLOTS_Q + k
                        last = nc.tensor.matmul(counts[:, r % 2, k // 4, NH * (k % 4):NH * (k % 4) + NH],
                                                hot_lo[:, u, slot, :], hot_hi[:, u, slot, :], start=True, stop=True)
                    last.then_inc(counted[u], 1)

            def one(i, t, is_last):
                for m in SHARE[t]:
                    count(i, m)
                turn_back(i, t)
                if not is_last:
                    turn(*after(i, t))

            turn(0, 0)
            over_steps(pe, one)

        @block.vector
        def _(dve):
            nc.vector.memset(zeros[:], 0.0)
            nc.vector.memset(peak[:, 0, 0:1], NEG)
            nc.vector.memset(num[:, 1, CHUNK - 1:CHUNK], 0.0)
            nc.vector.memset(den[:, 1, CHUNK - 1:CHUNK], 0.0).then_inc(begun, 1)
            dve.wait_ge(begun, 1)

            def compare(i, m):
                s, u, n = sub_of(i, m)
                dve.wait_ge(paired, s * 2 + 2)
                dve.wait_ge(counted[u], n * QUARTERS)
                for hots, ramp, two, width in ((hot_hi, S.ramp_hi, key2_hi, NH), (hot_lo, S.ramp_lo, key2_lo, P)):
                    nc.vector.tensor_tensor(
                        hots[:, u].rearrange("p v (h t) -> p v h t", t=2),
                        ramp[:].rearrange("p (h t) -> p h t", t=2).unsqueeze(1).to_broadcast([P, SUB, width // 2, 2]),
                        two[:, u].unsqueeze(2).to_broadcast([P, SUB, width // 2, 2]), ALU.is_equal).then_inc(hot, 1)

            def scan_scores(i, t):
                c, u, n = step_of(i, t)
                dve.wait_ge(v, c * V)
                dve.wait_ge(back[u], n)
                dve.wait_ge(flagged[u], n * 64 + 64)
                dve.wait_ge(turned[u], n + 1)
                nc.vector.tensor_tensor_scan(out=peak[:, u, 1:], data0=neg[:, u], data1=p_score[:],
                                             initial=peak[:, u, 0:1], op0=ALU.add, op1=ALU.max).then_inc(v, 1)
                dve.wait_ge(v, c * V + 1)
                nc.vector.tensor_tensor(args[:, u, 0], peak[:, u, 0:CHUNK], neg[:, u], ALU.add).then_inc(v, 1)
                nc.vector.tensor_tensor(args[:, u, 1], p_score[:], peak[:, u, 1:], ALU.subtract)
                dve.wait_ge(v, c * V + 2)
                nc.vector.tensor_tensor(args[:, u, 0], args[:, u, 0], peak[:, u, 1:], ALU.subtract).then_inc(exponents, 1)
                nc.vector.tensor_copy(peak[:, 1 - u, 0:1], peak[:, u, CHUNK:]).then_inc(v, 1)

            def scan_sums(i, t):
                c, u, n = step_of(i, t)
                dve.wait_ge(scanned, c * 2)
                dve.wait_ge(weighed, c + 1)
                nc.vector.tensor_tensor(value[:], weight[:, u, 1], p_val[:], ALU.mult).then_inc(used[u], 1)
                nc.vector.tensor_tensor_scan(out=den[:, u], data0=weight[:, u, 0], data1=weight[:, u, 1],
                                             initial=den[:, 1 - u, CHUNK - 1:], op0=ALU.mult, op1=ALU.add).then_inc(scanned, 1)
                dve.wait_ge(used[u], n + 1)
                nc.vector.tensor_tensor_scan(out=num[:, u], data0=weight[:, u, 0], data1=value[:],
                                             initial=num[:, 1 - u, CHUNK - 1:], op0=ALU.mult, op1=ALU.add).then_inc(scanned, 1)

            def one(i, t, is_last):
                for m in SHARE[t][:-1]:
                    compare(i, m)
                scan_scores(i, t)
                compare(i, SHARE[t][-1])
                scan_sums(i, t)

            over_steps(dve, one)

        @block.scalar
        def _(act):
            src_of = S.src_all[:, 0:E_PAD // P].rearrange("p (g c j) -> p g c j", g=GROUPS, j=LANES)
            src_after = S.src_all[:, 2 * LANES:2 * LANES + E_PAD // P].rearrange("p (g c j) -> p g c j", g=GROUPS, j=LANES)

            def pair_keys(first, u):
                for two, key in ((key2_hi, S.key_hi), (key2_lo, S.key_lo)):
                    nc.scalar.copy(two[:, u], key[:, bass.ds(first, SUB)].unsqueeze(2).to_broadcast([P, SUB, 2])).then_inc(paired, 1)

            def load_flags(i, t):
                c, u, n = step_of(i, t)
                act.wait_ge(used[u], n)
                for g in range(GROUPS):
                    first = c * CHUNK + g * GROUP_EDGES
                    act.dma_start(neg[FEAT * g:FEAT * (g + 1), u],
                                  D.neg[bass.ds(first, CHUNK)].unsqueeze(0).to_broadcast([FEAT, CHUNK])).then_inc(flagged[u], 16)

            def pack_rows(i, t):
                c, u, n = step_of(i, t)
                act.wait_ge(turned[u], n)
                act.wait_ge(gathered[u], n * (16 * EACH) + 16 * EACH)
                for w in range(2):
                    last = nc.scalar.copy(pack[:, u, :, w].rearrange("p j g f -> p g j f"),
                                          rows[:, u, :, :, FEAT * w:FEAT * (w + 1)])
                last.then_inc(packed[u], 1)
                nc.scalar.copy(ring[:, u].unsqueeze(2), src_after[:, :, bass.ds(c, 1), :]).then_inc(listed[u], 1)

            def keep_counts(i, m):
                s, u, n = sub_of(i, m)
                act.wait_ge(hot, s * 2)
                pair_keys(s * SUB + SUB, 1 - u)
                w = m // 2 % STAGES
                act.wait_ge(pair_stored[w], (i * pairs_on[w] + m // 2 // STAGES) * 16)
                for r in range(QUARTERS):
                    act.wait_ge(counted[u], n * QUARTERS + (r + 1))
                    at = u * SUB + r * SLOTS_Q
                    nc.scalar.copy(stage[:, w, :, at:at + SLOTS_Q].rearrange("p h (b v) -> p h b v", b=2),
                                   counts[:, r % 2, :, 0:4 * NH].rearrange("p b (v h) -> p h b v", h=NH)).then_inc(staged[r % 2], 1)

            def weigh(i, t):
                c, u, n = step_of(i, t)
                act.wait_ge(exponents, c + 1)
                nc.scalar.activation(weight[:, u], args[:, u], ACT.Exp).then_inc(weighed, 1)

            def put_out(i, t):
                c, u, n = step_of(i, t)
                act.wait_ge(out_stored[u], n * 16 * GROUPS)
                act.wait_ge(back[u], n + 1)
                nc.scalar.copy(out[:, u, :, :, 0:FEAT],
                               p_num[:].rearrange("p j (g f) -> p g j f", g=GROUPS)).then_inc(emptied, 1)
                nc.scalar.copy(out[:, u, :, :, FEAT:Y0_ROW],
                               p_stat[:].rearrange("p w j g -> p g j w")).then_inc(emptied, 1)

            for u in range(2):
                nc.scalar.copy(ring[:, u], src_of[:, :, u, :]).then_inc(first_listed, 1)
            def one(i, t, is_last):
                for m in SHARE[t][:-1]:
                    keep_counts(i, m)
                weigh(i, t)
                if not is_last:
                    load_flags(*after(i, t))
                    pack_rows(*after(i, t))
                keep_counts(i, SHARE[t][-1])
                put_out(i, t)

            load_flags(0, 0)
            pack_rows(0, 0)
            pair_keys(0, 0)
            over_steps(act, one)

        @block.sync
        def _(sp):
            sp.wait_ge(begun, 1)
            with sp.Fori(0, TURNS) as i:
                for t in range(ATTEND_STEPS):
                    sp.dma_start(D.inject[bass.ds((i * ATTEND_STEPS + t) * (GROUPS * CHUNK), GROUPS * CHUNK), :]
                                 .rearrange("(p r) f -> p (r f)", p=P), zeros[:]).then_inc(inject_zeroed, 16)
                    for m in SHARE[t]:
                        if m % 2:
                            w = m // 2 % STAGES
                            for half in range(2):
                                sp.wait_ge(staged[half], (i * COUNT_SUBS + m) * 2 + 2)
                            sp.dma_start(D.matrix[bass.ds(i * PAIRS + m // 2, 1), :, :, :].rearrange("s q p x -> p (s q) x"),
                                         stage[:, w].rearrange("p (q h) v -> p q (h v)", q=N_PARTS)).then_inc(pair_stored[w], 16)
                    c, u, n = step_of(i, t)
                    sp.wait_ge(emptied, c * 2 + 2)
                    for g in range(GROUPS):
                        first = c * CHUNK + g * GROUP_EDGES
                        sp.dma_start(D.scan0[bass.ds(first, CHUNK), :].rearrange("(p j) w -> p (j w)", j=LANES),
                                     out[:, u, g].rearrange("p j w -> p (j w)")).then_inc(out_stored[u], 16)
            sp.wait_ge(inject_zeroed, 16 * GROUP_CHUNKS)
            for w in range(STAGES):
                sp.wait_ge(pair_stored[w], 16 * pairs_on[w] * TURNS)
            for u in range(2):
                sp.wait_ge(out_stored[u], 16 * GROUPS * (GROUP_CHUNKS // 2))


def normalize(dve, link, T, S, out, cols, nth):
    T, square, mean, spread = T[:, cols], S.square[:, cols], S.stat[:, 0, cols], S.stat[:, 1, cols]
    link(dve.tensor_reduce(mean, T, AX.X, ALU.add))
    link(dve.tensor_scalar(mean, mean, 1.0 / FEAT, None, ALU.mult))
    link(dve.tensor_tensor(T, T, over_features(mean), ALU.subtract))
    link(dve.tensor_tensor(square, T, T, ALU.mult))
    link(dve.tensor_reduce(spread, square, AX.X, ALU.add))
    dve.tensor_scalar(spread, spread, 1.0 / FEAT, EPS, ALU.mult, ALU.add).then_inc(S.root_go, 1)
    dve.wait_ge(S.root_done, nth)
    link(dve.reciprocal(mean, spread))
    return link(dve.tensor_tensor(out[:, cols], T, over_features(mean), ALU.mult))


def take_root(nc, act, S, cols, nth):
    act.wait_ge(S.root_go, nth)
    nc.scalar.activation(S.stat[:, 1, cols], S.stat[:, 1, cols], ACT.Sqrt).then_inc(S.root_done, 1)


def finish_attention(nc, sb, sem, pb, D, S):
    S.square = sb("square_finish_attention", [P, NH, FEAT], f32)
    last = sb("last", [P, NH, Y0_ROW], f32)
    cut = sb("cut", [P, GROUPS - 1, Y0_ROW], f32)
    cut_dst = sb("cut_dst", [P, GROUPS - 1, 2], i32)
    cut_dst_f = sb("cut_dst_f", [P, GROUPS - 1, 2], f32)
    top = sb("top", [P, NH], f32)
    side = sb("side", [P, GROUPS, NH], f32)
    other = sb("other", [P, NH], f32)
    total = sb("total", [P, NH], f32)
    part = sb("part", [P, NH, FEAT], f32)

    cuts = sem("finish0_cuts_loaded")
    gathered = S.slice_gathered
    v = sem("finish0_vector_step")
    weighed = sem("finish0_weighed")
    steps, sided = [0], []

    def link(ins):
        steps[0] += 1
        ins.then_inc(v, 1)
        nc.vector.wait_ge(v, steps[0])
        return steps[0]

    with nc.Block() as block:
        @block.sync
        def _(sp):
            for g in range(GROUPS - 1):
                e = (g + 1) * GROUP_EDGES - 1
                sp.dma_start(cut[:, g, :], D.scan0[e:e + 1, :].to_broadcast([P, Y0_ROW])).then_inc(cuts, 16)
                sp.dma_start(cut_dst[:, g, :], D.dst[e:e + 2].unsqueeze(0).to_broadcast([P, 2])).then_inc(cuts, 16)

        @block.gpsimd
        def _(pool):
            for h in range(NH):
                nc.gpsimd.indirect_dma_start(out=last[:, h, :], out_offset=None, in_=D.scan0[:, :],
                                             in_offset=rows_of(S.last_edge[:, h:h + 1])).then_inc(gathered[h // SLICE], 16)

        @block.vector
        def _(dve):
            dve.wait_ge(cuts, 32 * (GROUPS - 1))
            link(nc.vector.tensor_copy(cut_dst_f[:], cut_dst[:]))
            for n, cols in enumerate(SLICES):
                ends, one = last[:, cols], other[:, cols]
                dve.wait_ge(gathered[n], 16 * SLICE)
                link(nc.vector.tensor_copy(top[:, cols], ends[:, :, FEAT + 1]))
                for g in range(GROUPS - 1):
                    link(nc.vector.tensor_scalar(one, S.node_id[:, cols], cut_dst_f[:, g, 0:1], None, ALU.is_equal))
                    link(nc.vector.tensor_scalar(side[:, g, cols], S.node_id[:, cols], cut_dst_f[:, g, 1:2], None, ALU.is_equal))
                    link(nc.vector.tensor_tensor(one, one, side[:, g, cols], ALU.mult))
                    link(nc.vector.tensor_scalar(one, one, 1.0, -NEG, ALU.subtract, ALU.mult))
                    link(nc.vector.tensor_scalar(side[:, g, cols], one, cut[:, g, FEAT + 1:FEAT + 2], None, ALU.add))
                    link(nc.vector.tensor_tensor(top[:, cols], top[:, cols], side[:, g, cols], ALU.max))
                link(nc.vector.tensor_copy(side[:, GROUPS - 1, cols], ends[:, :, FEAT + 1]))
                sided.append(link(nc.vector.tensor_tensor(side[:, :, cols], side[:, :, cols],
                                                          top[:, cols].unsqueeze(1).to_broadcast([P, GROUPS, SLICE]), ALU.subtract)))
                dve.wait_ge(weighed, n + 1)
                own, sums, whole = side[:, GROUPS - 1, cols], S.work[:, cols], total[:, cols]
                link(nc.vector.tensor_tensor(whole, ends[:, :, FEAT], own, ALU.mult))
                link(nc.vector.tensor_tensor(sums, ends[:, :, 0:FEAT], over_features(own), ALU.mult))
                for g in range(GROUPS - 1):
                    link(nc.vector.scalar_tensor_tensor(whole, side[:, g, cols], cut[:, g, FEAT:FEAT + 1], whole, ALU.mult, ALU.add))
                    link(nc.vector.tensor_tensor(part[:, cols], over_features(side[:, g, cols]),
                                                 cut[:, g, 0:FEAT].unsqueeze(1).to_broadcast([P, SLICE, FEAT]), ALU.mult))
                    link(nc.vector.tensor_tensor(sums, sums, part[:, cols], ALU.add))
                link(nc.vector.reciprocal(one, whole))
                link(nc.vector.tensor_tensor(one, one, S.has_edges[:, cols], ALU.mult))
                link(nc.vector.tensor_tensor(sums, sums, over_features(one), ALU.mult))
                link(nc.vector.tensor_tensor(sums, sums, S.base[:, cols], ALU.add))
                normalize(nc.vector, link, S.work, S, S.x, cols, n + 1)

        @block.scalar
        def _(act):
            for n, cols in enumerate(SLICES):
                act.wait_ge(v, sided[n])
                nc.scalar.activation(side[:, :, cols], side[:, :, cols], ACT.Exp).then_inc(weighed, 1)
                take_root(nc, act, S, cols, n + 1)


def propagate(nc, sb, sem, pb, D, S, name, turn, before, after):
    ROUNDS = 3
    PAIRS = BLOCK // PAIR
    split = sb("split", [P, NH, 3, FEAT], bf16)
    raw = sb("raw", [P, N_PARTS, PAIRS, HI_PART * PAIR], u8)
    part = sb("part", [P, PLACES, PAIRS, HI_PART * PAIR], bf16)
    sums = scaled = S.square = S.base
    keep = sb("keep", [3 * FEAT, BLOCK], i32)
    slot_sum = sb("slot_sum", [3 * FEAT, BLOCK], f32)
    carry = sb("carry", [3 * FEAT, 1], f32)
    out = sb("out", [P, LANES, FEAT], f32)
    p_dense = pb("p_dense", [3 * FEAT, 2, BLOCK], f32)
    p_out = pb("p_out", [P, LANES, 3 * FEAT], f32)

    loaded, widened, multiplied = S.part_loaded, S.part_widened, S.part_multiplied
    splitted, flagged, scanned, carried, back, emptied, stored, *gathered = S.block_sems
    first = turn * ROUNDS
    v = sem(name + "_vector_step")
    root = (turn + 1) * (len(SLICES) + 1)
    steps = [0]
    cut = SPLIT_PART * HI_PART
    sides = (slice(0, cut), slice(cut, NH))

    def widen(eng, copy, n, q):
        there = [other for other in range(N_PARTS) if PLACE[other] == PLACE[q]]
        earlier = there.index(q) - 1
        eng.wait_ge(multiplied[there[earlier]], n if earlier < 0 else n + 1)
        eng.wait_ge(loaded[q], n * 16 + 16)
        copy(part[:, PLACE[q]], raw[:, q]).then_inc(widened[q], 1)

    def over_blocks(eng, k, block):
        block(k * N_BLOCKS, 0, 0, True)
        with eng.Fori(0, N_BLOCKS // 2) as i:
            for u in range(2):
                block(k * N_BLOCKS + i * 2 + (u + 1), i * 2 + (u + 1), 1 - u, False)

    def link(ins):
        steps[0] += 1
        ins.then_inc(v, 1)
        nc.vector.wait_ge(v, steps[0])

    with nc.Block() as block:
        @block.sync
        def _(sp):
            with sp.Fori(first, first + ROUNDS) as k:
                with sp.Fori(0, N_BLOCKS) as b:
                    for q in range(N_PARTS):
                        blocks = sp.snap(sp.to_reg(k * N_BLOCKS + b))
                        sp.wait_ge(S.tables_done, 1)
                        sp.wait_ge(widened[q], blocks)
                        sp.dma_start(raw[:, q], D.matrix[bass.ds(b * PAIRS, PAIRS), q, :, :]
                                     .rearrange("s p x -> p s x")).then_inc(loaded[q], 16)

        @block.scalar
        def _(act):
            def store(n, b):
                act.wait_ge(emptied, n + 1)
                act.dma_start(D.slot_sums[bass.ds(b * BLOCK, BLOCK), :].rearrange("(p j) f -> p (j f)", j=LANES),
                              out[:].rearrange("p j f -> p (j f)")).then_inc(stored, 16)

            def one(n, b, bank, leads):
                widen(act, nc.scalar.copy, n, 0)
                widen(act, nc.scalar.copy, n, 1)
                act.wait_ge(scanned, n)
                act.dma_start(keep[:], D.slot_flags[bass.ds(b * BLOCK, BLOCK), :].rearrange("v o -> o v")
                              .to_broadcast([3 * FEAT, BLOCK])).then_inc(flagged, 16)
                if leads:
                    widen(act, nc.scalar.copy, n, 2)
                widen(act, nc.scalar.copy, n, 3)
                if not leads:
                    store(n - 1, b - 1)

            with act.Fori(first, first + ROUNDS) as k:
                over_blocks(act, k, one)
                store(k * N_BLOCKS + (N_BLOCKS - 1), N_BLOCKS - 1)
            take_root(nc, act, S, slice(0, NH), root)

        @block.tensor
        def _(pe):
            def turn_back(n):
                pe.wait_ge(S.tables_done, 1)
                pe.wait_ge(emptied, n)
                pe.wait_ge(scanned, n + 1)
                for j in range(LANES):
                    last = nc.tensor.transpose(p_out[:, j, :], slot_sum[:, j::LANES], S.ident[0:3 * FEAT, 0:3 * FEAT])
                last.then_inc(back, 1)

            def one(k, n, bank, leads):
                if not leads:
                    pe.wait_ge(scanned, n - 1)
                for q in range(N_PARTS):
                    if leads and q in (0, SPLIT_PART):
                        pe.wait_ge(splitted, k * 2 + (1 if q == 0 else 2))
                    pe.wait_ge(widened[q], n + 1)
                    here = part[:, PLACE[q]].rearrange("p s (h v) -> p s h v", v=PAIR)
                    for m in range(HI_PART):
                        h = q * HI_PART + m
                        last = nc.tensor.matmul(p_dense[:, bank], split[:, h].rearrange("p c f -> p (c f)"), here[:, :, m, :],
                                                start=(h == 0), stop=(h == NH - 1))
                    last.then_inc(multiplied[q], 1)
                    if q == 0 and not leads:
                        turn_back(n - 1)

            with pe.Fori(first, first + ROUNDS) as k:
                over_blocks(pe, k, lambda n, b, bank, leads: one(k, n, bank, leads))
                turn_back(k * N_BLOCKS + (N_BLOCKS - 1))

        @block.vector
        def _(dve):
            def split_x(side, follow):
                x, parts = scaled[:, side], split[:, side]
                follow(nc.vector.tensor_copy(parts[:, :, 0, :], x))
                follow(nc.vector.tensor_tensor(x, x, parts[:, :, 0, :], ALU.subtract))
                follow(nc.vector.tensor_copy(parts[:, :, 1, :], x))
                follow(nc.vector.tensor_tensor(x, x, parts[:, :, 1, :], ALU.subtract))
                nc.vector.tensor_copy(parts[:, :, 2, :], x).then_inc(splitted, 1)

            nc.vector.memset(carry[:], 0.0)
            if before is None:
                link(nc.vector.tensor_copy(scaled[:], S.x[:]))
            else:
                link(nc.vector.tensor_tensor(scaled[:], S.x[:], over_features(before[:]), ALU.mult))
            for side in sides:
                split_x(side, link)
            link(nc.vector.tensor_scalar(S.work[:], S.x[:], 1.25, None, ALU.mult))
            base = steps[0]
            V = 2 * (6 if before is None else 7)

            def add_parts(n):
                dve.wait_ge(stored, n * 16)
                dve.wait_ge(back, n + 1)
                nc.vector.tensor_reduce(out[:], p_out[:].rearrange("p j (c f) -> p j f c", c=3), AX.X, ALU.add).then_inc(emptied, 1)

            def one(n, b, bank, leads):
                if not leads:
                    widen(dve, nc.vector.tensor_copy, n, 2)
                    add_parts(n - 1)
                for q in (4, 5, 6):
                    widen(dve, nc.vector.tensor_copy, n, q)
                dve.wait_ge(flagged, n * 16 + 16)
                dve.wait_ge(carried, n)
                dve.wait_ge(back, n)
                dve.wait_ge(multiplied[N_PARTS - 1], n + 1)
                nc.vector.tensor_tensor_scan(out=slot_sum[:], data0=keep[:], data1=p_dense[:, bank], initial=carry[:, 0:1],
                                             op0=ALU.mult, op1=ALU.add).then_inc(scanned, 1)
                dve.wait_ge(scanned, n + 1)
                nc.vector.tensor_copy(carry[:], slot_sum[:, BLOCK - 1:]).then_inc(carried, 1)

            def round_of(k, is_last):
                done = [0]

                def step(ins):
                    done[0] += 1
                    ins.then_inc(v, 1)
                    dve.wait_ge(v, k * V + (base + done[0] - first * V))

                over_blocks(dve, k, one)
                add_parts(k * N_BLOCKS + (N_BLOCKS - 1))
                for n, side in enumerate(sides):
                    columns = side.stop - side.start
                    dve.wait_ge(gathered[n], k * (16 * columns) + 16 * columns)
                    dve.wait_ge(splitted, k * 2 + 2)
                    x = sums[:, side]
                    step(nc.vector.tensor_tensor(x, x, over_features(after[:, side]), ALU.mult))
                    step(nc.vector.scalar_tensor_tensor(S.work[:, side], x, 0.25, S.work[:, side], ALU.mult, ALU.add))
                    if not is_last:
                        if before is not None:
                            step(nc.vector.tensor_tensor(x, x, over_features(before[:, side]), ALU.mult))
                        split_x(side, step)
                return done[0]

            with dve.Fori(first, first + ROUNDS - 1) as k:
                round_of(k, False)
            steps[0] = base + (ROUNDS - 1) * V + round_of(first + ROUNDS - 1, True)
            normalize(nc.vector, link, S.work, S, S.x, slice(0, NH), root)

        @block.gpsimd
        def _(pool):
            ready = [min(N_BLOCKS, -(-(TILES + P * (h + 1)) // BLOCK)) for h in range(NH)]
            with pool.Fori(first, first + ROUNDS) as k:
                for blocks in sorted(set(ready)):
                    blocks_stored = pool.snap(pool.to_reg((k * N_BLOCKS + blocks) * 16))
                    pool.wait_ge(S.tables_done, 1)
                    pool.wait_ge(stored, blocks_stored)
                    for h in range(NH):
                        if ready[h] == blocks:
                            nc.gpsimd.indirect_dma_start(out=sums[:, h, :], out_offset=None, in_=D.slot_sums[0:blocks * BLOCK, :],
                                                         in_offset=rows_of(S.last_slot[:, h:h + 1])).then_inc(gathered[0 if h < cut else 1], 16)


def spread_nodes(nc, sb, sem, pb, D, S):
    stored = sem("spread_table_stored")
    placed = sem("spread_rows_placed")
    half_loaded = sem("spread_half_dst_loaded")
    half_gathered = sem("spread_half_row_gathered")
    half_placed = sem("spread_half_row_placed")
    half_dst = sb("half_dst", [P, 1], i32)
    half_x = sb("half_x", [P, FEAT], f32)
    with nc.Block() as block:
        @block.sync
        def _(sp):
            sp.dma_start(D.table2[:, :].rearrange("(h p) f -> p h f", p=P), S.x[:]).then_inc(stored, 16)
            sp.dma_start(half_dst[:], D.dst[HALF_EDGES:HALF_EDGES + 1].unsqueeze(0).to_broadcast([P, 1])).then_inc(half_loaded, 16)
            sp.wait_ge(stored, 16)
            sp.wait_ge(placed, 16 * NH)
            sp.wait_ge(half_gathered, 16)
            sp.dma_start(D.inject[HALF_EDGES:HALF_EDGES + 1, :], half_x[0:1, :]).then_inc(half_placed, 16)
            sp.wait_ge(half_placed, 16)

        @block.gpsimd
        def _(pool):
            for h in range(NH):
                nc.gpsimd.indirect_dma_start(out=D.inject[:, :], out_offset=rows_of(S.first_edge[:, h:h + 1]),
                                             in_=S.x[:, h, :], in_offset=None).then_inc(placed, 16)
            pool.wait_ge(half_loaded, 16)
            pool.wait_ge(stored, 16)
            nc.gpsimd.indirect_dma_start(out=half_x[:], out_offset=None, in_=D.table2[:, :],
                                         in_offset=rows_of(half_dst[:, 0:1])).then_inc(half_gathered, 16)
            pool.wait_ge(placed, 16 * NH)


def judge_edges(nc, sb, sem, pb, D, S):
    WIDE = 3 * FEAT
    HALVES = 2
    ring = sb("ring2", [P, 2, HALVES, LANES], i32)
    rows = sb("rows2", [P, 2, HALVES, LANES, WIDE], f32)
    keep = sb("keep2", [WIDE, 2, HALVES, CHUNK], bf16)
    neg = sb("neg2", [HALVES * FEAT, 2, CHUNK], bf16)
    feat = sb("feat2", [WIDE, 2, HALVES, CHUNK], f32)
    hidden = sb("hidden2", [HALVES * HID, 2, CHUNK], f32)
    best = sb("best2", [HALVES * FEAT, 2, CHUNK], f32)
    out = sb("out2", [P, 2, HALVES, LANES, FEAT], f32)
    w1 = sb("w1_2", [WIDE, HALVES, P], f32)
    w2 = sb("w2_2", [HALVES * HID, P], f32)
    b1 = sb("b1_2", [HALVES * HID, 1], f32)
    p_feat = pb("p_feat", [WIDE, 2, HALVES, CHUNK], f32)
    p_hid = pb("p_hid", [HALVES * HID, CHUNK], f32)
    p_msg = pb("p_msg", [P, 2, CHUNK], f32)
    p_back = pb("p_back", [P, LANES, HALVES * FEAT], f32)

    def pair_of(what):
        return [sem(f"judge_{what}_{u}") for u in range(2)]

    begun = sem("judge_first_states_made")
    w_loaded = sem("judge_weights_loaded")
    listed = sem("judge_sources_listed")
    gathered, loaded, turned = pair_of("rows_gathered"), pair_of("rows_loaded"), pair_of("rows_turned")
    copied, held, lifted, rectified = pair_of("features_copied"), pair_of("dst_held"), pair_of("hidden_multiplied"), pair_of("hidden_rectified")
    sent, topped, back = pair_of("messages_multiplied"), pair_of("maxima_scanned"), pair_of("maxima_turned_back")
    emptied, stored, flagged = pair_of("out_emptied"), pair_of("out_stored"), pair_of("neg_flags_loaded")
    STEPS = HALF_CHUNKS
    assert STEPS % 2 == 1
    last_edges = N_EDGES - (CHUNKS - 1) * CHUNK
    WEIGHTS = 16 * 5 * HALVES

    def skewed(eng, one):
        with eng.Fori(0, STEPS // 2) as i:
            one(i * 2 + 1, 1, i)
            one(i * 2 + 2, 0, i + 1)

    def before(u, n):
        return (0, n) if u else (1, n - 1)

    final = (0, STEPS // 2)

    with nc.Block() as block:
        @block.gpsimd
        def _(pool):
            def gather(k, u):
                listings = pool.snap(pool.to_reg(k + 1))
                pool.wait_ge(begun, 1)
                pool.wait_ge(listed, listings)
                for half in range(HALVES):
                    for j in range(LANES):
                        nc.gpsimd.indirect_dma_start(out=rows[:, u, half, j, 0:FEAT], out_offset=None, in_=D.table2[:, :],
                                                     in_offset=rows_of(ring[:, u, half, j:j + 1])).then_inc(gathered[u], 16)

            with pool.Fori(0, STEPS // 2) as i:
                for u in range(2):
                    gather(i * 2 + u, u)
            gather(STEPS - 1, 0)

        @block.sync
        def _(sp):
            sp.wait_ge(begun, 1)
            for half in range(HALVES):
                cols = slice(half * HID, (half + 1) * HID)
                for place, part in enumerate((0, 2, 1)):
                    sp.dma_start(w1[place * FEAT:(place + 1) * FEAT, half, cols], D.W1[part * FEAT:(part + 1) * FEAT, :]).then_inc(w_loaded, 16)
                sp.dma_start(w2[cols, half * FEAT:(half + 1) * FEAT], D.W2[:, :]).then_inc(w_loaded, 16)
                sp.dma_start(b1[cols, :], D.b1[:].unsqueeze(1), allow_slow_non_contiguous=True).then_inc(w_loaded, 16)

            def load(k, u, n, n_attr):
                before_last = sp.snap(sp.to_reg(n))
                sp.wait_ge(begun, 1)
                sp.wait_ge(turned[u], before_last)
                sp.wait_ge(held[u], before_last)
                for half in range(HALVES):
                    first = k * CHUNK + half * HALF_EDGES
                    sp.dma_start(rows[0:n_attr[half] // LANES, u, half, :, FEAT:2 * FEAT],
                                 D.attr[bass.ds(first, n_attr[half]), :].rearrange("(p j) f -> p j f", j=LANES)).then_inc(loaded[u], 16)
                    sp.dma_start(rows[:, u, half, :, 2 * FEAT:WIDE],
                                 D.inject[bass.ds(first, CHUNK), :].rearrange("(p j) f -> p j f", j=LANES)).then_inc(loaded[u], 16)
                    sp.dma_start(keep[2 * FEAT:WIDE, u, half],
                                 D.keep[bass.ds(first, CHUNK)].unsqueeze(0).to_broadcast([FEAT, CHUNK])).then_inc(loaded[u], 16)
                sp.wait_ge(begun, 1)
                sp.wait_ge(topped[u], before_last)
                for half in range(HALVES):
                    first = k * CHUNK + half * HALF_EDGES
                    sp.dma_start(neg[half * FEAT:(half + 1) * FEAT, u],
                                 D.neg[bass.ds(first, CHUNK)].unsqueeze(0).to_broadcast([FEAT, CHUNK])).then_inc(flagged[u], 16)

            with sp.Fori(0, STEPS // 2) as i:
                for u in range(2):
                    load(i * 2 + u, u, i, (CHUNK, CHUNK))
            load(STEPS - 1, 0, STEPS // 2, (CHUNK, last_edges))

        @block.tensor
        def _(pe):
            def turn(u, n):
                pe.wait_ge(copied[u], n)
                pe.wait_ge(held[u], n)
                pe.wait_ge(loaded[u], n * (48 * HALVES) + 48 * HALVES)
                pe.wait_ge(gathered[u], n * (16 * LANES * HALVES) + 16 * LANES * HALVES)
                for half in range(HALVES):
                    for j in range(LANES):
                        last = nc.tensor.transpose(p_feat[:, u, half, j::LANES], rows[:, u, half, j, :], S.ident[:])
                last.then_inc(turned[u], 1)

            def lift(u, n):
                pe.wait_ge(rectified[1 - u], n if u == 0 else n + 1)
                pe.wait_ge(copied[u], n + 1)
                pe.wait_ge(held[u], n + 1)
                for half in range(HALVES):
                    last = nc.tensor.matmul(p_hid[:], w1[:, half], feat[:, u, half], start=(half == 0), stop=(half == HALVES - 1))
                last.then_inc(lifted[u], 1)

            def send(u, n):
                pe.wait_ge(topped[u], n)
                pe.wait_ge(rectified[u], n + 1)
                nc.tensor.matmul(p_msg[:, u], w2[:], hidden[:, u], start=True, stop=True).then_inc(sent[u], 1)

            def turn_back(u, n):
                pe.wait_ge(w_loaded, WEIGHTS)
                pe.wait_ge(emptied[1 - u], n if u == 0 else n + 1)
                pe.wait_ge(topped[u], n + 1)
                for j in range(LANES):
                    last = nc.tensor.transpose(p_back[:, j, :], best[:, u, j::LANES], S.ident[0:HALVES * FEAT, 0:HALVES * FEAT])
                last.then_inc(back[u], 1)

            def one(k, u, n):
                turn(u, n)
                send(*before(u, n))
                lift(u, n)
                turn_back(*before(u, n))

            pe.wait_ge(w_loaded, WEIGHTS)
            turn(0, 0)
            lift(0, 0)
            skewed(pe, one)
            send(*final)
            turn_back(*final)

        @block.vector
        def _(dve):
            nc.vector.memset(w1[:], 0.0)
            nc.vector.memset(w2[:], 0.0)
            nc.vector.memset(feat[2 * FEAT:WIDE, 1, :, CHUNK - 1:], 0.0)
            nc.vector.memset(best[:, 1, CHUNK - 1:], NEG).then_inc(begun, 1)
            dve.wait_ge(begun, 1)

            def hold(u, n):
                dve.wait_ge(lifted[u], n)
                dve.wait_ge(held[1 - u], n if u == 0 else n + 1)
                dve.wait_ge(loaded[u], n * (48 * HALVES) + 48 * HALVES)
                dve.wait_ge(turned[u], n + 1)
                for half in range(HALVES):
                    last = nc.vector.tensor_tensor_scan(out=feat[2 * FEAT:WIDE, u, half], data0=keep[2 * FEAT:WIDE, u, half],
                                                        data1=p_feat[2 * FEAT:WIDE, u, half],
                                                        initial=feat[2 * FEAT:WIDE, 1 - u, half, CHUNK - 1:],
                                                        op0=ALU.mult, op1=ALU.add)
                last.then_inc(held[u], 1)

            def top(u, n):
                dve.wait_ge(back[u], n)
                dve.wait_ge(topped[1 - u], n if u == 0 else n + 1)
                dve.wait_ge(flagged[u], n * (16 * HALVES) + 16 * HALVES)
                dve.wait_ge(sent[u], n + 1)
                nc.vector.tensor_tensor_scan(out=best[:, u], data0=neg[:, u], data1=p_msg[0:HALVES * FEAT, u],
                                             initial=best[:, 1 - u, CHUNK - 1:],
                                             op0=ALU.add, op1=ALU.max).then_inc(topped[u], 1)

            def one(k, u, n):
                hold(u, n)
                top(*before(u, n))

            hold(0, 0)
            skewed(dve, one)
            top(*final)

        @block.scalar
        def _(act):
            src_of = S.src_all[:, 0:CHUNKS * LANES].rearrange("p (h k j) -> p h k j", h=HALVES, j=LANES)
            src_after = S.src_all[:, 2 * LANES:(2 + CHUNKS) * LANES].rearrange("p (h k j) -> p h k j", h=HALVES, j=LANES)
            for u in range(2):
                nc.scalar.copy(ring[:, u], src_of[:, :, u, :]).then_inc(listed, 1)
            act.wait_ge(w_loaded, WEIGHTS)

            def copy(k, u, n):
                act.wait_ge(lifted[u], n)
                act.wait_ge(turned[u], n + 1)
                nc.scalar.copy(feat[0:2 * FEAT, u], p_feat[0:2 * FEAT, u]).then_inc(copied[u], 1)
                act.wait_ge(gathered[u], n * (16 * LANES * HALVES) + 16 * LANES * HALVES)
                at = slice(k, k + 1) if isinstance(k, int) else bass.ds(k, 1)
                nc.scalar.copy(ring[:, u].unsqueeze(2), src_after[:, :, at, :]).then_inc(listed, 1)

            def rectify(u, n):
                act.wait_ge(sent[u], n)
                act.wait_ge(lifted[u], n + 1)
                nc.scalar.activation(hidden[:, u], p_hid[:], ACT.Relu, bias=b1[:, 0:1]).then_inc(rectified[u], 1)

            def put_out(k, u, n):
                act.wait_ge(stored[u], n * (16 * HALVES))
                act.wait_ge(back[u], n + 1)
                nc.scalar.copy(out[:, u], p_back[:].rearrange("p j (h f) -> p h j f", h=HALVES)).then_inc(emptied[u], 1)
                act.wait_ge(emptied[u], n + 1)
                for half in range(HALVES):
                    act.dma_start(D.scan2[bass.ds(k * CHUNK + half * HALF_EDGES, CHUNK), :].rearrange("(p j) f -> p (j f)", j=LANES),
                                  out[:, u, half].rearrange("p j f -> p (j f)")).then_inc(stored[u], 16)

            def one(k, u, n):
                copy(k, u, n)
                rectify(u, n)
                put_out(k - 1, *before(u, n))

            copy(0, 0, 0)
            rectify(0, 0)
            skewed(act, one)
            put_out(STEPS - 1, *final)
            act.wait_ge(stored[0], 16 * HALVES * (STEPS // 2 + 1))
            act.wait_ge(stored[1], 16 * HALVES * (STEPS // 2))


def finish_judging(nc, sb, sem, pb, D, S):
    S.square = sb("square_finish_judging", [P, NH, FEAT], f32)
    best = sb("best_node", [P, NH, FEAT], f32)
    b2 = sb("b2_all", [P, FEAT], f32)
    none = sb("none", [P, NH], f32)
    part = sb("part", [P, NH, FEAT], f32)
    cut = sb("cut2", [P, FEAT], f32)
    cut_dst = sb("cut_dst2", [P, 2], i32)
    cut_dst_f = sb("cut_dst2_f", [P, 2], f32)
    both = sb("both", [P, 2, NH], f32)
    cut_loaded = sem("finish2_cut_loaded")
    b2_loaded = sem("finish2_b2_loaded")
    gathered = S.slice_gathered
    v = sem("finish2_vector_step")
    root = len(SLICES) + 1
    steps = [0]

    def link(ins):
        steps[0] += 1
        ins.then_inc(v, 1)
        nc.vector.wait_ge(v, steps[0])
        return steps[0]

    with nc.Block() as block:
        @block.sync
        def _(sp):
            sp.dma_start(b2[:], D.b2[:].unsqueeze(0).to_broadcast([P, FEAT])).then_inc(b2_loaded, 16)
            e = HALF_EDGES - 1
            sp.dma_start(cut[:], D.scan2[e:e + 1, :].to_broadcast([P, FEAT])).then_inc(cut_loaded, 16)
            sp.dma_start(cut_dst[:], D.dst[e:e + 2].unsqueeze(0).to_broadcast([P, 2])).then_inc(cut_loaded, 16)

        @block.gpsimd
        def _(pool):
            for h in range(NH):
                nc.gpsimd.indirect_dma_start(out=best[:, h, :], out_offset=None, in_=D.scan2[:, :],
                                             in_offset=rows_of(S.last_edge[:, h:h + 1])).then_inc(gathered[h // SLICE], 16)

        @block.vector
        def _(dve):
            link(nc.vector.tensor_scalar(none[:], S.has_edges[:], 1.0, -2.0 * NEG, ALU.subtract, ALU.mult))
            dve.wait_ge(cut_loaded, 32)
            link(nc.vector.tensor_copy(cut_dst_f[:], cut_dst[:]))
            for side in range(2):
                link(nc.vector.tensor_scalar(both[:, side], S.node_id[:], cut_dst_f[:, side:side + 1], None, ALU.is_equal))
            link(nc.vector.tensor_tensor(both[:, 0], both[:, 0], both[:, 1], ALU.mult))
            link(nc.vector.tensor_scalar(both[:, 0], both[:, 0], 1.0, -NEG, ALU.subtract, ALU.mult))
            link(nc.vector.tensor_tensor(part[:], cut[:].unsqueeze(1).to_broadcast([P, NH, FEAT]), over_features(both[:, 0]), ALU.add))
            dve.wait_ge(b2_loaded, 16)
            for n, cols in enumerate(SLICES):
                top = best[:, cols]
                dve.wait_ge(gathered[n], 2 * 16 * SLICE)
                link(nc.vector.tensor_tensor(top, top, part[:, cols], ALU.max))
                link(nc.vector.tensor_tensor(top, top, b2[:].unsqueeze(1).to_broadcast([P, SLICE, FEAT]), ALU.add))
                link(nc.vector.tensor_tensor(top, top, over_features(none[:, cols]), ALU.add))
                link(nc.vector.tensor_tensor(top, top, S.x[:, cols], ALU.max))
                link(nc.vector.tensor_tensor(S.work[:, cols], top, S.x[:, cols], ALU.add))
                normalize(nc.vector, link, S.work, S, S.x, cols, root + n + 1)

        @block.scalar
        def _(act):
            for n, cols in enumerate(SLICES):
                take_root(nc, act, S, cols, root + n + 1)


def write_out(nc, sem, D, S):
    stored = sem("output_stored")
    full = N_NODES // P
    with nc.Block() as block:
        @block.sync
        def _(sp):
            sp.dma_start(D.out[0:full * P, :].rearrange("(h p) f -> p h f", p=P), S.x[:, 0:full, :]).then_inc(stored, 16)
            sp.dma_start(D.out[full * P:N_NODES, :], S.x[0:N_NODES - full * P, full, :]).then_inc(stored, 16)
            sp.wait_ge(stored, 32)


def graph_layers(nc, x, src, dst, attr, w1_W, w1_b, w2_W, w2_b, a, W1, b1, W2, b2, out):
    D = Names()
    D.x, D.src, D.dst, D.attr, D.out = x, src, dst, attr, out
    D.w1_W, D.w1_b, D.w2_W, D.w2_b, D.a = w1_W, w1_b, w2_W, w2_b, a
    D.W1, D.b1, D.W2, D.b2 = W1, b1, W2, b2

    def dram(name, shape, dt):
        return nc.dram_tensor(name, shape, dt, kind="Internal").ap()

    D.slot_flags = dram("slot_flags", [SLOTS + P, 1], i32)
    D.edge_table = dram("edge_table", [TILES, 2 * P], i32)
    D.keep = dram("keep_flags", [E_PAD], bf16)
    D.neg = dram("neg_flags", [E_PAD], bf16)
    D.inject = dram("inject", [E_PAD + N_PAD, FEAT], f32)
    D.table0 = dram("table0", [N_PAD, 2 * FEAT], f32)
    D.table2 = dram("table2", [N_PAD, FEAT], f32)
    D.info = dram("info", [INFO_SPARE + SLOTS, 2], i32)
    D.matrix = dram("matrix", [SLOTS // PAIR, N_PARTS, P, HI_PART * PAIR], u8)
    D.scan0 = dram("scan0", [E_PAD, Y0_ROW], f32)
    D.scan2 = dram("scan2", [CHUNKS * CHUNK, FEAT], f32)
    D.slot_sums = dram("slot_sums", [SLOTS, FEAT], f32)

    with ExitStack() as whole:
        def keeper(stack, alloc, prefix=""):
            return lambda name, *spec: stack.enter_context(alloc(prefix + name, *spec))

        sb = keeper(whole, nc.sbuf_tensor)
        sem = keeper(whole, nc.semaphore)
        S = Names()
        S.tables_done = sem("tables_done")
        S.root_go, S.root_done = sem("variance_made"), sem("root_taken")
        S.slice_gathered = [sem(f"ends_of_slice{n}_gathered") for n in range(len(SLICES))]
        S.part_loaded, S.part_widened, S.part_multiplied = (
            [sem(f"propagate_part{q}_{what}") for q in range(N_PARTS)] for what in ("loaded", "widened", "multiplied"))
        S.block_sems = [sem("propagate_" + what) for what in (
            "x_split", "flags_loaded", "block_scanned", "carry_kept", "block_turned_back", "block_emptied",
            "block_stored", "sums0_gathered", "sums1_gathered")]
        S.x = sb("x_sb", [P, NH, FEAT], f32)
        S.base = sb("base", [P, NH, FEAT], f32)
        S.stat = sb("stat", [P, 2, NH], f32)
        S.ident = sb("ident", [P, P], f32)
        S.ident_bf = sb("ident_bf", [P, P], bf16)
        S.before = sb("before", [P, P], f32)
        S.group_pick = sb("group_pick", [P, GROUPS], f32)
        S.ramp_hi = sb("ramp_hi", [P, NH], bf16)
        S.ramp_lo = sb("ramp_lo", [P, P], bf16)
        S.slot_id = sb("slot_id", [P, SLOT_COLS], f32)
        S.node_id = sb("node_id", [P, NH], f32)
        S.src_all = sb("src_all", [P, E_PAD // P + 2 * LANES], i32)
        S.has_edges, S.mean_scale, S.norm_scale = (
            sb(name, [P, NH], f32) for name in ("has_edges", "mean_scale", "norm_scale"))
        S.last_slot, S.last_edge, S.first_edge = (
            sb(name, [P, NH], i32) for name in ("last_slot", "last_edge", "first_edge"))

        def stage(build, *more):
            with ExitStack() as local:
                prefix = "_".join([build.__name__, *more[:1], ""])
                build(nc, keeper(local, nc.sbuf_tensor, prefix), sem, keeper(local, nc.psum_tensor, prefix), D, S, *more)

        stage(prepare_constants)
        with ExitStack() as local:
            S.key_hi = keeper(local, nc.sbuf_tensor)("key_hi_all", [P, SLOTS + SUB], bf16)
            S.key_lo = keeper(local, nc.sbuf_tensor)("key_lo_all", [P, SLOTS + SUB], bf16)
            stage(prepare_slots_and_nodes)
            stage(prepare_ends)
            stage(attend_and_count)
        S.work = sb("work", [P, NH, FEAT], f32)
        stage(finish_attention)
        stage(propagate, "mean", 0, None, S.mean_scale)
        stage(spread_nodes)
        stage(judge_edges)
        stage(finish_judging)
        stage(propagate, "norm", 1, S.norm_scale, S.norm_scale)
        write_out(nc, sem, D, S)


_INS = ["x", "src", "dst", "edge_attr_32", "L0_gnn_w1_W", "L0_gnn_w1_b", "L0_gnn_w2_W", "L0_gnn_w2_b", "L0_gnn_a",
        "L2_gnn_W1", "L2_gnn_b1", "L2_gnn_W2", "L2_gnn_b2"]


def kernel(**inputs):
    import numpy as _np
    import concourse.bacc as _bacc
    from concourse import mybir as _mybir
    from concourse.bass_utils import run_bass_kernel_spmd as _run

    nc = _bacc.Bacc("TRN2", target_bir_lowering=False, num_devices=1)
    arrays, args = {}, []
    for name in _INS:
        a = _np.ascontiguousarray(inputs[name])
        arrays[f"in_{name}_dram"] = a
        args.append(nc.dram_tensor(f"in_{name}_dram", a.shape, _mybir.dt.from_np(a.dtype), kind="ExternalInput").ap())
    args.append(nc.dram_tensor("out_dram", (N_NODES, FEAT), _mybir.dt.float32, kind="ExternalOutput").ap())
    graph_layers(nc, *args)
    r = _run(nc, [arrays], core_ids=[0])
    return r.results[0]["out_dram"]
```
